# Optimizing a Trainium2 kernel written in Bass

```python
import numpy as np
import jax
import jax.numpy as jnp

def _softmax(x, axis=-1):
    return jax.nn.softmax(x, axis=axis)

def _gelu(x):
    return jax.nn.gelu(x, approximate=True)

def _silu(x):
    return jax.nn.silu(x)

def _sigmoid(x):
    return jax.nn.sigmoid(x)

def _layernorm(x, axis=-1, eps=1e-05):
    m = jnp.mean(x, axis=axis, keepdims=True)
    v = jnp.var(x, axis=axis, keepdims=True)
    return (x - m) / jnp.sqrt(v + eps)

def _scatter_add(tgt, idx, src, axis=0):
    return tgt.at[idx].add(src)

def _segment_sum(src, seg, n):
    return jax.ops.segment_sum(src, seg, n)
kernel_name = 'mk_seq_postln_d2_jaxref_r4_4ec5d5'

def setup_inputs(seed: int=0):
    np.random.seed(seed)
    _w = jnp.asarray

    def _L0_attn_setup():
        import jax, jax.numpy as jnp
        import numpy as np
        B, S, D, H, DH, FF = (4, 1024, 256, 16, 64, 1024)
        EPS = 1e-06

        def _layer_norm(x, g, b):
            m = jnp.mean(x, axis=-1, keepdims=True)
            v = jnp.mean(jnp.square(x - m), axis=-1, keepdims=True)
            return (x - m) * jax.lax.rsqrt(v + 1e-05) * g + b
        key = jax.random.key(seed)
        ks = jax.random.split(key, 8)
        s = 0.02
        return {'src': jax.random.normal(ks[0], (B, S, D), dtype=jnp.float32), 'Wq': jax.random.normal(ks[1], (D, H * DH), dtype=jnp.float32) * s, 'bq': jnp.zeros((H * DH,), jnp.float32), 'Wk': jax.random.normal(ks[2], (D, H * DH), dtype=jnp.float32) * s, 'bk': jnp.zeros((H * DH,), jnp.float32), 'Wv': jax.random.normal(ks[3], (D, H * DH), dtype=jnp.float32) * s, 'bv': jnp.zeros((H * DH,), jnp.float32), 'Wo': jax.random.normal(ks[4], (H * DH, D), dtype=jnp.float32) * s, 'bo': jnp.zeros((D,), jnp.float32), 'W1': jax.random.normal(ks[5], (D, FF), dtype=jnp.float32) * s, 'b1': jnp.zeros((FF,), jnp.float32), 'W2': jax.random.normal(ks[6], (FF, D), dtype=jnp.float32) * s, 'b2': jnp.zeros((D,), jnp.float32), 'g1': jnp.ones((D,), jnp.float32), 'be1': jnp.zeros((D,), jnp.float32), 'g2': jnp.ones((D,), jnp.float32), 'be2': jnp.zeros((D,), jnp.float32)}
    _L0_attn_in = _L0_attn_setup()

    def _L0_ffn_setup():
        import jax, jax.numpy as jnp
        import numpy as np
        B, S, H, F, E = (1, 512, 256, 512, 8)

        def _swiglu(x, wg, wu, wd):
            return jax.nn.silu(x @ wg.T) * (x @ wu.T) @ wd.T
        key = jax.random.key(seed)
        ks = jax.random.split(key, 8)
        sc = 1.0 / np.sqrt(H)
        scf = 1.0 / np.sqrt(F)
        return {'hidden_states': jax.random.normal(ks[0], (B, S, H), jnp.float32), 'gate_w': jax.random.normal(ks[1], (E, H), jnp.float32) * sc, 'shared_gate': jax.random.normal(ks[2], (F, H), jnp.float32) * sc, 'shared_up': jax.random.normal(ks[3], (F, H), jnp.float32) * sc, 'shared_down': jax.random.normal(ks[4], (H, F), jnp.float32) * scf, 'r_gate': jax.random.normal(ks[5], (E, F, H), jnp.float32) * sc, 'r_up': jax.random.normal(ks[6], (E, F, H), jnp.float32) * sc, 'r_down': jax.random.normal(ks[7], (E, H, F), jnp.float32) * scf}
    _L0_ffn_in = _L0_ffn_setup()

    def _L1_attn_setup():
        import jax, jax.numpy as jnp
        import numpy as np
        D, H, DK, DV, F, R = (256, 16, 64, 64, 1024, 64)
        B, T = (4, 512)
        KCONV = 4
        EPS = 1e-06

        def rmsnorm(x, w):
            return x * jax.lax.rsqrt(jnp.mean(x * x, axis=-1, keepdims=True) + EPS) * w

        def _reference_tuple_inner(x, norm_in_w, conv_w, conv_b, q_w, k_w, v_w, out_w, alpha_w, alpha_b, beta_w, beta_b, head_norm_w, u1_w, u1_b, u2_w, u2_b, ff_norm_w, ff_w1, ff_w3, ff_w2):
            bsz, seq, _ = x.shape
            h = rmsnorm(x, norm_in_w)
            hc = jax.lax.conv_general_dilated(h.transpose(0, 2, 1), conv_w, (1,), [(KCONV - 1, 0)], dimension_numbers=('NCH', 'OIH', 'NCH'), feature_group_count=D)
            h = jax.nn.silu((hc + conv_b[None, :, None]).transpose(0, 2, 1))
            q = (h @ q_w).reshape(bsz, seq, H, DK)
            k = (h @ k_w).reshape(bsz, seq, H, DK)
            v = (h @ v_w).reshape(bsz, seq, H, DV)
            q = q / (jnp.linalg.norm(q, axis=-1, keepdims=True) + EPS)
            k = k / (jnp.linalg.norm(k, axis=-1, keepdims=True) + EPS)
            alpha = jax.nn.sigmoid(h @ alpha_w + alpha_b).reshape(bsz, seq, H, DK)
            beta = jax.nn.sigmoid(h @ beta_w + beta_b)

            def step(s, inp):
                qt, kt, vt, at, bt = inp
                s = s * at[..., None]
                u = jnp.einsum('bhd,bhdv->bhv', kt, s)
                s = s + bt[..., None, None] * (kt[..., None] * (vt - u)[..., None, :])
                out = jnp.einsum('bhdv,bhd->bhv', s, qt)
                return (s, out)
            tm = lambda a: jnp.swapaxes(a, 0, 1)
            s0 = jnp.zeros((bsz, H, DK, DV), x.dtype)
            s_final, outs = jax.lax.scan(step, s0, (tm(q), tm(k), tm(v), tm(alpha), tm(beta)))
            y = tm(outs)
            y = y * jax.lax.rsqrt(jnp.mean(y * y, axis=-1, keepdims=True) + EPS) * head_norm_w
            y = y.reshape(bsz, seq, H * DV)
            gate = jax.nn.sigmoid(jax.nn.silu(x @ u1_w + u1_b) @ u2_w + u2_b)
            y = x + y @ out_w * gate
            y2 = rmsnorm(y, ff_norm_w)
            y = y + jax.nn.silu(y2 @ ff_w1) * (y2 @ ff_w3) @ ff_w2
            return (y, s_final)
        key = jax.random.key(seed)
        ks = jax.random.split(key, 16)
        n = lambda k, shape: jax.random.normal(k, shape, jnp.float32) * 0.02
        return dict(x=jax.random.normal(ks[0], (B, T, D), jnp.float32), norm_in_w=jnp.ones((D,), jnp.float32), conv_w=n(ks[1], (D, 1, KCONV)), conv_b=jnp.zeros((D,), jnp.float32), q_w=n(ks[2], (D, H * DK)), k_w=n(ks[3], (D, H * DK)), v_w=n(ks[4], (D, H * DV)), out_w=n(ks[5], (H * DV, D)), alpha_w=n(ks[6], (D, H * DK)), alpha_b=jnp.zeros((H * DK,), jnp.float32), beta_w=n(ks[7], (D, H)), beta_b=jnp.zeros((H,), jnp.float32), head_norm_w=jnp.ones((H, DV), jnp.float32), u1_w=n(ks[8], (D, R)), u1_b=jnp.zeros((R,), jnp.float32), u2_w=n(ks[9], (R, D)), u2_b=jnp.zeros((D,), jnp.float32), ff_norm_w=jnp.ones((D,), jnp.float32), ff_w1=n(ks[10], (D, F)), ff_w3=n(ks[11], (D, F)), ff_w2=n(ks[12], (F, D)))
    _L1_attn_in = _L1_attn_setup()

    def _L1_ffn_setup():
        import jax, jax.numpy as jnp
        import numpy as np
        DIM = 256

        def _reference_tuple_inner(x, W_r, W_k, W_v, mu_r, mu_k):
            B, T, C = x.shape
            x_prev = jnp.concatenate([jnp.zeros((B, 1, C), x.dtype), x[:, :-1, :]], axis=1)
            xr = mu_r * x + (1.0 - mu_r) * x_prev
            xk = mu_k * x + (1.0 - mu_k) * x_prev
            r = jax.nn.sigmoid(jnp.einsum('btc,dc->btd', xr, W_r))
            k = jnp.einsum('btc,dc->btd', xk, W_k)
            k_act = jnp.square(jax.nn.relu(k))
            out = r * jnp.einsum('btc,dc->btd', k_act, W_v)
            new_state = x[:, -1, :]
            return (out, new_state)
        key = jax.random.key(seed)
        ks = jax.random.split(key, 6)
        B, T, C = (8, 512, DIM)
        x = jax.random.normal(ks[0], (B, T, C), dtype=jnp.float32)
        s = 1.0 / np.sqrt(C)
        W_r = jax.random.uniform(ks[1], (C, C), jnp.float32, -s, s)
        W_k = jax.random.uniform(ks[2], (C, C), jnp.float32, -s, s)
        W_v = jax.random.uniform(ks[3], (C, C), jnp.float32, -s, s)
        mu_r = jax.random.uniform(ks[4], (C,), jnp.float32)
        mu_k = jax.random.uniform(ks[5], (C,), jnp.float32)
        return {'x': x, 'W_r': W_r, 'W_k': W_k, 'W_v': W_v, 'mu_r': mu_r, 'mu_k': mu_k}
    _L1_ffn_in = _L1_ffn_setup()
    _d = {'L0_attn_src': _L0_attn_in['src'], 'L0_attn_Wq': _L0_attn_in['Wq'], 'L0_attn_bq': _L0_attn_in['bq'], 'L0_attn_Wk': _L0_attn_in['Wk'], 'L0_attn_bk': _L0_attn_in['bk'], 'L0_attn_Wv': _L0_attn_in['Wv'], 'L0_attn_bv': _L0_attn_in['bv'], 'L0_attn_Wo': _L0_attn_in['Wo'], 'L0_attn_bo': _L0_attn_in['bo'], 'L0_attn_W1': _L0_attn_in['W1'], 'L0_attn_b1': _L0_attn_in['b1'], 'L0_attn_W2': _L0_attn_in['W2'], 'L0_attn_b2': _L0_attn_in['b2'], 'L0_attn_g1': _L0_attn_in['g1'], 'L0_attn_be1': _L0_attn_in['be1'], 'L0_attn_g2': _L0_attn_in['g2'], 'L0_attn_be2': _L0_attn_in['be2'], 'L0_ffn_gate_w': _L0_ffn_in['gate_w'], 'L0_ffn_shared_gate': _L0_ffn_in['shared_gate'], 'L0_ffn_shared_up': _L0_ffn_in['shared_up'], 'L0_ffn_shared_down': _L0_ffn_in['shared_down'], 'L0_ffn_r_gate': _L0_ffn_in['r_gate'], 'L0_ffn_r_up': _L0_ffn_in['r_up'], 'L0_ffn_r_down': _L0_ffn_in['r_down'], 'L1_attn_norm_in_w': _L1_attn_in['norm_in_w'], 'L1_attn_conv_w': _L1_attn_in['conv_w'], 'L1_attn_conv_b': _L1_attn_in['conv_b'], 'L1_attn_q_w': _L1_attn_in['q_w'], 'L1_attn_k_w': _L1_attn_in['k_w'], 'L1_attn_v_w': _L1_attn_in['v_w'], 'L1_attn_out_w': _L1_attn_in['out_w'], 'L1_attn_alpha_w': _L1_attn_in['alpha_w'], 'L1_attn_alpha_b': _L1_attn_in['alpha_b'], 'L1_attn_beta_w': _L1_attn_in['beta_w'], 'L1_attn_beta_b': _L1_attn_in['beta_b'], 'L1_attn_head_norm_w': _L1_attn_in['head_norm_w'], 'L1_attn_u1_w': _L1_attn_in['u1_w'], 'L1_attn_u1_b': _L1_attn_in['u1_b'], 'L1_attn_u2_w': _L1_attn_in['u2_w'], 'L1_attn_u2_b': _L1_attn_in['u2_b'], 'L1_attn_ff_norm_w': _L1_attn_in['ff_norm_w'], 'L1_attn_ff_w1': _L1_attn_in['ff_w1'], 'L1_attn_ff_w3': _L1_attn_in['ff_w3'], 'L1_attn_ff_w2': _L1_attn_in['ff_w2'], 'L1_ffn_W_r': _L1_ffn_in['W_r'], 'L1_ffn_W_k': _L1_ffn_in['W_k'], 'L1_ffn_W_v': _L1_ffn_in['W_v'], 'L1_ffn_mu_r': _L1_ffn_in['mu_r'], 'L1_ffn_mu_k': _L1_ffn_in['mu_k']}
    _x0 = _d['L0_attn_src']
    _d['L0_attn_src'] = jax.random.normal(jax.random.fold_in(jax.random.key(seed), 1), (2, 2048, 256), dtype=_x0.dtype)
    del _x0
    return _d

def reference(L0_attn_src, L0_attn_Wq, L0_attn_bq, L0_attn_Wk, L0_attn_bk, L0_attn_Wv, L0_attn_bv, L0_attn_Wo, L0_attn_bo, L0_attn_W1, L0_attn_b1, L0_attn_W2, L0_attn_b2, L0_attn_g1, L0_attn_be1, L0_attn_g2, L0_attn_be2, L0_ffn_gate_w, L0_ffn_shared_gate, L0_ffn_shared_up, L0_ffn_shared_down, L0_ffn_r_gate, L0_ffn_r_up, L0_ffn_r_down, L1_attn_norm_in_w, L1_attn_conv_w, L1_attn_conv_b, L1_attn_q_w, L1_attn_k_w, L1_attn_v_w, L1_attn_out_w, L1_attn_alpha_w, L1_attn_alpha_b, L1_attn_beta_w, L1_attn_beta_b, L1_attn_head_norm_w, L1_attn_u1_w, L1_attn_u1_b, L1_attn_u2_w, L1_attn_u2_b, L1_attn_ff_norm_w, L1_attn_ff_w1, L1_attn_ff_w3, L1_attn_ff_w2, L1_ffn_W_r, L1_ffn_W_k, L1_ffn_W_v, L1_ffn_mu_r, L1_ffn_mu_k):

    def _L0_attn_ref(src, Wq, bq, Wk, bk, Wv, bv, Wo, bo, W1, b1, W2, b2, g1, be1, g2, be2):
        import jax, jax.numpy as jnp
        import numpy as np
        B, S, D, H, DH, FF = (4, 1024, 256, 16, 64, 1024)
        EPS = 1e-06

        def _layer_norm(x, g, b):
            m = jnp.mean(x, axis=-1, keepdims=True)
            v = jnp.mean(jnp.square(x - m), axis=-1, keepdims=True)
            return (x - m) * jax.lax.rsqrt(v + 1e-05) * g + b
        b, s = (src.shape[0], src.shape[1])
        q = (src @ Wq + bq).reshape(b, s, H, DH)
        k = (src @ Wk + bk).reshape(b, s, H, DH)
        v = (src @ Wv + bv).reshape(b, s, H, DH)
        Q = jax.nn.elu(q) + 1.0
        K = jax.nn.elu(k) + 1.0
        KV = jnp.einsum('bshd,bshm->bhdm', K, v)
        Z = 1.0 / (jnp.einsum('bshd,bhd->bsh', Q, K.sum(axis=1)) + EPS)
        o = jnp.einsum('bshd,bhdm,bsh->bshm', Q, KV, Z).reshape(b, s, H * DH)
        attn_out = o @ Wo + bo
        x = _layer_norm(src + attn_out, g1, be1)
        y = jax.nn.gelu(x @ W1 + b1, approximate=False) @ W2 + b2
        return _layer_norm(x + y, g2, be2)

    def _L0_ffn_ref(hidden_states, gate_w, shared_gate, shared_up, shared_down, r_gate, r_up, r_down):
        import jax, jax.numpy as jnp
        import numpy as np
        B, S, H, F, E = (1, 512, 256, 512, 8)

        def _swiglu(x, wg, wu, wd):
            return jax.nn.silu(x @ wg.T) * (x @ wu.T) @ wd.T
        b, s, h = hidden_states.shape
        x = hidden_states.reshape(-1, h)
        shared_out = _swiglu(x, shared_gate, shared_up, shared_down)
        logits = x @ gate_w.T
        top_id = jnp.argmax(logits, axis=-1)
        score = jax.nn.sigmoid(jnp.max(logits, axis=-1))
        xs = x * score[:, None]

        def body(acc, ws):
            wg, wu, wd, e = ws
            xe = jnp.where((top_id == e)[:, None], xs, 0.0)
            return (acc + _swiglu(xe, wg, wu, wd), None)
        acc0 = jnp.zeros_like(x)
        routed_out, _ = jax.lax.scan(body, acc0, (r_gate, r_up, r_down, jnp.arange(E)))
        return (shared_out + routed_out).reshape(b, s, h)

    def _L1_attn_ref(x, norm_in_w, conv_w, conv_b, q_w, k_w, v_w, out_w, alpha_w, alpha_b, beta_w, beta_b, head_norm_w, u1_w, u1_b, u2_w, u2_b, ff_norm_w, ff_w1, ff_w3, ff_w2):
        import jax, jax.numpy as jnp
        import numpy as np
        D, H, DK, DV, F, R = (256, 16, 64, 64, 1024, 64)
        B, T = (4, 512)
        KCONV = 4
        EPS = 1e-06

        def rmsnorm(x, w):
            return x * jax.lax.rsqrt(jnp.mean(x * x, axis=-1, keepdims=True) + EPS) * w

        def _reference_tuple_inner(x, norm_in_w, conv_w, conv_b, q_w, k_w, v_w, out_w, alpha_w, alpha_b, beta_w, beta_b, head_norm_w, u1_w, u1_b, u2_w, u2_b, ff_norm_w, ff_w1, ff_w3, ff_w2):
            bsz, seq, _ = x.shape
            h = rmsnorm(x, norm_in_w)
            hc = jax.lax.conv_general_dilated(h.transpose(0, 2, 1), conv_w, (1,), [(KCONV - 1, 0)], dimension_numbers=('NCH', 'OIH', 'NCH'), feature_group_count=D)
            h = jax.nn.silu((hc + conv_b[None, :, None]).transpose(0, 2, 1))
            q = (h @ q_w).reshape(bsz, seq, H, DK)
            k = (h @ k_w).reshape(bsz, seq, H, DK)
            v = (h @ v_w).reshape(bsz, seq, H, DV)
            q = q / (jnp.linalg.norm(q, axis=-1, keepdims=True) + EPS)
            k = k / (jnp.linalg.norm(k, axis=-1, keepdims=True) + EPS)
            alpha = jax.nn.sigmoid(h @ alpha_w + alpha_b).reshape(bsz, seq, H, DK)
            beta = jax.nn.sigmoid(h @ beta_w + beta_b)

            def step(s, inp):
                qt, kt, vt, at, bt = inp
                s = s * at[..., None]
                u = jnp.einsum('bhd,bhdv->bhv', kt, s)
                s = s + bt[..., None, None] * (kt[..., None] * (vt - u)[..., None, :])
                out = jnp.einsum('bhdv,bhd->bhv', s, qt)
                return (s, out)
            tm = lambda a: jnp.swapaxes(a, 0, 1)
            s0 = jnp.zeros((bsz, H, DK, DV), x.dtype)
            s_final, outs = jax.lax.scan(step, s0, (tm(q), tm(k), tm(v), tm(alpha), tm(beta)))
            y = tm(outs)
            y = y * jax.lax.rsqrt(jnp.mean(y * y, axis=-1, keepdims=True) + EPS) * head_norm_w
            y = y.reshape(bsz, seq, H * DV)
            gate = jax.nn.sigmoid(jax.nn.silu(x @ u1_w + u1_b) @ u2_w + u2_b)
            y = x + y @ out_w * gate
            y2 = rmsnorm(y, ff_norm_w)
            y = y + jax.nn.silu(y2 @ ff_w1) * (y2 @ ff_w3) @ ff_w2
            return (y, s_final)
        return _reference_tuple_inner(x, norm_in_w, conv_w, conv_b, q_w, k_w, v_w, out_w, alpha_w, alpha_b, beta_w, beta_b, head_norm_w, u1_w, u1_b, u2_w, u2_b, ff_norm_w, ff_w1, ff_w3, ff_w2)[0]

    def _L1_ffn_ref(x, W_r, W_k, W_v, mu_r, mu_k):
        import jax, jax.numpy as jnp
        import numpy as np
        DIM = 256

        def _reference_tuple_inner(x, W_r, W_k, W_v, mu_r, mu_k):
            B, T, C = x.shape
            x_prev = jnp.concatenate([jnp.zeros((B, 1, C), x.dtype), x[:, :-1, :]], axis=1)
            xr = mu_r * x + (1.0 - mu_r) * x_prev
            xk = mu_k * x + (1.0 - mu_k) * x_prev
            r = jax.nn.sigmoid(jnp.einsum('btc,dc->btd', xr, W_r))
            k = jnp.einsum('btc,dc->btd', xk, W_k)
            k_act = jnp.square(jax.nn.relu(k))
            out = r * jnp.einsum('btc,dc->btd', k_act, W_v)
            new_state = x[:, -1, :]
            return (out, new_state)
        return _reference_tuple_inner(x, W_r, W_k, W_v, mu_r, mu_k)[0]
    x = L0_attn_src
    x = _layernorm(x + _L0_attn_ref(x, L0_attn_Wq, L0_attn_bq, L0_attn_Wk, L0_attn_bk, L0_attn_Wv, L0_attn_bv, L0_attn_Wo, L0_attn_bo, L0_attn_W1, L0_attn_b1, L0_attn_W2, L0_attn_b2, L0_attn_g1, L0_attn_be1, L0_attn_g2, L0_attn_be2), axis=-1)
    x = _layernorm(x + _L0_ffn_ref(x, L0_ffn_gate_w, L0_ffn_shared_gate, L0_ffn_shared_up, L0_ffn_shared_down, L0_ffn_r_gate, L0_ffn_r_up, L0_ffn_r_down), axis=-1)
    x = _layernorm(x + _L1_attn_ref(x, L1_attn_norm_in_w, L1_attn_conv_w, L1_attn_conv_b, L1_attn_q_w, L1_attn_k_w, L1_attn_v_w, L1_attn_out_w, L1_attn_alpha_w, L1_attn_alpha_b, L1_attn_beta_w, L1_attn_beta_b, L1_attn_head_norm_w, L1_attn_u1_w, L1_attn_u1_b, L1_attn_u2_w, L1_attn_u2_b, L1_attn_ff_norm_w, L1_attn_ff_w1, L1_attn_ff_w3, L1_attn_ff_w2), axis=-1)
    x = _layernorm(x + _L1_ffn_ref(x, L1_ffn_W_r, L1_ffn_W_k, L1_ffn_W_v, L1_ffn_mu_r, L1_ffn_mu_k), axis=-1)
    return x

_drawn_inputs = setup_inputs


def setup_inputs(seed=0):
    import zlib

    import numpy as np

    out = dict(_drawn_inputs(seed))
    spreads = {'L0_attn_bq': (0.0, 2.0),
     'L0_attn_bk': (0.0, 2.0),
     'L0_attn_bv': (0.0, 0.1),
     'L0_attn_bo': (0.0, 0.1),
     'L0_attn_b1': (0.0, 0.1),
     'L0_attn_b2': (0.0, 0.1),
     'L0_attn_g1': (1.0, 0.2),
     'L0_attn_be1': (0.0, 0.1),
     'L0_attn_g2': (1.0, 0.2),
     'L0_attn_be2': (0.0, 0.1),
     'L1_attn_norm_in_w': (1.0, 0.6),
     'L1_attn_conv_b': (0.0, 0.1),
     'L1_attn_alpha_b': (0.0, 0.8),
     'L1_attn_beta_b': (0.0, 0.8),
     'L1_attn_head_norm_w': (1.0, 0.6),
     'L1_attn_u1_b': (0.0, 0.8),
     'L1_attn_u2_b': (0.0, 0.8),
     'L1_attn_ff_norm_w': (1.0, 0.6)}
    factors = {'L0_attn_Wq': 24.321,
     'L0_attn_Wk': 8.0,
     'L0_attn_Wv': 5.091,
     'L1_attn_alpha_w': 8.0,
     'L1_attn_beta_w': 34.44,
     'L1_attn_u1_w': 8.0,
     'L1_attn_u2_w': 8.0,
     'L1_attn_ff_w1': 3.196,
     'L1_attn_ff_w3': 3.162,
     'L1_attn_ff_w2': 3.163,
     'L1_ffn_W_r': 3.128,
     'L1_ffn_mu_r': 6.385}
    for name, (base, spread) in spreads.items():
        noise = np.random.default_rng([zlib.crc32(name.encode()), seed]).standard_normal(out[name].shape)
        drawn = base * np.exp(spread * noise) if base else spread * noise
        out[name] = jnp.asarray(drawn.astype(out[name].dtype))
    for name, factor in factors.items():
        out[name] = (out[name] * factor).astype(out[name].dtype)
    return out
```

```python
from contextlib import ExitStack

import numpy as np

import concourse.bass as bass
from concourse import mybir

F32 = mybir.dt.float32
ACT = mybir.ActivationFunctionType
ALU = mybir.AluOpType
AX_X = mybir.AxisListType.X

P = 128
NB, T = 2, 2048
D = 256
KD = D // P
H, DH = 16, 64
HP = H // 2
FF = 1024
KF = FF // P
NE, FE = 8, 512
BLK = 512
NBLK = T // BLK
CH = 64
NCH = BLK // CH
PAD = 4


def phase_semaphore(nc, ctx, name):
    s = nc.alloc_semaphore(name)
    ctx.callback(nc.clear_and_free_semaphores, [s])
    return s


def decoder_program(nc, io, phases="ACDFE"):
    with ExitStack() as ctx:
        def sem(name):
            return ctx.enter_context(nc.semaphore(name))

        x = ctx.enter_context(nc.sbuf_tensor("x", [P, KD, NB, PAD + T], F32))
        ones = ctx.enter_context(nc.sbuf_tensor("mean_ones", [P, P], F32))
        x_loaded, consts_ready = sem("x_loaded"), sem("consts_ready")
        x_padded = sem("x_padded")
        with nc.Block() as block:
            @block.sync
            def _(sp):
                for k in range(KD):
                    sp.dma_start(x[:, k, :, PAD:], io["x"][:, k]).then_inc(x_loaded, 16)
                sp.wait_ge(x_loaded, 16 * KD)
                sp.wait_ge(consts_ready, 1)
                sp.wait_ge(x_padded, 1)

            @block.gpsimd
            def _(pool):
                nc.gpsimd.memset(ones[:], 1.0 / D).then_inc(consts_ready, 1)
                nc.gpsimd.memset(x[:, :, :, 0:PAD], 0.0).then_inc(x_padded, 1)
        if "A" in phases:
            linear_attention(nc, io, x, ones)
            nc.all_engine_barrier()
        if "C" in phases:
            experts(nc, io, x, ones)
            nc.all_engine_barrier()
        if "D" in phases:
            delta_rule(nc, io, x, ones)
            nc.all_engine_barrier()
        if "F" in phases:
            delta_feed_forward(nc, io, x, ones)
            nc.all_engine_barrier()
        if "E" in phases:
            channel_mix(nc, io, x, ones)
        else:
            stored = sem("stored")
            with nc.Block() as block:
                @block.sync
                def _(sp):
                    for k in range(KD):
                        sp.dma_start(io["out"][:, k], x[:, k, :, PAD:]).then_inc(stored, 16)
                    sp.wait_ge(stored, 16 * KD)


class Norm:

    def __init__(self, nc, ctx, name, ones, centred=True):
        self.nc, self.ones, self.centred = nc, ones, centred
        sem = lambda s: phase_semaphore(nc, ctx, f"{name}_{s}")
        self.mean_ready, self.centre_ready = sem("mean_ready"), sem("centre_ready")
        self.square_ready, self.var_ready, self.rstd_ready = sem("square_ready"), sem("var_ready"), sem("rstd_ready")
        self.std_ready, self.done = sem("std_ready"), sem("done")
        self.square = ctx.enter_context(nc.sbuf_tensor(f"{name}_square", [P, KD, BLK], F32))
        self.centre = ctx.enter_context(nc.sbuf_tensor(f"{name}_centre", [P, KD, BLK], F32))
        self.std = ctx.enter_context(nc.sbuf_tensor(f"{name}_std", [P, BLK], F32))
        self.eps = ctx.enter_context(nc.sbuf_tensor(f"{name}_eps", [P, 1], F32))
        self.rstd = ctx.enter_context(nc.sbuf_tensor(f"{name}_rstd", [P, BLK], F32))

    def tensor(self, pe, n, z, z_ready, z_value, mean_psum, var_psum):
        nc = self.nc
        if self.centred:
            pe.wait_ge(z_ready, z_value)
            for k in range(KD):
                mm = nc.tensor.matmul(mean_psum, self.ones[:], z[:, k], start=(k == 0), stop=(k == KD - 1))
            mm.then_inc(self.mean_ready, 1)
        pe.wait_ge(self.square_ready, n + 1)
        for k in range(KD):
            mm = nc.tensor.matmul(var_psum, self.ones[:], self.square[:, k], start=(k == 0), stop=(k == KD - 1))
        mm.then_inc(self.var_ready, 1)

    def scalar(self, act, n, var_psum, z=None, z_ready=None, z_value=None, after_rstd=True):
        if self.centred:
            act.wait_ge(self.centre_ready, n + 1)
            z = self.centre
        else:
            act.wait_ge(z_ready, z_value)
        self.nc.scalar.activation(self.square[:], z[:], ACT.Square).then_inc(self.square_ready, 1)
        act.wait_ge(self.var_ready, n + 1)
        if after_rstd:
            act.wait_ge(self.rstd_ready, n)
        self.nc.scalar.activation(self.std[:], var_psum, ACT.Sqrt, bias=self.eps[:]).then_inc(self.std_ready, 1)

    def vector(self, dve, n, z, out, mean_psum):
        nc = self.nc
        if self.centred:
            dve.wait_ge(self.mean_ready, n + 1)
            nc.vector.tensor_tensor(self.centre[:], z[:], mean_psum.unsqueeze(1).broadcast_to([P, KD, BLK]),
                                    ALU.subtract).then_inc(self.centre_ready, 1)
            z = self.centre
        dve.wait_ge(self.std_ready, n + 1)
        nc.vector.reciprocal(self.rstd[:], self.std[:]).then_inc(self.rstd_ready, 1)
        dve.wait_ge(self.rstd_ready, n + 1)
        nc.vector.tensor_tensor(out, z[:], self.rstd[:].unsqueeze(1).broadcast_to([P, KD, BLK]),
                                ALU.mult).then_inc(self.done, 1)


def linear_attention(nc, io, x, ones):
    with ExitStack() as ctx:
        def sem(name):
            return phase_semaphore(nc, ctx, name)

        def sb(name, shape):
            return ctx.enter_context(nc.sbuf_tensor(name, shape, F32))

        def ps(name, shape):
            return ctx.enter_context(nc.psum_tensor(name, shape, F32))

        wq, wk, wv = sb("wq", [P, KD, FF]), sb("wk", [P, KD, FF]), sb("wv", [P, KD, FF])
        wo, w1, w2 = sb("wo", [P, HP, D]), sb("w1", [P, KD, FF]), sb("w2", [P, KF, D])
        bk, bv = sb("bk", [P, FF]), sb("bv", [P, FF])
        cols = sb("l0_columns", [P, 8 + 8 + 2 * 6])
        bq, b1 = cols[:, 0:8], cols[:, 8:16]
        bo, b2, g1, be1, g2, be2 = (cols[:, 16 + 2 * j:18 + 2 * j] for j in range(6))
        pair_mask = sb("pair_mask", [P, P])
        zeros = sb("zeros", [P, BLK])
        x_tile = sb("x_tile", [P, KD, P])
        k_raw, k_exp, k_elu = sb("k_raw", [P, FF]), sb("k_exp", [P, FF]), sb("k_elu", [P, FF])
        v_one = sb("v_one", [P, HP, P + 1])
        kv, ksum = sb("kv", [P, HP, P]), sb("ksum", [P, HP, P])
        q_exp, q_relu, q_elu = sb("q_exp", [P, 2, BLK]), sb("q_relu", [P, 2, BLK]), sb("q_elu", [P, 2, BLK])
        den = sb("den", [P, 2, BLK])
        o = sb("o", [P, HP, BLK])
        z, y = sb("z", [P, KD, BLK]), sb("y", [P, KD, BLK])
        hidden = o
        norm = Norm(nc, ctx, "l0_norm", ones)

        weights_in, masked, cleared = sem("l0_weights_in"), sem("l0_mask_ready"), sem("l0_cleared")
        tile_in, k_psum_ready, v_psum_ready = sem("tile_in"), sem("k_psum_ready"), sem("v_psum_ready")
        k_raw_ready, k_exp_ready, k_min_ready = sem("k_raw_ready"), sem("k_exp_ready"), sem("k_min_ready")
        k_ready, v_ready, kv_added = sem("k_ready"), sem("v_ready"), sem("kv_added")
        kv_summed, kv_ready = sem("kv_summed"), sem("kv_ready")
        q_psum_ready, q_exp_ready, q_relu_ready, q_ready = sem("q_psum_ready"), sem("q_exp_ready"), sem("q_relu_ready"), sem("q_ready")
        num_ready, den_ready, inv_ready, o_ready = sem("num_ready"), sem("den_ready"), sem("inv_ready"), sem("o_ready")
        wo_ready, z_ready, ln1_ready = sem("wo_ready"), sem("z_ready"), sem("ln1_ready")
        h_psum_ready, hidden_ready, w2_ready, x_written = sem("h_psum_ready"), sem("hidden_ready"), sem("w2_ready"), sem("x_written")
        ln2_ready = sem("ln2_ready")

        NT = T // P
        n_weights = 11

        def kv_pass(b):
            with ExitStack() as cp:
                k_ps = cp.enter_context(nc.psum_tensor(f"k_ps{b}", [P, FF], F32))
                v_ps = cp.enter_context(nc.psum_tensor(f"v_ps{b}", [P, FF], F32))
                kv_ps = cp.enter_context(nc.psum_tensor(f"kv_ps{b}", [P, 3, BLK], F32))
                W = P + 1

                def pair(hp):
                    return kv_ps[:, hp // 3, W * (hp % 3):W * (hp % 3) + W]

                with nc.Block() as block:
                    @block.sync
                    def _(sp):
                        if b == 0:
                            for dst, name in ((wk, "wk"), (wv, "wv"), (bk, "bk"), (bv, "bv"), (cols, "l0_cols"),
                                              (pair_mask, "pair_mask"), (wq, "wq"), (wo, "wo"), (w1, "w1"), (w2, "w2")):
                                sp.dma_start(dst[:], io[name]).then_inc(weights_in, 16)
                        with sp.Fori(0, NT) as t:
                            sp.wait_ge(v_psum_ready, t + NT * b)
                            sp.dma_start(x_tile[:], io["x"][:, :, b, bass.ds(t * P, P)]).then_inc(tile_in, 16)

                    @block.gpsimd
                    def _(pool):
                        if b == 0:
                            nc.gpsimd.memset(norm.eps[:], 1e-5).then_inc(cleared, 1)
                            nc.gpsimd.memset(zeros[:], 0.0).then_inc(cleared, 1)
                            nc.gpsimd.memset(v_one[:, :, P:W], 1.0).then_inc(cleared, 1)

                    @block.scalar
                    def _(act):
                        with act.Fori(0, NT) as t:
                            act.wait_ge(k_raw_ready, t + (NT * b + 1))
                            act.wait_ge(k_ready, t + NT * b)
                            nc.scalar.activation(k_exp[:], k_raw[:], ACT.Exp).then_inc(k_exp_ready, 1)

                    @block.vector
                    def _(dve):
                        if b == 0:
                            dve.wait_ge(weights_in, 16 * 10)
                            dve.wait_ge(cleared, 3)
                        with dve.Fori(0, NT) as t:
                            n = t + NT * b
                            dve.wait_ge(k_psum_ready, n + 1)
                            nc.vector.tensor_tensor(k_raw[:], k_ps[:], bk[:], ALU.add).then_inc(k_raw_ready, 1)
                            dve.wait_ge(v_psum_ready, n + 1)
                            dve.wait_ge(kv_added, n)
                            nc.vector.tensor_tensor(v_one[:, :, 0:P], v_ps[:].rearrange("p (h c) -> p h c", c=P),
                                                    bv[:].rearrange("p (h c) -> p h c", c=P), ALU.add).then_inc(v_ready, 1)
                            dve.wait_ge(k_exp_ready, n + 1)
                            nc.vector.tensor_scalar(k_exp[:], k_exp[:], 1.0, None, ALU.min).then_inc(k_min_ready, 1)
                            dve.wait_ge(k_min_ready, n + 1)
                            nc.vector.scalar_tensor_tensor(k_elu[:], k_raw[:], 0.0, k_exp[:], ALU.max, ALU.add).then_inc(k_ready, 1)
                        dve.wait_ge(kv_summed, b + 1)
                        for hp in range(HP):
                            nc.vector.tensor_tensor(kv[:, hp], pair(hp)[:, 0:P], pair_mask[:], ALU.mult).then_inc(kv_ready, 1)
                            nc.vector.tensor_scalar(ksum[:, hp], pair_mask[:], pair(hp)[:, P:W], None, ALU.mult).then_inc(kv_ready, 1)
                        dve.wait_ge(kv_ready, 2 * HP * (b + 1))

                    @block.tensor
                    def _(pe):
                        if b == 0:
                            pe.wait_ge(weights_in, 16 * 10)
                            pe.wait_ge(cleared, 3)
                        for j in range(3):
                            nc.tensor.matmul(kv_ps[:, j, 0:3 * W], zeros[:, 0:P], zeros[:, 0:3 * W], start=True, stop=False,
                                             skip_group_check=True)
                        with pe.Fori(0, NT) as t:
                            n = t + NT * b
                            pe.wait_ge(tile_in, 16 * n + 16)
                            pe.wait_ge(k_raw_ready, n)
                            for half in range(2):
                                for k in range(KD):
                                    mm = nc.tensor.matmul(k_ps[:, BLK * half:BLK * half + BLK], x_tile[:, k],
                                                          wk[:, k, BLK * half:BLK * half + BLK], start=(k == 0), stop=(k == KD - 1))
                            mm.then_inc(k_psum_ready, 1)
                            pe.wait_ge(v_ready, n)
                            for half in range(2):
                                for k in range(KD):
                                    mm = nc.tensor.matmul(v_ps[:, BLK * half:BLK * half + BLK], x_tile[:, k],
                                                          wv[:, k, BLK * half:BLK * half + BLK], start=(k == 0), stop=(k == KD - 1))
                            mm.then_inc(v_psum_ready, 1)
                            pe.wait_ge(v_ready, n + 1)
                            pe.wait_ge(k_ready, n + 1)
                            for hp in range(HP):
                                mm = nc.tensor.matmul(pair(hp), k_elu[:, P * hp:P * hp + P], v_one[:, hp], start=False, stop=False,
                                                      skip_group_check=True)
                            mm.then_inc(kv_added, 1)
                        for j in range(3):
                            mm = nc.tensor.matmul(kv_ps[:, j, 0:3 * W], zeros[:, 0:P], zeros[:, 0:3 * W], start=False, stop=True,
                                                  skip_group_check=True)
                        mm.then_inc(kv_summed, 1)

        def block_pass(b):
            with ExitStack() as cp:
                bank = [cp.enter_context(nc.psum_tensor(f"l0_bank{b}_{j}", [P, BLK], F32)) for j in range(8)]
                q_ps, num_ps, den_ps, acc = bank[0:2], bank[2:4], bank[4:6], bank[6:8]
                h_ps, mean_ps, var_ps = bank[0:4], bank[4], bank[5]

                with nc.Block() as block:
                    @block.tensor
                    def _(pe):
                        with pe.Fori(0, NBLK) as i:
                            n = i + NBLK * b
                            pe.wait_ge(x_written, n)
                            for hp in range(HP + 1):
                                if hp < HP:
                                    if hp >= 2:
                                        pe.wait_ge(q_exp_ready, HP * n + (hp - 1))
                                        pe.wait_ge(q_relu_ready, HP * n + (hp - 1))
                                    for k in range(KD):
                                        mm = nc.tensor.matmul(q_ps[hp % 2][:], wq[:, k, P * hp:P * hp + P],
                                                              x[:, k, b, bass.ds(PAD + i * BLK, BLK)], start=(k == 0), stop=(k == KD - 1))
                                    mm.then_inc(q_psum_ready, 1)
                                if hp >= 1:
                                    g = hp - 1
                                    pe.wait_ge(q_ready, HP * n + (g + 1))
                                    if g >= 2:
                                        pe.wait_ge(o_ready, HP * n + (g - 1))
                                    nc.tensor.matmul(den_ps[g % 2][:], ksum[:, g], q_elu[:, g % 2], start=True, stop=True).then_inc(den_ready, 1)
                                    nc.tensor.matmul(num_ps[g % 2][:], kv[:, g], q_elu[:, g % 2], start=True, stop=True).then_inc(num_ready, 1)
                            for hp in range(HP):
                                pe.wait_ge(o_ready, HP * n + (hp + 1))
                                for m in range(KD):
                                    mm = nc.tensor.matmul(acc[m][:], wo[:, hp, P * m:P * m + P], o[:, hp], start=(hp == 0), stop=(hp == HP - 1))
                            mm.then_inc(wo_ready, 1)
                            norm.tensor(pe, 3 * n, z, z_ready, 3 * n + 1, mean_ps[:], var_ps[:])
                            pe.wait_ge(ln1_ready, 2 * n + 2)
                            for m in range(KF):
                                if m >= 4:
                                    pe.wait_ge(hidden_ready, KF * n + (m - 3))
                                for k in range(KD):
                                    mm = nc.tensor.matmul(h_ps[m % 4][:], w1[:, k, P * m:P * m + P], y[:, k], start=(k == 0), stop=(k == KD - 1))
                                mm.then_inc(h_psum_ready, 1)
                            for f in range(KF):
                                pe.wait_ge(hidden_ready, KF * n + (f + 1))
                                for m in range(KD):
                                    mm = nc.tensor.matmul(acc[m][:], w2[:, f, P * m:P * m + P], hidden[:, f], start=(f == 0), stop=(f == KF - 1))
                            mm.then_inc(w2_ready, 1)
                            norm.tensor(pe, 3 * n + 1, z, z_ready, 3 * n + 2, mean_ps[:], var_ps[:])
                            norm.tensor(pe, 3 * n + 2, z, z_ready, 3 * n + 3, mean_ps[:], var_ps[:])

                    @block.scalar
                    def _(act):
                        with act.Fori(0, NBLK) as i:
                            n = i + NBLK * b
                            for hp in range(HP):
                                act.wait_ge(q_psum_ready, HP * n + (hp + 1))
                                if hp >= 2:
                                    act.wait_ge(q_ready, HP * n + (hp - 1))
                                nc.scalar.activation(q_exp[:, hp % 2], q_ps[hp % 2][:], ACT.Exp, bias=bq[:, hp:hp + 1]).then_inc(q_exp_ready, 1)
                                nc.scalar.activation(q_relu[:, hp % 2], q_ps[hp % 2][:], ACT.Relu, bias=bq[:, hp:hp + 1]).then_inc(q_relu_ready, 1)
                            norm.scalar(act, 3 * n, var_ps[:])
                            for m in range(KF):
                                act.wait_ge(h_psum_ready, KF * n + (m + 1))
                                nc.scalar.activation(hidden[:, m], h_ps[m % 4][:], ACT.Gelu, bias=b1[:, m:m + 1]).then_inc(hidden_ready, 1)
                            norm.scalar(act, 3 * n + 1, var_ps[:])
                            norm.scalar(act, 3 * n + 2, var_ps[:])

                    @block.vector
                    def _(dve):
                        with dve.Fori(0, NBLK) as i:
                            n = i + NBLK * b
                            x_block = x[:, :, b, bass.ds(PAD + i * BLK, BLK)]
                            for hp in range(HP + 1):
                                if hp < HP:
                                    dve.wait_ge(q_exp_ready, HP * n + (hp + 1))
                                    dve.wait_ge(q_relu_ready, HP * n + (hp + 1))
                                    if hp >= 2:
                                        dve.wait_ge(num_ready, HP * n + (hp - 1))
                                    nc.vector.scalar_tensor_tensor(q_elu[:, hp % 2], q_exp[:, hp % 2], 1.0, q_relu[:, hp % 2],
                                                                   ALU.min, ALU.add).then_inc(q_ready, 1)
                                if hp >= 1:
                                    g = hp - 1
                                    dve.wait_ge(den_ready, HP * n + (g + 1))
                                    nc.vector.tensor_scalar(den[:, g % 2], den_ps[g % 2][:], 1e-6, None, ALU.add).then_inc(inv_ready, 1)
                                    dve.wait_ge(inv_ready, 2 * HP * n + (2 * g + 1))
                                    nc.vector.reciprocal(den[:, g % 2], den[:, g % 2]).then_inc(inv_ready, 1)
                                    dve.wait_ge(inv_ready, 2 * HP * n + (2 * g + 2))
                                    dve.wait_ge(num_ready, HP * n + (g + 1))
                                    nc.vector.tensor_tensor(o[:, g], num_ps[g % 2][:], den[:, g % 2], ALU.mult).then_inc(o_ready, 1)
                            dve.wait_ge(wo_ready, n + 1)
                            for m in range(KD):
                                last = nc.vector.scalar_tensor_tensor(z[:, m], acc[m][:], bo[:, m:m + 1], x_block[:, m], ALU.add, ALU.add)
                            last.then_inc(z_ready, 1)
                            dve.wait_ge(z_ready, 3 * n + 1)
                            norm.vector(dve, 3 * n, z, y[:], mean_ps[:])
                            dve.wait_ge(norm.done, 3 * n + 1)
                            for m in range(KD):
                                nc.vector.tensor_scalar(y[:, m], y[:, m], g1[:, m:m + 1], be1[:, m:m + 1], ALU.mult, ALU.add).then_inc(ln1_ready, 1)
                            dve.wait_ge(w2_ready, n + 1)
                            dve.wait_ge(ln1_ready, 2 * n + 2)
                            for m in range(KD):
                                last = nc.vector.scalar_tensor_tensor(z[:, m], acc[m][:], b2[:, m:m + 1], y[:, m], ALU.add, ALU.add)
                            last.then_inc(z_ready, 1)
                            norm.vector(dve, 3 * n + 1, z, y[:], mean_ps[:])
                            dve.wait_ge(norm.done, 3 * n + 2)
                            for m in range(KD):
                                nc.vector.tensor_scalar(y[:, m], y[:, m], g2[:, m:m + 1], be2[:, m:m + 1], ALU.mult, ALU.add).then_inc(ln2_ready, 1)
                            dve.wait_ge(ln2_ready, 2 * n + 2)
                            nc.vector.tensor_tensor(z[:], y[:], x_block, ALU.add).then_inc(z_ready, 1)
                            norm.vector(dve, 3 * n + 2, z, x_block, mean_ps[:])
                            dve.wait_ge(norm.done, 3 * n + 3)
                            dve.sem_inc(x_written, 1)

        for b in range(NB):
            kv_pass(b)
            block_pass(b)


def experts(nc, io, x, ones):
    with ExitStack() as ctx:
        def sem(name):
            return phase_semaphore(nc, ctx, name)

        def sb(name, shape):
            return ctx.enter_context(nc.sbuf_tensor(name, shape, F32))

        SH = NE
        KE = FE // P
        wg, wu = sb("expert_gate", [P, NE + 1, KD, FE]), sb("expert_up", [P, NE + 1, KD, FE])
        wd = sb("expert_down", [P, NE + 1, KE, D])
        router, ident = sb("router", [P, KD, NE]), sb("ident", [P, P])
        rank = sb("rank", [P, 4, NE])
        pick = sb("pick", [NE, NE, P])
        logit_rows = sb("logit_rows", [NE, BLK])
        top, first = sb("top", [P, 4]), sb("first", [P, 4])
        hit, share = sb("hit", [P, 4, NE]), sb("share", [P, 4, NE])
        share_rows = sb("share_rows", [NE, BLK])
        xe = sb("xe", [P, 2, KD, BLK])
        silu, act_in = sb("silu", [P, 2, BLK]), sb("expert_hidden", [P, KE, BLK])
        z = sb("moe_z", [P, KD, BLK])
        norm = Norm(nc, ctx, "moe_norm", ones)
        bank = [ctx.enter_context(nc.psum_tensor(f"moe_bank{j}", [P, BLK], F32)) for j in range(8)]
        gate_ps, up_ps, acc, spread_ps, small_ps = bank[0:2], bank[2:4], bank[4:6], bank[6], bank[7]

        weights_in, eps_ready = sem("moe_weights_in"), sem("moe_eps_ready")
        logits_ready, rows_ready, turned, top_ready = sem("logits_ready"), sem("rows_ready"), sem("turned"), sem("top_ready")
        route_step, score_ready, share_ready = sem("route_step"), sem("score_ready"), sem("share_ready")
        share_turned, share_rows_ready = sem("share_turned"), sem("share_rows_ready")
        spread_ready, xe_ready = sem("spread_ready"), sem("xe_ready")
        gate_ready, up_ready, silu_ready, hidden_ready = sem("gate_ready"), sem("up_ready"), sem("silu_ready"), sem("expert_hidden_ready")
        down_done, acc_ready, z_ready, x_written = sem("down_done"), sem("expert_acc_ready"), sem("moe_z_ready"), sem("moe_x_written")
        score = sb("score", [P, 4])
        ORDER = [SH] + list(range(NE))
        NX = len(ORDER)

        with nc.Block() as block:
            @block.sync
            def _(sp):
                for dst, name in ((router, "router"), (ident, "ident"), (rank, "rank"), (pick, "pick")):
                    sp.dma_start(dst[:], io[name]).then_inc(weights_in, 16)
                for e in ORDER:
                    for dst, name in ((wg, "expert_gate"), (wu, "expert_up"), (wd, "expert_down")):
                        sp.dma_start(dst[:, e], io[name][:, e]).then_inc(weights_in, 16)

            @block.gpsimd
            def _(pool):
                nc.gpsimd.memset(norm.eps[:], 1e-5).then_inc(eps_ready, 1)

            @block.tensor
            def _(pe):
                pe.wait_ge(weights_in, 16 * (4 + 3 * NX))
                with pe.Fori(0, NB) as b, pe.Fori(0, NBLK) as i:
                    n = i + NBLK * b
                    xb = [x[:, k, :, :].rearrange("p b t -> p (b t)")[:, bass.ds(PAD + b * (PAD + T) + i * BLK, BLK)] for k in range(KD)]
                    pe.wait_ge(x_written, n)
                    for k in range(KD):
                        mm = nc.tensor.matmul(small_ps[0:NE, :], router[:, k], xb[k], start=(k == 0), stop=(k == KD - 1))
                    mm.then_inc(logits_ready, 1)
                    for j, e in enumerate(ORDER):
                        if j == 1:
                            pe.wait_ge(rows_ready, n + 1)
                            for s in range(4):
                                mm = nc.tensor.matmul(small_ps[:, NE * s:NE * s + NE], logit_rows[:, P * s:P * s + P], ident[0:NE, 0:NE], start=True, stop=True)
                            mm.then_inc(turned, 1)
                            pe.wait_ge(share_ready, n + 1)
                            for s in range(4):
                                mm = nc.tensor.transpose(small_ps[0:NE, P * s:P * s + P], share[:, s], ident[:])
                            mm.then_inc(share_turned, 1)
                            pe.wait_ge(share_rows_ready, n + 1)
                            nc.tensor.matmul(spread_ps[:], pick[:, e], share_rows[:], start=True, stop=True).then_inc(spread_ready, 1)
                        if j >= 1:
                            pe.wait_ge(xe_ready, NE * n + j)
                            if j < NE:
                                nc.tensor.matmul(spread_ps[:], pick[:, ORDER[j + 1]], share_rows[:], start=True, stop=True).then_inc(spread_ready, 1)
                        src = xb if e == SH else [xe[:, j % 2, k] for k in range(KD)]
                        for m in range(KE):
                            c = (NX * n + j) * KE + m
                            if j or m >= 2:
                                pe.wait_ge(hidden_ready, c - 1)
                            for k in range(KD):
                                mm = nc.tensor.matmul(gate_ps[m % 2][:], wg[:, e, k, P * m:P * m + P], src[k], start=(k == 0), stop=(k == KD - 1))
                            mm.then_inc(gate_ready, 1)
                            for k in range(KD):
                                mm = nc.tensor.matmul(up_ps[m % 2][:], wu[:, e, k, P * m:P * m + P], src[k], start=(k == 0), stop=(k == KD - 1))
                            mm.then_inc(up_ready, 1)
                        for f in range(KE):
                            pe.wait_ge(hidden_ready, (NX * n + j) * KE + (f + 1))
                            for m in range(KD):
                                mm = nc.tensor.matmul(acc[m][:], wd[:, e, f, P * m:P * m + P], act_in[:, f],
                                                      start=(j == 0 and f == 0), stop=(j == NX - 1 and f == KE - 1))
                        mm.then_inc(down_done, 1)
                    norm.tensor(pe, n, z, z_ready, n + 1, small_ps[:], spread_ps[:])

            @block.scalar
            def _(act):
                act.wait_ge(eps_ready, 1)
                with act.Fori(0, NB) as b, act.Fori(0, NBLK) as i:
                    n = i + NBLK * b
                    for j in range(NX):
                        if j == 1:
                            act.wait_ge(top_ready, n + 1)
                            nc.scalar.activation(score[:], top[:], ACT.Sigmoid).then_inc(score_ready, 1)
                        for m in range(KE):
                            c = (NX * n + j) * KE + m
                            act.wait_ge(gate_ready, c + 1)
                            if j or m >= 2:
                                act.wait_ge(hidden_ready, c - 1)
                            nc.scalar.activation(silu[:, m % 2], gate_ps[m % 2][:], ACT.Silu).then_inc(silu_ready, 1)
                    norm.scalar(act, n, spread_ps[:])

            @block.vector
            def _(dve):
                dve.wait_ge(weights_in, 16 * (4 + 3 * NX))
                with dve.Fori(0, NB) as b, dve.Fori(0, NBLK) as i:
                    n = i + NBLK * b
                    x_block = x[:].rearrange("p k b t -> p k (b t)")[:, :, bass.ds(PAD + b * (PAD + T) + i * BLK, BLK)]
                    dve.wait_ge(logits_ready, n + 1)
                    nc.vector.tensor_copy(logit_rows[:], small_ps[0:NE, :]).then_inc(rows_ready, 1)
                    for j in range(NX):
                        if j == 1:
                            logits = small_ps[:, 0:4 * NE].rearrange("p (s e) -> p s e", e=NE)
                            dve.wait_ge(turned, n + 1)
                            nc.vector.tensor_reduce(top[:], logits, AX_X, ALU.max).then_inc(top_ready, 1)
                            dve.wait_ge(top_ready, n + 1)
                            nc.vector.tensor_tensor(hit[:], logits, top[:].unsqueeze(2).broadcast_to([P, 4, NE]), ALU.is_equal).then_inc(route_step, 1)
                            dve.wait_ge(route_step, 4 * n + 1)
                            nc.vector.tensor_tensor(hit[:], hit[:], rank[:], ALU.mult).then_inc(route_step, 1)
                            dve.wait_ge(route_step, 4 * n + 2)
                            nc.vector.tensor_reduce(first[:], hit[:], AX_X, ALU.max).then_inc(route_step, 1)
                            dve.wait_ge(route_step, 4 * n + 3)
                            nc.vector.tensor_tensor(hit[:], hit[:], first[:].unsqueeze(2).broadcast_to([P, 4, NE]), ALU.is_equal).then_inc(route_step, 1)
                            dve.wait_ge(route_step, 4 * n + 4)
                            dve.wait_ge(score_ready, n + 1)
                            nc.vector.tensor_tensor(share[:], hit[:], score[:].unsqueeze(2).broadcast_to([P, 4, NE]), ALU.mult).then_inc(share_ready, 1)
                            dve.wait_ge(share_turned, n + 1)
                            nc.vector.tensor_copy(share_rows[:], small_ps[0:NE, :]).then_inc(share_rows_ready, 1)

                        def input_of(j):
                            dve.wait_ge(spread_ready, NE * n + j)
                            if j >= 3:
                                dve.wait_ge(down_done, NX * n + (j - 1))
                            nc.vector.tensor_tensor(xe[:, j % 2], x_block, spread_ps[:].unsqueeze(1).broadcast_to([P, KD, BLK]),
                                                    ALU.mult).then_inc(xe_ready, 1)

                        if j == 1:
                            input_of(1)
                        for m in range(KE):
                            c = (NX * n + j) * KE + m
                            if m == 2 and 1 <= j < NE:
                                input_of(j + 1)
                            dve.wait_ge(silu_ready, c + 1)
                            dve.wait_ge(up_ready, c + 1)
                            if m == 0 and j:
                                dve.wait_ge(down_done, NX * n + j)
                            nc.vector.tensor_tensor(act_in[:, m], up_ps[m % 2][:], silu[:, m % 2], ALU.mult).then_inc(hidden_ready, 1)
                    dve.wait_ge(down_done, NX * n + NX)
                    for m in range(KD):
                        last = nc.vector.tensor_tensor(z[:, m], acc[m][:], x_block[:, m], ALU.add)
                    last.then_inc(z_ready, 1)
                    norm.vector(dve, n, z, x_block, small_ps[:])
                    dve.wait_ge(norm.done, n + 1)
                    dve.sem_inc(x_written, 1)


def delta_rule(nc, io, x, ones):
    CB = 2
    TB = CB * CH
    NT = T // TB
    G4 = HP // 2
    LEVELS = (32, 16, 8)
    LIMIT = float(np.exp(12.0))

    with ExitStack() as ctx:
        def sem(name):
            return phase_semaphore(nc, ctx, "d_" + name)

        def sb(name, shape):
            return ctx.enter_context(nc.sbuf_tensor("d_" + name, shape, F32))

        wq, wk, wv, wa = (sb(w, [P, KD, FF]) for w in ("wq", "wk", "wv", "wa"))
        wb, u1, u2 = sb("wb", [P, KD, H]), sb("u1", [P, KD, DH]), sb("u2", [DH, D])
        wo, head_norm = sb("wo", [P, HP, D]), sb("head_norm", [P, HP])
        cols = sb("cols", [P, 2 + 8 + 2 + 8 + 2 + 1 + 1])
        norm_w, conv_w, conv_b, a_b = cols[:, 0:2], cols[:, 2:10], cols[:, 10:12], cols[:, 12:20]
        u2_b, u1_b, b_b = cols[:, 20:22], cols[0:DH, 22:23], cols[0:H, 23:24]
        pick = sb("pick", [H, HP, P])
        pair_mask, ident = sb("pair_mask", [P, P]), sb("ident", [P, P])
        masks = sb("masks", [P, 6, 2, CH])
        q_masks = sb("q_masks", [P, 3, CH])
        carry_on = sb("carry_on", [P, CB * HP * CH])
        eps = sb("eps", [P, 2])

        square, std, rstd = sb("square", [P, KD, TB]), sb("std", [P, TB]), sb("rstd", [P, TB])
        hn, conv, h = sb("hn", [P, KD, 3 + TB]), sb("conv", [P, KD, TB]), sb("h", [P, KD, TB])
        q, k, kb, n_ = (sb(w, [P, CB, HP, CH]) for w in ("q", "k", "kb", "n"))
        v = sb("v", [P, CB, HP, CH])
        b_rows = sb("b_rows", [H, TB])
        yT = sb("yT", [P, HP // 2, 2, TB])
        ex = sb("ex", [P, 7, G4, CH])
        lhs = sb("lhs", [P, 2, 4, G4, P])
        rhs = sb("rhs", [P, 2, 4, G4, 2, CH])
        kG, qG, kH = sb("kG", [P, 2, G4, P]), sb("qG", [P, 2, G4, P]), sb("kH", [P, 2, G4, P])
        g_last = sb("g_last", [P, 2, G4])
        U = sb("U", [P, 2, 6, G4, P])
        qk_sq = U[:, 0, 0:4].rearrange("p (a m) h t -> p a (m h t)", a=2)
        Tm, V, Y = lhs[:, :, 3], lhs[:, :, 1], lhs[:, :, 2]
        QK = U[:, :, 0]
        qk_part = sb("qk_part", [P, 3, G4, CH])
        B, W, S, yn = (sb(w, [P, 2, G4, CH]) for w in ("B", "W", "S", "yn"))
        ss = sb("ss", [P, 2, G4])
        u_hid, gate, mid = sb("u_hid", [DH, TB]), sb("gate", [P, KD, TB]), sb("mid", [P, 2, KD, TB])
        bank = [[ctx.enter_context(nc.psum_tensor(f"d_bank{g}{j}", [P, BLK], F32)) for j in range(4)] for g in range(2)]

        once = """weights_in cleared wo_scaled square var std rstd hn conv_a h k_ps q_ps a_ps b_ps v_ps z_sum a_exp a_min a_log n
            raw sq sum_ps qk_std qk_inv q_ready kb_ready b_rows b_ps2 v_ready
            out_ps u1_ps u_hid u2_ps gate_ready gated stored0 stored1 carry""".split()
        of_groups = """pool_d ex_neg exps lvl_in state_in prod u_ready qk_part y_ps y_sb dt_ps dv_ps t_sb v2 v_sb kt_ps kt_sb r_ps b_sb
            w_ps w_sb o_ps s_ps s_mul s_sb ysq ss y_std ss_inv yn yt_ps yt_sb""".split()
        s = {name: sem(name) for name in once}
        s |= {name: (sem(name + "0"), sem(name + "1")) for name in of_groups}

        def fori2(eng):
            return eng.Fori(0, NB), eng.Fori(0, NT)

        def pairs(t):
            return t[:].rearrange("p (h c) -> p h c", h=G4)

        def by_chunk(t, half):
            return t[:, :, G4 * half:G4 * half + G4].rearrange("p c h t -> p h c t")

        with nc.Block() as block:
            @block.sync
            def _(sp):
                for dst, name in ((cols, "d_cols"), (wa, "d_wa"), (wk, "d_wk"), (wq, "d_wq"), (wv, "d_wv"), (wb, "d_wb"), (pick, "d_pick"),
                                  (pair_mask, "pair_mask"), (ident, "ident"), (masks, "d_masks"), (q_masks, "d_q_masks"), (wo, "d_wo"),
                                  (head_norm, "d_head_norm"), (u1, "d_u1"), (u2, "d_u2"), (carry_on, "d_carry_on")):
                    sp.dma_start(dst[:], io[name]).then_inc(s["weights_in"], 16)
                with sp.Fori(0, NB) as b, sp.Fori(0, NT // 2) as i:
                    for half in range(2):
                        turn = i + (NT // 2) * b
                        sp.wait_ge(s["gated"], 4 * turn + (2 * half + 2))
                        sp.dma_start(io["mid"][:, :, b, bass.ds((2 * i + half) * TB, TB)], mid[:, half]).then_inc(s[f"stored{half}"], 16)
                for half in range(2):
                    sp.wait_ge(s[f"stored{half}"], 16 * NB * NT // 2)

            @block.gpsimd
            def _(pool):
                nc.gpsimd.memset(lhs[:], 0.0).then_inc(s["cleared"], 1)
                nc.gpsimd.memset(rhs[:], 0.0).then_inc(s["cleared"], 1)
                for t in (kG, qG, kH):
                    nc.gpsimd.memset(t[:], 0.0).then_inc(s["cleared"], 1)
                nc.gpsimd.memset(eps[:, 0:1], 1e-6).then_inc(s["cleared"], 1)
                nc.gpsimd.memset(eps[:, 1:2], 0.0).then_inc(s["cleared"], 1)
                pool.wait_ge(s["cleared"], 7)
                pool.wait_ge(s["weights_in"], 16 * 16)
                with pool.Fori(0, NB) as b:
                    with pool.Fori(0, NT) as i:
                        n = i + NT * b
                        pool.wait_ge(s["raw"], 4 * n + 4)
                        nc.gpsimd.tensor_tensor(qk_sq[:, 0], k[:].rearrange("p c h t -> p (c h t)"), k[:].rearrange("p c h t -> p (c h t)"), ALU.mult).then_inc(s["sq"], 1)
                        nc.gpsimd.tensor_tensor(qk_sq[:, 1], q[:].rearrange("p c h t -> p (c h t)"), q[:].rearrange("p c h t -> p (c h t)"), ALU.mult).then_inc(s["sq"], 1)
                        for c in range(CB):
                            for g in range(2):
                                u = n * CB + c
                                hs = slice(G4 * g, G4 * g + G4)
                                if c == 0 and g == 0:
                                    pool.wait_ge(s["n"], n + 1)
                                pool.wait_ge(s["lvl_in"][1 - g], u + g)
                                nn = n_[:, c, hs].rearrange("p h t -> p (h t)")
                                for l, half in enumerate(LEVELS):
                                    nv = nn.rearrange("p (m u t) -> p m u t", u=2, t=half)
                                    ev = ex[:, l].rearrange("p h t -> p (h t)").rearrange("p (m u t) -> p m u t", u=2, t=half)
                                    mid_n = nv[:, :, 0, half - 1:half].broadcast_to([P, G4 * CH // (2 * half), half])
                                    nc.gpsimd.tensor_tensor(ev[:, :, 0], nv[:, :, 0], mid_n, ALU.subtract)
                                    nc.gpsimd.tensor_tensor(ev[:, :, 1], mid_n, nv[:, :, 1], ALU.subtract)
                                nv = nn.rearrange("p (m t) -> p m t", t=CH)
                                nc.gpsimd.tensor_tensor(ex[:, 3], nv, nv[:, :, CH - 1:CH].broadcast_to([P, G4, CH]), ALU.subtract)
                                nv = nn.rearrange("p (m t) -> p m t", t=8)
                                nc.gpsimd.tensor_tensor(ex[:, 4].rearrange("p h t -> p (h t)").rearrange("p (m t) -> p m t", t=8),
                                                        nv[:, :, 3:4].broadcast_to([P, G4 * 8, 8]), nv, ALU.subtract).then_inc(s["pool_d"][g], 1)
                                if c == 0 and g == 0:
                                    pool.wait_ge(s["kb_ready"], 2 * n + 2)
                                pool.wait_ge(s["exps"][g], u + 1)
                                pool.wait_ge(s["s_ps"][g], u)
                                parts = [(dst, src, l, head) for head in range(2) for dst, src, l in ((kG, k, 6), (qG, q, 6), (kH, kb, 3))]
                                for j, (dst, src, l, head) in enumerate(parts):
                                    r = slice(DH * head, DH * head + DH)
                                    nc.gpsimd.tensor_tensor(dst[r, g, :, r], src[r, c, hs], ex[r, l], ALU.mult).then_inc(s["state_in"][g], 1)
                                    pool.wait_ge(s["state_in"][g], 6 * u + (j + 1))
                            for g in range(2):
                                u = n * CB + c
                                pool.wait_ge(s["u_ready"][g], 6 * u + 5)
                                nc.gpsimd.tensor_tensor(V[:, g], ident[:].unsqueeze(1).broadcast_to([P, G4, P]), U[:, g, 0], ALU.subtract).then_inc(s["v2"][g], 1)

            @block.scalar
            def _(act):
                act.wait_ge(s["cleared"], 7)
                act.wait_ge(s["weights_in"], 16 * 16)
                with act.Fori(0, NB) as b, act.Fori(0, NT) as i:
                    n = i + NT * b
                    x_block = x[:].rearrange("p k b t -> p k (b t)")[:, :, bass.ds(PAD + b * (PAD + T) + i * TB, TB)]
                    nc.scalar.activation(square[:], x_block, ACT.Square).then_inc(s["square"], 1)
                    act.wait_ge(s["var"], n + 1)
                    nc.scalar.activation(std[:], bank[0][0][:, 0:TB], ACT.Sqrt, bias=eps[:, 0:1]).then_inc(s["std"], 1)
                    act.wait_ge(s["conv_a"], n + 1)
                    for kk in range(KD):
                        last = nc.scalar.activation(h[:, kk], conv[:, kk], ACT.Silu, bias=conv_b[:, kk:kk + 1])
                    last.then_inc(s["h"], 1)
                    act.wait_ge(s["z_sum"], 2 * n + 2)
                    nc.scalar.activation(n_[:], n_[:], ACT.Exp, scale=-1.0).then_inc(s["a_exp"], 1)
                    for half in range(2):
                        act.wait_ge(s["k_ps"], 2 * n + (half + 1))
                        nc.scalar.copy(by_chunk(k, half), [bank[0][3], bank[1][0]][half][:].rearrange("p (h c t) -> p h c t", h=G4, c=CB)).then_inc(s["raw"], 1)
                    for half in range(2):
                        act.wait_ge(s["q_ps"], 2 * n + (half + 1))
                        nc.scalar.copy(by_chunk(q, half), [bank[1][1], bank[1][2]][half][:].rearrange("p (h c t) -> p h c t", h=G4, c=CB)).then_inc(s["raw"], 1)
                    act.wait_ge(s["a_min"], n + 1)
                    nc.scalar.activation(n_[:], n_[:], ACT.Ln, bias=1.0).then_inc(s["a_log"], 1)
                    act.wait_ge(s["b_ps"], n + 1)
                    nc.scalar.activation(b_rows[:], bank[0][1][0:H, 0:TB], ACT.Sigmoid, bias=b_b).then_inc(s["b_rows"], 1)
                    for j, half in ((0, 0), (0, 1), (1, 0), (1, 1)):
                        act.wait_ge(s["sum_ps"], 4 * n + (2 * j + half + 1))
                        nc.scalar.activation(qk_sq[:, j, BLK * half:BLK * half + BLK], [bank[1][0], bank[0][3], bank[1][1], bank[1][2]][2 * j + half][:],
                                             ACT.Sqrt, bias=eps[:, 1:2]).then_inc(s["qk_std"], 1)
                    for c in range(CB):
                        for g in range(2):
                            u = n * CB + c
                            hs = slice(G4 * g, G4 * g + G4)
                            act.wait_ge(s["pool_d"][g], u + 1)
                            nc.scalar.activation(ex[:, 5], ex[:, 4], ACT.Exp, scale=-1.0).then_inc(s["ex_neg"][g], 1)
                            nc.scalar.activation(ex[:, 0:4], ex[:, 0:4], ACT.Exp)
                            act.wait_ge(s["ex_neg"][g], u + 1)
                            nc.scalar.activation(ex[:, 4], ex[:, 4], ACT.Exp)
                            nc.scalar.activation(ex[:, 6], n_[:, c, hs], ACT.Exp, scale=-1.0).then_inc(s["exps"][g], 1)
                        for j in range(5):
                            for g in range(2):
                                u = n * CB + c
                                act.wait_ge(s["y_ps"][g], 6 * u + (j + 2))
                                nc.scalar.copy(Y[:, g], pairs(bank[g][3])).then_inc(s["y_sb"][g], 1)
                        for g in range(2):
                            u = n * CB + c
                            act.wait_ge(s["kt_ps"][g], u + 1)
                            nc.scalar.copy(kH[:, g], pairs(bank[g][0])).then_inc(s["kt_sb"][g], 1)
                        for g in range(2):
                            u = n * CB + c
                            act.wait_ge(s["w_ps"][g], u + 1)
                            nc.scalar.copy(W[:, g], bank[g][2][:, 0:G4 * CH].rearrange("p (h t) -> p h t", h=G4)).then_inc(s["w_sb"][g], 1)
                        for g in range(2):
                            u = n * CB + c
                            act.wait_ge(s["o_ps"][g], u + 1)
                            nc.scalar.activation(yn[:, g], bank[g][1][:, 0:G4 * CH].rearrange("p (h t) -> p h t", h=G4), ACT.Square).then_inc(s["ysq"][g], 1)
                        for g in range(2):
                            u = n * CB + c
                            act.wait_ge(s["ss"][g], u + 1)
                            nc.scalar.activation(ss[:, g], ss[:, g], ACT.Sqrt, scale=1.0 / DH, bias=eps[:, 0:1]).then_inc(s["y_std"][g], 1)
                    act.wait_ge(s["u1_ps"], n + 1)
                    nc.scalar.activation(u_hid[:], bank[0][1][0:DH, 0:TB], ACT.Silu, bias=u1_b).then_inc(s["u_hid"], 1)
                    act.wait_ge(s["u2_ps"], n + 1)
                    for m in range(KD):
                        last = nc.scalar.activation(gate[:, m], bank[0][2][:, TB * m:TB * m + TB], ACT.Sigmoid, bias=u2_b[:, m:m + 1])
                    last.then_inc(s["gate_ready"], 1)

            @block.vector
            def _(dve):
                dve.wait_ge(s["cleared"], 7)
                dve.wait_ge(s["weights_in"], 16 * 16)
                nc.vector.tensor_tensor(wo[:], wo[:], head_norm[:].unsqueeze(2).broadcast_to([P, HP, D]), ALU.mult).then_inc(s["wo_scaled"], 1)
                with dve.Fori(0, NB) as b:
                  nc.vector.memset(S[:], 0.0).then_inc(s["carry"], 1)
                  nc.vector.memset(hn[:, :, 0:3], 0.0).then_inc(s["carry"], 1)
                  with dve.Fori(0, NT // 2) as i2:
                   for blk in range(2):
                    i = 2 * i2 + blk
                    n = i + NT * b
                    x_block = x[:].rearrange("p k b t -> p k (b t)")[:, :, bass.ds(PAD + b * (PAD + T) + i * TB, TB)]
                    if blk == 0:
                        dve.wait_ge(s["carry"], 2 * b + 2)
                    dve.wait_ge(s["std"], n + 1)
                    nc.vector.reciprocal(rstd[:], std[:]).then_inc(s["rstd"], 1)
                    dve.wait_ge(s["rstd"], n + 1)
                    for kk in range(KD):
                        last = nc.vector.scalar_tensor_tensor(hn[:, kk, 3:], x_block[:, kk], norm_w[:, kk:kk + 1], rstd[:], ALU.mult, ALU.mult)
                    last.then_inc(s["hn"], 1)
                    dve.wait_ge(s["hn"], 5 * n + 1)
                    for tap in range(4):
                        for kk in range(KD):
                            w = conv_w[:, 4 * kk + tap:4 * kk + tap + 1]
                            if tap == 0:
                                last = nc.vector.tensor_scalar(conv[:, kk], hn[:, kk, 0:TB], w, None, ALU.mult)
                            else:
                                last = nc.vector.scalar_tensor_tensor(conv[:, kk], hn[:, kk, tap:tap + TB], w, conv[:, kk], ALU.mult, ALU.add)
                        if tap < 3:
                            last.then_inc(s["hn"], 1)
                            dve.wait_ge(s["hn"], 5 * n + (tap + 2))
                    last.then_inc(s["hn"], 1)
                    dve.wait_ge(s["hn"], 5 * n + 5)
                    nc.vector.tensor_copy(hn[:, :, 0:3], hn[:, :, TB:TB + 3]).then_inc(s["conv_a"], 1)
                    dve.wait_ge(s["conv_a"], n + 1)
                    for half in range(2):
                        dve.wait_ge(s["a_ps"], 2 * n + (half + 1))
                        nc.vector.tensor_tensor(by_chunk(n_, half), bank[0][1 + half][:].rearrange("p (h c t) -> p h c t", h=G4, c=CB),
                                                a_b[:, G4 * half:G4 * half + G4].unsqueeze(2).unsqueeze(3).broadcast_to([P, G4, CB, CH]), ALU.add).then_inc(s["z_sum"], 1)
                    dve.wait_ge(s["a_exp"], n + 1)
                    nc.vector.tensor_scalar(n_[:], n_[:], LIMIT, None, ALU.min).then_inc(s["a_min"], 1)
                    for c in range(CB):
                        dve.wait_ge(s["v_ps"], 2 * n + (c + 1))
                        nc.vector.tensor_copy(v[:, c], [bank[1][3], bank[0][0]][c][:].rearrange("p (h t) -> p h t", h=HP)).then_inc(s["v_ready"], 1)
                    dve.wait_ge(s["a_log"], n + 1)
                    flat = lambda t: t[:].rearrange("p c h t -> p (c h t)")
                    nc.vector.tensor_tensor_scan(flat(n_), carry_on[:], flat(n_), 0.0, ALU.mult, ALU.add).then_inc(s["n"], 1)
                    for j, t in ((0, k), (1, q)):
                        dve.wait_ge(s["qk_std"], 4 * n + (2 * j + 2))
                        nc.vector.tensor_scalar(qk_sq[:, j], qk_sq[:, j], 1e-6, None, ALU.add).then_inc(s["qk_inv"], 1)
                        dve.wait_ge(s["qk_inv"], 4 * n + (2 * j + 1))
                        nc.vector.reciprocal(qk_sq[:, j], qk_sq[:, j]).then_inc(s["qk_inv"], 1)
                        dve.wait_ge(s["qk_inv"], 4 * n + (2 * j + 2))
                        nc.vector.tensor_tensor(flat(t), flat(t), qk_sq[:, j], ALU.mult).then_inc(s["q_ready"], 1)
                    dve.wait_ge(s["q_ready"], 2 * n + 2)
                    for half in range(2):
                        dve.wait_ge(s["b_ps2"], 2 * n + (half + 1))
                        nc.vector.tensor_tensor(by_chunk(kb, half), by_chunk(k, half), [bank[0][2], bank[0][3]][half][:].rearrange("p (h c t) -> p h c t", h=G4, c=CB),
                                                ALU.mult).then_inc(s["kb_ready"], 1)
                    dve.wait_ge(s["kb_ready"], 2 * n + 2)
                    for c in range(CB):
                        for g in range(2):
                            u = n * CB + c
                            hs = slice(G4 * g, G4 * g + G4)
                            dve.wait_ge(s["exps"][g], u + 1)
                            for l, half in enumerate(LEVELS):
                                def lv(t):
                                    return t.rearrange("p h (m u t) -> p h m u t", u=2, t=half)
                                e = lv(ex[:, l])
                                for j, t in ((0, k), (1, q)):
                                    nc.vector.tensor_tensor(lv(rhs[:, g, l, :, j])[:, :, :, 1], lv(t[:, c, hs])[:, :, :, 1], e[:, :, :, 1], ALU.mult)
                                for head in range(2):
                                    r = slice(DH * head, DH * head + DH)
                                    nc.vector.tensor_tensor(lv(lhs[r, g, l, :, r])[:, :, :, 0], lv(kb[r, c, hs])[:, :, :, 0], e[r, :, :, 0], ALU.mult)
                            for j, t in ((0, k), (1, q)):
                                nc.vector.tensor_tensor(rhs[:, g, 3, :, j], t[:, c, hs], ex[:, 4], ALU.mult)
                            for head in range(2):
                                r = slice(DH * head, DH * head + DH)
                                nc.vector.tensor_tensor(lhs[r, g, 3, :, r], kb[r, c, hs], ex[r, 5], ALU.mult)
                            nc.vector.tensor_copy(g_last[:, g], ex[:, 6, :, CH - 1]).then_inc(s["lvl_in"][g], 1)
                        for g in range(2):
                            u = n * CB + c
                            def spread(bk, m):
                                src = bk[:].rearrange("p (h a t) -> p h a t", h=G4, a=2)[:, :, 0].unsqueeze(2).broadcast_to([P, G4, 2, CH])
                                dst = U[:, g, m].rearrange("p h (a t) -> p h a t", a=2)
                                return nc.vector.tensor_tensor(dst, src, masks[:, m].unsqueeze(1).broadcast_to([P, G4, 2, CH]), ALU.mult)
                            def q_side(bk):
                                return bk[:].rearrange("p (h a t) -> p h a t", h=G4, a=2)[:, :, 1]
                            dve.wait_ge(s["prod"][g], 4 * u + 1)
                            for m in range(3):
                                spread(bank[g][3], m).then_inc(s["u_ready"][g], 1)
                            nc.vector.tensor_tensor(qk_part[:, 0], q_side(bank[g][3]), q_masks[:, 0].unsqueeze(1).broadcast_to([P, G4, CH]), ALU.mult).then_inc(s["qk_part"][g], 1)
                            for j in (1, 2):
                                dve.wait_ge(s["prod"][g], 4 * u + (j + 1))
                                spread(bank[g][3 - j], 2 + j).then_inc(s["u_ready"][g], 1)
                                nc.vector.tensor_tensor(qk_part[:, j], q_side(bank[g][3 - j]), q_masks[:, j].unsqueeze(1).broadcast_to([P, G4, CH]), ALU.mult).then_inc(s["qk_part"][g], 1)
                            dve.wait_ge(s["prod"][g], 4 * u + 4)
                            spread(bank[g][0], 5)
                            dve.wait_ge(s["qk_part"][g], 5 * u + 3)
                            nc.vector.tensor_tensor(qk_part[:, 2], q_side(bank[g][0]), qk_part[:, 2], ALU.add).then_inc(s["u_ready"][g], 1)
                            nc.vector.tensor_tensor(qk_part[:, 1], qk_part[:, 1], qk_part[:, 0], ALU.add).then_inc(s["qk_part"][g], 1)
                            dve.wait_ge(s["y_ps"][g], 6 * u + 1)
                            nc.vector.tensor_tensor(Tm[:, g], ident[:].unsqueeze(1).broadcast_to([P, G4, P]), pairs(bank[g][3]), ALU.subtract).then_inc(s["t_sb"][g], 1)
                            dve.wait_ge(s["v2"][g], u + 1)
                            dve.wait_ge(s["qk_part"][g], 5 * u + 4)
                            dve.wait_ge(s["u_ready"][g], 6 * u + 6)
                            for head in range(2):
                                r = slice(DH * head, DH * head + DH)
                                last = nc.vector.tensor_tensor(QK[r, g, :, r], qk_part[r, 1], qk_part[r, 2], ALU.add)
                            last.then_inc(s["qk_part"][g], 1)
                            dve.wait_ge(s["qk_part"][g], 5 * u + 5)
                        for j in range(5):
                            for g in range(2):
                                u = n * CB + c
                                if j < 4:
                                    dve.wait_ge(s["dt_ps"][g], 4 * u + (j + 1))
                                    dve.wait_ge(s["t_sb"][g], 5 * u + (j + 1))
                                    nc.vector.tensor_tensor(Tm[:, g], Tm[:, g], pairs(bank[g][2]), ALU.subtract).then_inc(s["t_sb"][g], 1)
                                dve.wait_ge(s["dv_ps"][g], 5 * u + (j + 1))
                                if j:
                                    dve.wait_ge(s["v_sb"][g], 5 * u + j)
                                nc.vector.tensor_tensor(V[:, g], V[:, g], pairs(bank[g][1]), ALU.subtract).then_inc(s["v_sb"][g], 1)
                        for g in range(2):
                            u = n * CB + c
                            hs = slice(G4 * g, G4 * g + G4)
                            few = lambda bk: bk[:, 0:G4 * CH].rearrange("p (h t) -> p h t", h=G4)
                            dve.wait_ge(s["r_ps"][g], u + 1)
                            nc.vector.tensor_tensor(B[:, g], v[:, c, hs], few(bank[g][3]), ALU.subtract).then_inc(s["b_sb"][g], 1)
                        for g in range(2):
                            u = n * CB + c
                            dve.wait_ge(s["o_ps"][g], u + 1)
                            nc.vector.tensor_tensor(S[:, g], S[:, g], g_last[:, g].unsqueeze(2).broadcast_to([P, G4, CH]), ALU.mult).then_inc(s["s_mul"][g], 1)
                            dve.wait_ge(s["s_mul"][g], u + 1)
                            dve.wait_ge(s["s_ps"][g], u + 1)
                            nc.vector.tensor_tensor(S[:, g], S[:, g], few(bank[g][0]), ALU.add).then_inc(s["s_sb"][g], 1)
                            dve.wait_ge(s["ysq"][g], u + 1)
                            nc.vector.tensor_reduce(ss[:, g], yn[:, g], AX_X, ALU.add).then_inc(s["ss"][g], 1)
                        for g in range(2):
                            u = n * CB + c
                            dve.wait_ge(s["y_std"][g], u + 1)
                            nc.vector.reciprocal(ss[:, g], ss[:, g]).then_inc(s["ss_inv"][g], 1)
                            dve.wait_ge(s["ss_inv"][g], u + 1)
                            nc.vector.tensor_tensor(yn[:, g], few(bank[g][1]), ss[:, g].unsqueeze(2).broadcast_to([P, G4, CH]), ALU.mult).then_inc(s["yn"][g], 1)
                        for g in range(2):
                            u = n * CB + c
                            dve.wait_ge(s["yt_ps"][g], u + 1)
                            nc.vector.tensor_copy(yT[:, 2 * g:2 * g + 2, :, CH * c:CH * c + CH],
                                                  bank[g][3][:, 0:2 * P].rearrange("p (a h t) -> p a h t", a=2, h=2)).then_inc(s["yt_sb"][g], 1)
                    dve.wait_ge(s["out_ps"], n + 1)
                    dve.wait_ge(s["gate_ready"], n + 1)
                    dve.wait_ge(s[f"stored{blk}"], 16 * (i2 + (NT // 2) * b))
                    nc.vector.tensor_tensor(mid[:, blk], bank[0][0][:, 0:KD * TB].rearrange("p (k t) -> p k t", k=KD), gate[:], ALU.mult).then_inc(s["gated"], 1)
                    dve.wait_ge(s["gated"], 2 * n + 1)
                    nc.vector.tensor_tensor(mid[:, blk], mid[:, blk], x_block, ALU.add).then_inc(s["gated"], 1)

            @block.tensor
            def _(pe):
                pe.wait_ge(s["cleared"], 7)
                pe.wait_ge(s["weights_in"], 16 * 16)
                pe.wait_ge(s["wo_scaled"], 1)
                with pe.Fori(0, NB) as b, pe.Fori(0, NT) as i:
                    n = i + NT * b
                    x_flat = x[:].rearrange("p k b t -> p k (b t)")
                    x_block = [x_flat[:, k, bass.ds(PAD + b * (PAD + T) + i * TB, TB)] for k in range(KD)]
                    pe.wait_ge(s["gated"], 2 * n)
                    pe.wait_ge(s["square"], n + 1)
                    for kk in range(KD):
                        mm = nc.tensor.matmul(bank[0][0][:, 0:TB], ones[:], square[:, kk], start=(kk == 0), stop=(kk == KD - 1))
                    mm.then_inc(s["var"], 1)
                    pe.wait_ge(s["h"], n + 1)

                    def project(w, halves, done):
                        for half in range(2):
                            for j in range(G4):
                                hp = G4 * half + j
                                for kk in range(KD):
                                    mm = nc.tensor.matmul(halves[half][:, P * j:P * j + P], w[:, kk, P * hp:P * hp + P], h[:, kk],
                                                          start=(kk == 0), stop=(kk == KD - 1))
                            mm.then_inc(done, 1)
                    project(wa, (bank[0][1], bank[0][2]), s["a_ps"])
                    project(wk, (bank[0][3], bank[1][0]), s["k_ps"])
                    project(wq, (bank[1][1], bank[1][2]), s["q_ps"])
                    for c in range(CB):
                        if c == 1:
                            pe.wait_ge(s["std"], n + 1)
                        for head in range(2):
                            r = slice(DH * head, DH * head + DH)
                            for kk in range(KD):
                                mm = nc.tensor.matmul([bank[1][3], bank[0][0]][c][r, :], h[:, kk, CH * c:CH * c + CH],
                                                      wv[:, kk].rearrange("p (h a t) -> p h a t", a=2, t=DH)[:, :, head],
                                                      start=(kk == 0), stop=(kk == KD - 1))
                        mm.then_inc(s["v_ps"], 1)
                    pe.wait_ge(s["z_sum"], 2 * n + 2)
                    for kk in range(KD):
                        mm = nc.tensor.matmul(bank[0][1][0:H, 0:TB], wb[:, kk], h[:, kk], start=(kk == 0), stop=(kk == KD - 1))
                    mm.then_inc(s["b_ps"], 1)
                    pe.wait_ge(s["raw"], 4 * n + 4)
                    for j, half in ((0, 0), (0, 1), (1, 0), (1, 1)):
                        if half == 0:
                            pe.wait_ge(s["sq"], 2 * n + (j + 1))
                        nc.tensor.matmul([bank[1][0], bank[0][3], bank[1][1], bank[1][2]][2 * j + half][:], pair_mask[:], qk_sq[:, j, BLK * half:BLK * half + BLK],
                                         start=True, stop=True).then_inc(s["sum_ps"], 1)
                    pe.wait_ge(s["b_rows"], n + 1)
                    for half in range(2):
                        if half == 1:
                            pe.wait_ge(s["qk_std"], 4 * n + 2)
                        for j in range(G4):
                            mm = nc.tensor.matmul([bank[0][2], bank[0][3]][half][:, P * j:P * j + P], pick[:, G4 * half + j], b_rows[:], start=True, stop=True)
                        mm.then_inc(s["b_ps2"], 1)
                    for c in range(CB):
                        for g in range(2):
                            u = n * CB + c
                            if c == 0:
                                pe.wait_ge(s["qk_std"], 4 * n + 4)
                                pe.wait_ge(s["v_ready"], 2 * n + 2)
                                pe.wait_ge(s["kb_ready"], 2 * n + 2)
                            else:
                                pe.wait_ge(s["yt_sb"][g], u)
                                pe.wait_ge(s["s_sb"][g], u)
                            pe.wait_ge(s["lvl_in"][g], u + 1)
                            for j in range(4):
                                for hp in range(G4):
                                    mm = nc.tensor.matmul(bank[g][3 - j][:, P * hp:P * hp + P], lhs[:, g, [3, 2, 1, 0][j], hp],
                                                          rhs[:, g, [3, 2, 1, 0][j], hp].rearrange("p a t -> p (a t)"), start=True, stop=True)
                                mm.then_inc(s["prod"][g], 1)
                        for j in range(6):
                            for g in range(2):
                                u = n * CB + c
                                pe.wait_ge(s["u_ready"][g], 6 * u + (j + 1))
                                if j == 0:
                                    pe.wait_ge(s["qk_part"][g], 5 * u + 1)
                                else:
                                    pe.wait_ge(s["t_sb"][g], 5 * u + j)
                                for hp in range(G4):
                                    mm = nc.tensor.matmul(bank[g][3][:, P * hp:P * hp + P], U[:, g, j, hp], ident[:] if j == 0 else Tm[:, g, hp], start=True, stop=True)
                                mm.then_inc(s["y_ps"][g], 1)
                            for g in range(2):
                                u = n * CB + c
                                if j == 0:
                                    continue
                                pe.wait_ge(s["y_sb"][g], 5 * u + j)
                                if j == 1:
                                    pe.wait_ge(s["v2"][g], u + 1)
                                    pe.wait_ge(s["qk_part"][g], 5 * u + 3)
                                    pe.wait_ge(s["u_ready"][g], 6 * u + 5)
                                else:
                                    pe.wait_ge(s["v_sb"][g], 5 * u + (j - 1))
                                if j < 5:
                                    for hp in range(G4):
                                        mm = nc.tensor.matmul(bank[g][2][:, P * hp:P * hp + P], V[:, g, hp], Y[:, g, hp], start=True, stop=True)
                                    mm.then_inc(s["dt_ps"][g], 1)
                                for hp in range(G4):
                                    mm = nc.tensor.matmul(bank[g][1][:, P * hp:P * hp + P], Y[:, g, hp], V[:, g, hp], start=True, stop=True)
                                mm.then_inc(s["dv_ps"][g], 1)
                        for g in range(2):
                            u = n * CB + c
                            pe.wait_ge(s["state_in"][g], 6 * u + 6)
                            for hp in range(G4):
                                mm = nc.tensor.transpose(bank[g][0][:, P * hp:P * hp + P], kH[:, g, hp], ident[:])
                            mm.then_inc(s["kt_ps"][g], 1)
                        for g in range(2):
                            u = n * CB + c
                            pe.wait_ge(s["carry"], 2 * b + 2)
                            pe.wait_ge(s["s_sb"][g], u)
                            for hp in range(G4):
                                mm = nc.tensor.matmul(bank[g][3][:, CH * hp:CH * hp + CH], kG[:, g, hp], S[:, g, hp], start=True, stop=True)
                            mm.then_inc(s["r_ps"][g], 1)
                        for g in range(2):
                            u = n * CB + c
                            pe.wait_ge(s["b_sb"][g], u + 1)
                            pe.wait_ge(s["v_sb"][g], 5 * u + 5)
                            for hp in range(G4):
                                mm = nc.tensor.matmul(bank[g][2][:, CH * hp:CH * hp + CH], V[:, g, hp], B[:, g, hp], start=True, stop=True)
                            mm.then_inc(s["w_ps"][g], 1)
                        for g in range(2):
                            u = n * CB + c
                            pe.wait_ge(s["w_sb"][g], u + 1)
                            for hp in range(G4):
                                nc.tensor.matmul(bank[g][1][:, CH * hp:CH * hp + CH], qG[:, g, hp], S[:, g, hp], start=True, stop=False)
                                mm = nc.tensor.matmul(bank[g][1][:, CH * hp:CH * hp + CH], QK[:, g, hp], W[:, g, hp], start=False, stop=True)
                            mm.then_inc(s["o_ps"][g], 1)
                            pe.wait_ge(s["kt_sb"][g], u + 1)
                            for hp in range(G4):
                                mm = nc.tensor.matmul(bank[g][0][:, CH * hp:CH * hp + CH], kH[:, g, hp], W[:, g, hp], start=True, stop=True)
                            mm.then_inc(s["s_ps"][g], 1)
                        for g in range(2):
                            u = n * CB + c
                            pe.wait_ge(s["yn"][g], u + 1)
                            for a in range(2):
                                mm = nc.tensor.transpose(bank[g][3][:, P * a:P * a + P], yn[:, g, 2 * a:2 * a + 2].rearrange("p h t -> p (h t)"), ident[:])
                            mm.then_inc(s["yt_ps"][g], 1)
                    for kk in range(KD):
                        mm = nc.tensor.matmul(bank[0][1][0:DH, 0:TB], u1[:, kk], x_block[kk], start=(kk == 0), stop=(kk == KD - 1))
                    mm.then_inc(s["u1_ps"], 1)
                    pe.wait_ge(s["u_hid"], n + 1)
                    for m in range(KD):
                        mm = nc.tensor.matmul(bank[0][2][:, TB * m:TB * m + TB], u2[:, P * m:P * m + P], u_hid[:], start=True, stop=True)
                    mm.then_inc(s["u2_ps"], 1)
                    for g in range(2):
                        pe.wait_ge(s["yt_sb"][g], CB * n + CB)
                    for m in range(KD):
                        for a in range(HP // 2):
                            for head in range(2):
                                mm = nc.tensor.matmul(bank[0][0][:, TB * m:TB * m + TB], wo[:, 2 * a + head, P * m:P * m + P], yT[:, a, head],
                                                      start=(a == 0 and head == 0), stop=(a == HP // 2 - 1 and head == 1))
                    mm.then_inc(s["out_ps"], 1)


def delta_feed_forward(nc, io, x, ones):
    with ExitStack() as ctx:
        def sem(name):
            return phase_semaphore(nc, ctx, "f_" + name)

        def sb(name, shape):
            return ctx.enter_context(nc.sbuf_tensor("f_" + name, shape, F32))

        w1, w3, w2 = sb("w1", [P, KD, FF]), sb("w3", [P, KD, FF]), sb("w2", [P, KF, D])
        norm_w = sb("norm_w", [P, KD])
        mid, y2, z = sb("mid", [P, 2, KD, BLK]), sb("y2", [P, KD, BLK]), sb("z", [P, KD, BLK])
        silu, hidden = sb("silu", [P, 2, BLK]), sb("hidden", [P, KF, BLK])
        rms = Norm(nc, ctx, "f_rms", ones, centred=False)
        norm = Norm(nc, ctx, "f_norm", ones)
        bank = [ctx.enter_context(nc.psum_tensor(f"f_bank{j}", [P, BLK], F32)) for j in range(8)]
        gate_ps, up_ps, acc, mean_ps, var_ps = bank[0:2], bank[2:4], bank[4:6], bank[6], bank[7]
        weights_in, eps_ready, mid_in = sem("weights_in"), sem("eps_ready"), [sem("mid_in0"), sem("mid_in1")]
        y2_ready, gate_done, up_done, silu_ready, hidden_ready = sem("y2_ready"), sem("gate_done"), sem("up_done"), sem("silu_ready"), sem("hidden_ready")
        down_done, z_ready = sem("down_done"), sem("z_ready")
        sum_ready = [sem("sum_ready0"), sem("sum_ready1")]
        HB = NBLK // 2

        with nc.Block() as block:
            @block.sync
            def _(sp):
                for dst, name in ((w1, "f_w1"), (w3, "f_w3"), (w2, "f_w2"), (norm_w, "f_norm_w")):
                    sp.dma_start(dst[:], io[name]).then_inc(weights_in, 16)
                with sp.Fori(0, NB) as b, sp.Fori(0, HB) as i:
                    for half in range(2):
                        sp.wait_ge(sum_ready[half], i + HB * b)
                        sp.dma_start(mid[:, half], io["mid"][:, :, b, bass.ds((2 * i + half) * BLK, BLK)]).then_inc(mid_in[half], 16)

            @block.gpsimd
            def _(pool):
                nc.gpsimd.memset(norm.eps[:], 1e-5).then_inc(eps_ready, 1)
                nc.gpsimd.memset(rms.eps[:], 1e-6).then_inc(eps_ready, 1)

            @block.tensor
            def _(pe):
                pe.wait_ge(weights_in, 16 * 4)
                with pe.Fori(0, NB) as b, pe.Fori(0, HB) as i:
                    for half in range(2):
                        n = 2 * i + half + NBLK * b
                        rms.tensor(pe, n, None, None, None, mean_ps[:], var_ps[:])
                        pe.wait_ge(y2_ready, KD * n + KD)
                        for m in range(KF):
                            c = KF * n + m
                            if m >= 2:
                                pe.wait_ge(hidden_ready, c - 1)
                            for w, dst, done in ((w1, gate_ps, gate_done), (w3, up_ps, up_done)):
                                for k in range(KD):
                                    mm = nc.tensor.matmul(dst[m % 2][:], w[:, k, P * m:P * m + P], y2[:, k], start=(k == 0), stop=(k == KD - 1))
                                mm.then_inc(done, 1)
                        for f in range(KF):
                            pe.wait_ge(hidden_ready, KF * n + (f + 1))
                            for m in range(KD):
                                mm = nc.tensor.matmul(acc[m][:], w2[:, f, P * m:P * m + P], hidden[:, f], start=(f == 0), stop=(f == KF - 1))
                        mm.then_inc(down_done, 1)
                        norm.tensor(pe, n, z, z_ready, n + 1, mean_ps[:], var_ps[:])

            @block.scalar
            def _(act):
                act.wait_ge(eps_ready, 2)
                with act.Fori(0, NB) as b, act.Fori(0, HB) as i:
                    for half in range(2):
                        n = 2 * i + half + NBLK * b
                        rms.scalar(act, n, var_ps[:], mid[:, half], mid_in[half], 16 * (i + HB * b + 1))
                        for m in range(KF):
                            c = KF * n + m
                            act.wait_ge(gate_done, c + 1)
                            if m >= 2:
                                act.wait_ge(hidden_ready, c - 1)
                            nc.scalar.activation(silu[:, m % 2], gate_ps[m % 2][:], ACT.Silu).then_inc(silu_ready, 1)
                        norm.scalar(act, n, var_ps[:])

            @block.vector
            def _(dve):
                dve.wait_ge(weights_in, 16 * 4)
                with dve.Fori(0, NB) as b, dve.Fori(0, HB) as i:
                    for half in range(2):
                        n = 2 * i + half + NBLK * b
                        start = b * (PAD + T) + PAD + (2 * i + half) * BLK
                        x_block = x[:].rearrange("p k b t -> p k (b t)")[:, :, bass.ds(start, BLK)]
                        dve.wait_ge(mid_in[half], 16 * (i + HB * b + 1))
                        rms.vector(dve, n, mid[:, half], y2[:], mean_ps[:])
                        dve.wait_ge(rms.done, n + 1)
                        for k in range(KD):
                            nc.vector.tensor_scalar(y2[:, k], y2[:, k], norm_w[:, k:k + 1], None, ALU.mult).then_inc(y2_ready, 1)
                        for m in range(KF):
                            c = KF * n + m
                            dve.wait_ge(silu_ready, c + 1)
                            dve.wait_ge(up_done, c + 1)
                            nc.vector.tensor_tensor(hidden[:, m], up_ps[m % 2][:], silu[:, m % 2], ALU.mult).then_inc(hidden_ready, 1)
                        nc.vector.tensor_tensor(z[:], x_block, mid[:, half], ALU.add).then_inc(sum_ready[half], 1)
                        dve.wait_ge(down_done, n + 1)
                        dve.wait_ge(sum_ready[half], i + HB * b + 1)
                        for m in range(KD):
                            last = nc.vector.tensor_tensor(z[:, m], acc[m][:], z[:, m], ALU.add)
                        last.then_inc(z_ready, 1)
                        dve.wait_ge(z_ready, n + 1)
                        norm.vector(dve, n, z, x_block, mean_ps[:])
                        dve.wait_ge(norm.done, n + 1)


def channel_mix(nc, io, x, ones):
    with ExitStack() as ctx:
        def sem(name):
            return phase_semaphore(nc, ctx, name)

        def sb(name, shape):
            return ctx.enter_context(nc.sbuf_tensor(name, shape, F32))

        wr, wk, wv = sb("mix_wr", [P, KD, D]), sb("mix_wk", [P, KD, D]), sb("mix_wv", [P, KD, D])
        mu = sb("mu", [P, 2 * KD])
        step, xr, xk = sb("mix_step", [P, KD, BLK]), sb("xr", [P, KD, BLK]), sb("xk", [P, KD, BLK])
        r, k_relu, k_act = sb("mix_r", [P, KD, BLK]), sb("k_relu", [P, KD, BLK]), sb("k_act", [P, KD, BLK])
        z, y = sb("mix_z", [P, KD, BLK]), sb("mix_y", [P, 2, KD, BLK])
        norm = Norm(nc, ctx, "mix_norm", ones)
        bank = [ctx.enter_context(nc.psum_tensor(f"mix_bank{j}", [P, BLK], F32)) for j in range(8)]
        r_ps, k_ps, v_ps, mean_ps, var_ps = bank[0:2], bank[2:4], bank[4:6], bank[6], bank[7]

        weights_in, eps_ready = sem("mix_weights_in"), sem("mix_eps_ready")
        step_ready, xk_ready, xr_ready = sem("mix_step_ready"), sem("xk_ready"), sem("xr_ready")
        k_done, r_done, v_done = sem("mix_k_done"), sem("mix_r_done"), sem("mix_v_done")
        relu_ready, r_ready, k_act_ready, gated, z_ready = sem("relu_ready"), sem("mix_r_ready"), sem("k_act_ready"), sem("gated"), sem("mix_z_ready")
        stored, written = [sem("out_stored0"), sem("out_stored1")], sem("out_written")
        HB = NBLK // 2

        with nc.Block() as block:
            @block.sync
            def _(sp):
                for dst, name in ((wr, "mix_wr"), (wk, "mix_wk"), (wv, "mix_wv"), (mu, "mu")):
                    sp.dma_start(dst[:], io[name]).then_inc(weights_in, 16)
                with sp.Fori(0, NB) as b, sp.Fori(0, HB) as i:
                    for half in range(2):
                        n = 2 * i + half + NBLK * b
                        sp.wait_ge(written, n + 1)
                        sp.dma_start(io["out"][:, :, b, bass.ds((2 * i + half) * BLK, BLK)], y[:, half]).then_inc(stored[half], 16)
                for half in range(2):
                    sp.wait_ge(stored[half], 16 * NB * HB)

            @block.gpsimd
            def _(pool):
                nc.gpsimd.memset(norm.eps[:], 1e-5).then_inc(eps_ready, 1)
                with pool.Fori(0, NB) as b, pool.Fori(0, HB) as i:
                    for half in range(2):
                        n = 2 * i + half + NBLK * b
                        pool.wait_ge(relu_ready, n + 1)
                        nc.gpsimd.tensor_tensor(k_act[:], k_relu[:], k_relu[:], ALU.mult).then_inc(k_act_ready, 1)

            @block.tensor
            def _(pe):
                pe.wait_ge(weights_in, 16 * 4)
                with pe.Fori(0, NB) as b, pe.Fori(0, HB) as i:
                    for half in range(2):
                        n = 2 * i + half + NBLK * b
                        for dst, w, src, ready, done in ((k_ps, wk, xk, xk_ready, k_done), (r_ps, wr, xr, xr_ready, r_done)):
                            pe.wait_ge(ready, KD * (n + 1))
                            pe.wait_ge(gated, n)
                            for m in range(KD):
                                for k in range(KD):
                                    mm = nc.tensor.matmul(dst[m][:], w[:, k, P * m:P * m + P], src[:, k], start=(k == 0), stop=(k == KD - 1))
                            mm.then_inc(done, 1)
                        pe.wait_ge(k_act_ready, n + 1)
                        for m in range(KD):
                            for k in range(KD):
                                mm = nc.tensor.matmul(v_ps[m][:], wv[:, k, P * m:P * m + P], k_act[:, k], start=(k == 0), stop=(k == KD - 1))
                        mm.then_inc(v_done, 1)
                        norm.tensor(pe, n, z, z_ready, n + 1, mean_ps[:], var_ps[:])

            @block.scalar
            def _(act):
                act.wait_ge(eps_ready, 1)
                with act.Fori(0, NB) as b, act.Fori(0, HB) as i:
                    for half in range(2):
                        n = 2 * i + half + NBLK * b
                        act.wait_ge(k_done, n + 1)
                        act.wait_ge(k_act_ready, n)
                        act.wait_ge(v_done, n)
                        for m in range(KD):
                            last = nc.scalar.activation(k_relu[:, m], k_ps[m][:], ACT.Relu)
                        last.then_inc(relu_ready, 1)
                        act.wait_ge(r_done, n + 1)
                        for m in range(KD):
                            last = nc.scalar.activation(r[:, m], r_ps[m][:], ACT.Sigmoid)
                        last.then_inc(r_ready, 1)
                        norm.scalar(act, n, var_ps[:])

            @block.vector
            def _(dve):
                dve.wait_ge(weights_in, 16 * 4)
                with dve.Fori(0, NB) as b, dve.Fori(0, HB) as i:
                    for half in range(2):
                        n = 2 * i + half + NBLK * b
                        start = b * (PAD + T) + PAD + (2 * i + half) * BLK
                        tokens = x[:].rearrange("p k b t -> p k (b t)")
                        now, before = tokens[:, :, bass.ds(start, BLK)], tokens[:, :, bass.ds(start - 1, BLK)]
                        nc.vector.tensor_tensor(step[:], now, before, ALU.subtract).then_inc(step_ready, 1)
                        dve.wait_ge(step_ready, n + 1)
                        dve.wait_ge(r_done, n)
                        for dst, col, ready in ((xk, KD, xk_ready), (xr, 0, xr_ready)):
                            for k in range(KD):
                                nc.vector.scalar_tensor_tensor(dst[:, k], step[:, k], mu[:, col + k:col + k + 1], before[:, k],
                                                               ALU.mult, ALU.add).then_inc(ready, 1)
                        dve.wait_ge(v_done, n + 1)
                        dve.wait_ge(r_ready, n + 1)
                        for m in range(KD):
                            last = nc.vector.tensor_tensor(r[:, m], v_ps[m][:], r[:, m], ALU.mult)
                        last.then_inc(gated, 1)
                        dve.wait_ge(gated, n + 1)
                        nc.vector.tensor_tensor(z[:], r[:], now, ALU.add).then_inc(z_ready, 1)
                        dve.wait_ge(stored[half], 16 * (i + HB * b))
                        norm.vector(dve, n, z, y[:, half], mean_ps[:])
                        dve.wait_ge(norm.done, n + 1)
                        dve.sem_inc(written, 1)


def host_layout(inputs):
    a = {k: np.asarray(v) for k, v in inputs.items()}

    def rows(w):
        return np.ascontiguousarray(w.reshape(-1, P, w.shape[-1]).transpose(1, 0, 2))

    def cols(*vs):
        return np.ascontiguousarray(np.concatenate([v.reshape(-1, P).T for v in vs], axis=1))

    def spread(v):
        return np.ascontiguousarray(np.broadcast_to(v.reshape(1, -1), (P, v.size)))

    out = {"x": np.ascontiguousarray(a["L0_attn_src"].reshape(NB, T, KD, P).transpose(3, 2, 0, 1))}
    for k, n in (("wq", "Wq"), ("wk", "Wk"), ("wv", "Wv"), ("wo", "Wo"), ("w1", "W1"), ("w2", "W2")):
        out[k] = rows(a["L0_attn_" + n])
    out["bk"], out["bv"] = spread(a["L0_attn_bk"]), spread(a["L0_attn_bv"])
    out["l0_cols"] = cols(*(a["L0_attn_" + n] for n in ("bq", "b1", "bo", "b2", "g1", "be1", "g2", "be2")))
    head = np.arange(P) // DH
    out["pair_mask"] = (head[:, None] == head[None, :]).astype(np.float32)
    out["ident"] = np.eye(P, dtype=np.float32)
    out["router"] = rows(a["L0_ffn_gate_w"].T)
    for name, w in (("gate", "gate"), ("up", "up"), ("down", "down")):
        every = np.concatenate([a["L0_ffn_r_" + w], a["L0_ffn_shared_" + w][None]]).transpose(0, 2, 1)
        out["expert_" + name] = np.ascontiguousarray(np.stack([rows(w) for w in every], axis=1))
    out["rank"] = np.ascontiguousarray(np.broadcast_to(NE - np.arange(NE, dtype=np.float32), (P, 4, NE)))
    out["pick"] = np.ascontiguousarray(np.broadcast_to(np.eye(NE, dtype=np.float32)[:, :, None], (NE, NE, P)))
    for k in ("r", "k", "v"):
        out["mix_w" + k] = rows(a["L1_ffn_W_" + k].T)
    out["mu"] = cols(a["L1_ffn_mu_r"], a["L1_ffn_mu_k"])
    A = {k[8:]: v for k, v in a.items() if k.startswith("L1_attn_")}
    for name, w in (("wq", "q_w"), ("wk", "k_w"), ("wv", "v_w"), ("wa", "alpha_w"), ("wb", "beta_w"), ("u1", "u1_w")):
        out["d_" + name] = rows(A[w])
    out["d_u2"] = np.ascontiguousarray(A["u2_w"])
    conv = A["conv_w"].reshape(KD, P, 4).transpose(1, 0, 2).reshape(P, 4 * KD)
    u1_b, b_b = np.zeros((P, 1), np.float32), np.zeros((P, 1), np.float32)
    u1_b[:DH, 0], b_b[:H, 0] = A["u1_b"], A["beta_b"]
    out["d_cols"] = np.ascontiguousarray(np.concatenate(
        [cols(A["norm_in_w"]), conv, cols(A["conv_b"], A["alpha_b"], A["u2_b"]), u1_b, b_b], axis=1))
    def by_two_pairs(t):
        t = t.reshape(HP // 2, 2, 2, DH, -1).transpose(1, 3, 0, 2, 4)
        return np.ascontiguousarray(t.reshape(P, HP, -1))
    out["d_wo"] = by_two_pairs(A["out_w"])
    out["d_head_norm"] = by_two_pairs(A["head_norm_w"])[:, :, 0].copy()
    pair_head = (2 * np.arange(HP)[:, None] + head[None, :])
    out["d_pick"] = (np.arange(H)[:, None, None] == pair_head[None]).astype(np.float32)
    for w in ("w1", "w3", "w2"):
        out["f_" + w] = rows(A["ff_" + w])
    out["f_norm_w"] = cols(A["ff_norm_w"])
    t = np.arange(CH)
    j, i = t[:, None], t[None, :]
    masks = np.zeros((2, CH, 6, 2, CH), np.float32)
    for m in range(6):
        s = 1 << m
        ok = (j // (2 * s) == i // (2 * s)) & (j // s % 2 == 0) & (i // s % 2 == 1)
        for w in range(2):
            masks[w, :, m, w] = ok
    out["d_masks"] = masks.reshape(P, 6, 2, CH)
    q_masks = np.stack([(j // 8 == i // 8) & (j <= i)] + [(j // (2 * s) == i // (2 * s)) & (j // s % 2 == 0) & (i // s % 2 == 1) for s in (8, 16)], axis=1)
    out["d_q_masks"] = np.concatenate([q_masks, q_masks]).astype(np.float32)
    out["d_carry_on"] = np.ascontiguousarray(np.broadcast_to((t > 0).astype(np.float32), (P, 2 * HP, CH)).reshape(P, 2 * HP * CH))
    return out


def kernel(**inputs):
    import concourse.bacc as bacc
    from concourse.bass_utils import run_bass_kernel_spmd as run

    nc = bacc.Bacc("TRN2", target_bir_lowering=False, num_devices=1)
    arrays = {f"in_{k}": v for k, v in host_layout(inputs).items()}
    io = {k[3:]: nc.dram_tensor(k, a.shape, F32, kind="ExternalInput").ap() for k, a in arrays.items()}
    io["out"] = nc.dram_tensor("out", (P, KD, NB, T), F32, kind="ExternalOutput").ap()
    io["mid"] = nc.dram_tensor("mid", (P, KD, NB, T), F32).ap()
    decoder_program(nc, io)
    got = run(nc, [arrays], core_ids=[0]).results[0]["out"]
    return np.ascontiguousarray(np.transpose(got, (2, 3, 1, 0)).reshape(NB, T, D))
```

```python
from contextlib import ExitStack

import numpy as np

import concourse.bass as bass
from concourse import mybir

F32 = mybir.dt.float32
ACT = mybir.ActivationFunctionType
ALU = mybir.AluOpType
AX_X = mybir.AxisListType.X

P = 128
NB, T = 2, 2048
D = 256
KD = D // P
H, DH = 16, 64
HP = H // 2
FF = 1024
KF = FF // P
NE, FE = 8, 512
BLK = 512
NBLK = T // BLK
CH = 64
NCH = BLK // CH
START = 1
PAD = 4


class Phase(ExitStack):

    def __init__(self, nc):
        super().__init__()
        self.nc, self.semaphores = nc, []
        self.callback(lambda: nc.clear_and_free_semaphores(self.semaphores))

    def semaphore(self, name):
        self.semaphores.append(self.nc.alloc_semaphore(name))
        return self.semaphores[-1]

    def preset(self):
        nc = self.nc
        engines = (nc.sync, nc.gpsimd, nc.scalar, nc.vector, nc.tensor)
        for n, s in enumerate(self.semaphores):
            engines[n % len(engines)].sem_inc(s, START)
        nc.all_engine_barrier()


def load_x(nc, io_x, x, loaded_name):
    with ExitStack() as ctx:
        x_loaded, x_padded = (ctx.enter_context(nc.semaphore(n)) for n in (loaded_name, loaded_name + "_pad"))
        with nc.Block() as block:
            @block.sync
            def _(sp):
                for k in range(KD):
                    sp.dma_start(x[:, k, :, PAD:], io_x[:, k]).then_inc(x_loaded, 16)
                sp.wait_ge(x_loaded, 16 * KD)
                sp.wait_ge(x_padded, 1)

            @block.gpsimd
            def _(pool):
                nc.gpsimd.memset(x[:, :, :, 0:PAD], 0.0).then_inc(x_padded, 1)


def decoder_program(nc, io, phases="ACDFE"):
    with ExitStack() as ctx:
        ones = ctx.enter_context(nc.sbuf_tensor("mean_ones", [P, P], F32))
        ones_ready = ctx.enter_context(nc.semaphore("ones_ready"))
        with nc.Block() as block:
            @block.gpsimd
            def _(pool):
                nc.gpsimd.memset(ones[:], 1.0 / D).then_inc(ones_ready, 1)
                pool.wait_ge(ones_ready, 1)

        def x_in_sbuf(name):
            return nc.sbuf_tensor(name, [P, KD, NB, PAD + T], F32)

        with x_in_sbuf("x_first") as x:
            if "A" in phases or "C" in phases:
                load_x(nc, io["x"], x, "x0_loaded")
            if "A" in phases:
                linear_attention(nc, io, x, ones)
                nc.all_engine_barrier()
            if "C" in phases:
                experts(nc, io, x, ones)
                nc.all_engine_barrier()
            if phases[-1] == "A":
                debug_store(nc, io, x)
        if "D" in phases:
            delta_rule(nc, io, ones)
            nc.all_engine_barrier()
        with x_in_sbuf("x_last") as x:
            if "F" in phases:
                delta_feed_forward(nc, io, x, ones)
                nc.all_engine_barrier()
            if phases == "E":
                load_x(nc, io["x"], x, "x3_loaded")
            if "E" in phases:
                channel_mix(nc, io, x, ones)
            if phases[-1] == "F":
                debug_store(nc, io, x)


def debug_store(nc, io, x):
    with nc.semaphore("stored") as stored, nc.Block() as block:
        @block.sync
        def _(sp):
            for k in range(KD):
                sp.dma_start(io["out"][:, k], x[:, k, :, PAD:]).then_inc(stored, 16)
            sp.wait_ge(stored, 16 * KD)


class Norm:

    def __init__(self, nc, ctx, name, ones, centred=True):
        self.nc, self.ones, self.centred = nc, ones, centred
        sem = lambda s: ctx.semaphore(f"{name}_{s}")
        self.mean_ready, self.centre_ready = sem("mean_ready"), sem("centre_ready")
        self.square_ready, self.var_ready, self.rstd_ready = sem("square_ready"), sem("var_ready"), sem("rstd_ready")
        self.std_ready, self.done = sem("std_ready"), sem("done")
        self.square = ctx.enter_context(nc.sbuf_tensor(f"{name}_square", [P, KD, BLK], F32))
        self.centre = ctx.enter_context(nc.sbuf_tensor(f"{name}_centre", [P, KD, BLK], F32))
        self.std = ctx.enter_context(nc.sbuf_tensor(f"{name}_std", [P, BLK], F32))
        self.eps = ctx.enter_context(nc.sbuf_tensor(f"{name}_eps", [P, 1], F32))
        self.rstd = ctx.enter_context(nc.sbuf_tensor(f"{name}_rstd", [P, BLK], F32))

    def tensor(self, pe, n, z, z_ready, z_value, mean_psum, var_psum):
        nc = self.nc
        if self.centred:
            pe.wait_ge(z_ready, z_value + START)
            for k in range(KD):
                mm = nc.tensor.matmul(mean_psum, self.ones[:], z[:, k], start=(k == 0), stop=(k == KD - 1))
            mm.then_inc(self.mean_ready, 1)
        pe.wait_ge(self.square_ready, n + 1 + START)
        for k in range(KD):
            mm = nc.tensor.matmul(var_psum, self.ones[:], self.square[:, k], start=(k == 0), stop=(k == KD - 1))
        mm.then_inc(self.var_ready, 1)

    def scalar(self, act, n, var_psum, z=None, z_ready=None, z_value=None, after_rstd=True):
        if self.centred:
            act.wait_ge(self.centre_ready, n + 1 + START)
            z = self.centre
        else:
            act.wait_ge(z_ready, z_value + START)
        self.nc.scalar.activation(self.square[:], z[:], ACT.Square).then_inc(self.square_ready, 1)
        act.wait_ge(self.var_ready, n + 1 + START)
        if after_rstd:
            act.wait_ge(self.rstd_ready, n + START)
        self.nc.scalar.activation(self.std[:], var_psum, ACT.Sqrt, bias=self.eps[:]).then_inc(self.std_ready, 1)

    def vector(self, dve, n, z, out, mean_psum):
        nc = self.nc
        if self.centred:
            dve.wait_ge(self.mean_ready, n + 1 + START)
            nc.vector.tensor_tensor(self.centre[:], z[:], mean_psum.unsqueeze(1).broadcast_to([P, KD, BLK]),
                                    ALU.subtract).then_inc(self.centre_ready, 1)
            z = self.centre
        dve.wait_ge(self.std_ready, n + 1 + START)
        nc.vector.reciprocal(self.rstd[:], self.std[:]).then_inc(self.rstd_ready, 1)
        dve.wait_ge(self.rstd_ready, n + 1 + START)
        nc.vector.tensor_tensor(out, z[:], self.rstd[:].unsqueeze(1).broadcast_to([P, KD, BLK]),
                                ALU.mult).then_inc(self.done, 1)


def linear_attention(nc, io, x, ones):
    with Phase(nc) as ctx:
        def sem(name):
            return ctx.semaphore(name)

        def sb(name, shape):
            return ctx.enter_context(nc.sbuf_tensor(name, shape, F32))

        def ps(name, shape):
            return ctx.enter_context(nc.psum_tensor(name, shape, F32))

        wq, wk, wv = sb("wq", [P, KD, FF]), sb("wk", [P, KD, FF]), sb("wv", [P, KD, FF])
        wo, w1, w2 = sb("wo", [P, HP, D]), sb("w1", [P, KD, FF]), sb("w2", [P, KF, D])
        bk, bv = sb("bk", [P, FF]), sb("bv", [P, FF])
        cols = sb("l0_columns", [P, 8 + 8 + 2 * 6])
        bq, b1 = cols[:, 0:8], cols[:, 8:16]
        bo, b2, g1, be1, g2, be2 = (cols[:, 16 + 2 * j:18 + 2 * j] for j in range(6))
        pair_mask = sb("pair_mask", [P, P])
        zeros = sb("zeros", [P, BLK])
        x_tile = sb("x_tile", [P, KD, P])
        k_raw, k_exp, k_elu = sb("k_raw", [P, FF]), sb("k_exp", [P, FF]), sb("k_elu", [P, FF])
        v_one = sb("v_one", [P, HP, P + 1])
        kv, ksum = sb("kv", [P, HP, P]), sb("ksum", [P, HP, P])
        q_exp, q_relu, q_elu = sb("q_exp", [P, 2, BLK]), sb("q_relu", [P, 2, BLK]), sb("q_elu", [P, 2, BLK])
        den = sb("den", [P, 2, BLK])
        o = sb("o", [P, HP, BLK])
        z, y = sb("z", [P, KD, BLK]), sb("y", [P, KD, BLK])
        hidden = o
        norm = Norm(nc, ctx, "l0_norm", ones)

        weights_in, masked, cleared = sem("l0_weights_in"), sem("l0_mask_ready"), sem("l0_cleared")
        tile_in, k_psum_ready, v_psum_ready = sem("tile_in"), sem("k_psum_ready"), sem("v_psum_ready")
        k_raw_ready, k_exp_ready, k_min_ready = sem("k_raw_ready"), sem("k_exp_ready"), sem("k_min_ready")
        k_ready, v_ready, kv_added = sem("k_ready"), sem("v_ready"), sem("kv_added")
        kv_summed, kv_ready = sem("kv_summed"), sem("kv_ready")
        q_psum_ready, q_exp_ready, q_relu_ready, q_ready = sem("q_psum_ready"), sem("q_exp_ready"), sem("q_relu_ready"), sem("q_ready")
        num_ready, den_ready, inv_ready, o_ready = sem("num_ready"), sem("den_ready"), sem("inv_ready"), sem("o_ready")
        wo_ready, z_ready, ln1_ready = sem("wo_ready"), sem("z_ready"), sem("ln1_ready")
        h_psum_ready, hidden_ready, w2_ready, x_written = sem("h_psum_ready"), sem("hidden_ready"), sem("w2_ready"), sem("x_written")
        ln2_ready = sem("ln2_ready")

        NT = T // P
        n_weights = 11

        def kv_pass(b):
            with ExitStack() as cp:
                k_ps = cp.enter_context(nc.psum_tensor(f"k_ps{b}", [P, FF], F32))
                v_ps = cp.enter_context(nc.psum_tensor(f"v_ps{b}", [P, FF], F32))
                kv_ps = cp.enter_context(nc.psum_tensor(f"kv_ps{b}", [P, 3, BLK], F32))
                W = P + 1

                def pair(hp):
                    return kv_ps[:, hp // 3, W * (hp % 3):W * (hp % 3) + W]

                with nc.Block() as block:
                    @block.sync
                    def _(sp):
                        if b == 0:
                            for dst, name in ((wk, "wk"), (wv, "wv"), (bk, "bk"), (bv, "bv"), (cols, "l0_cols"),
                                              (pair_mask, "pair_mask"), (wq, "wq"), (wo, "wo"), (w1, "w1"), (w2, "w2")):
                                sp.dma_start(dst[:], io[name]).then_inc(weights_in, 16)
                        with sp.Fori(0, NT) as t:
                            sp.wait_ge(v_psum_ready, t + NT * b + START)
                            sp.dma_start(x_tile[:], io["x"][:, :, b, bass.ds(t * P, P)]).then_inc(tile_in, 16)

                    @block.gpsimd
                    def _(pool):
                        if b == 0:
                            nc.gpsimd.memset(norm.eps[:], 1e-5).then_inc(cleared, 1)
                            nc.gpsimd.memset(zeros[:], 0.0).then_inc(cleared, 1)
                            nc.gpsimd.memset(v_one[:, :, P:W], 1.0).then_inc(cleared, 1)

                    @block.scalar
                    def _(act):
                        with act.Fori(0, NT) as t:
                            act.wait_ge(k_raw_ready, t + (NT * b + 1) + START)
                            act.wait_ge(k_ready, t + NT * b + START)
                            nc.scalar.activation(k_exp[:], k_raw[:], ACT.Exp).then_inc(k_exp_ready, 1)

                    @block.vector
                    def _(dve):
                        if b == 0:
                            dve.wait_ge(weights_in, 16 * 10 + START)
                            dve.wait_ge(cleared, 3 + START)
                        with dve.Fori(0, NT) as t:
                            n = t + NT * b
                            dve.wait_ge(k_psum_ready, n + 1 + START)
                            nc.vector.tensor_tensor(k_raw[:], k_ps[:], bk[:], ALU.add).then_inc(k_raw_ready, 1)
                            dve.wait_ge(v_psum_ready, n + 1 + START)
                            dve.wait_ge(kv_added, n + START)
                            nc.vector.tensor_tensor(v_one[:, :, 0:P], v_ps[:].rearrange("p (h c) -> p h c", c=P),
                                                    bv[:].rearrange("p (h c) -> p h c", c=P), ALU.add).then_inc(v_ready, 1)
                            dve.wait_ge(k_exp_ready, n + 1 + START)
                            nc.vector.tensor_scalar(k_exp[:], k_exp[:], 1.0, None, ALU.min).then_inc(k_min_ready, 1)
                            dve.wait_ge(k_min_ready, n + 1 + START)
                            nc.vector.scalar_tensor_tensor(k_elu[:], k_raw[:], 0.0, k_exp[:], ALU.max, ALU.add).then_inc(k_ready, 1)
                        dve.wait_ge(kv_summed, b + 1 + START)
                        for hp in range(HP):
                            nc.vector.tensor_tensor(kv[:, hp], pair(hp)[:, 0:P], pair_mask[:], ALU.mult).then_inc(kv_ready, 1)
                            nc.vector.tensor_scalar(ksum[:, hp], pair_mask[:], pair(hp)[:, P:W], None, ALU.mult).then_inc(kv_ready, 1)
                        dve.wait_ge(kv_ready, 2 * HP * (b + 1) + START)

                    @block.tensor
                    def _(pe):
                        if b == 0:
                            pe.wait_ge(weights_in, 16 * 10 + START)
                            pe.wait_ge(cleared, 3 + START)
                        for j in range(3):
                            nc.tensor.matmul(kv_ps[:, j, 0:3 * W], zeros[:, 0:P], zeros[:, 0:3 * W], start=True, stop=False,
                                             skip_group_check=True)
                        with pe.Fori(0, NT) as t:
                            n = t + NT * b
                            pe.wait_ge(tile_in, 16 * n + 16 + START)
                            pe.wait_ge(k_raw_ready, n + START)
                            for half in range(2):
                                for k in range(KD):
                                    mm = nc.tensor.matmul(k_ps[:, BLK * half:BLK * half + BLK], x_tile[:, k],
                                                          wk[:, k, BLK * half:BLK * half + BLK], start=(k == 0), stop=(k == KD - 1))
                            mm.then_inc(k_psum_ready, 1)
                            pe.wait_ge(v_ready, n + START)
                            for half in range(2):
                                for k in range(KD):
                                    mm = nc.tensor.matmul(v_ps[:, BLK * half:BLK * half + BLK], x_tile[:, k],
                                                          wv[:, k, BLK * half:BLK * half + BLK], start=(k == 0), stop=(k == KD - 1))
                            mm.then_inc(v_psum_ready, 1)
                            pe.wait_ge(v_ready, n + 1 + START)
                            pe.wait_ge(k_ready, n + 1 + START)
                            for hp in range(HP):
                                mm = nc.tensor.matmul(pair(hp), k_elu[:, P * hp:P * hp + P], v_one[:, hp], start=False, stop=False,
                                                      skip_group_check=True)
                            mm.then_inc(kv_added, 1)
                        for j in range(3):
                            mm = nc.tensor.matmul(kv_ps[:, j, 0:3 * W], zeros[:, 0:P], zeros[:, 0:3 * W], start=False, stop=True,
                                                  skip_group_check=True)
                        mm.then_inc(kv_summed, 1)

        def block_pass(b):
            with ExitStack() as cp:
                bank = [cp.enter_context(nc.psum_tensor(f"l0_bank{b}_{j}", [P, BLK], F32)) for j in range(8)]
                q_ps, num_ps, den_ps, acc = bank[0:2], bank[2:4], bank[4:6], bank[6:8]
                h_ps, mean_ps, var_ps = bank[0:4], bank[4], bank[5]

                with nc.Block() as block:
                    @block.tensor
                    def _(pe):
                        with pe.Fori(0, NBLK) as i:
                            n = i + NBLK * b
                            pe.wait_ge(x_written, n + START)
                            for hp in range(HP + 1):
                                if hp < HP:
                                    if hp >= 2:
                                        pe.wait_ge(q_exp_ready, HP * n + (hp - 1) + START)
                                        pe.wait_ge(q_relu_ready, HP * n + (hp - 1) + START)
                                    for k in range(KD):
                                        mm = nc.tensor.matmul(q_ps[hp % 2][:], wq[:, k, P * hp:P * hp + P],
                                                              x[:, k, b, bass.ds(PAD + i * BLK, BLK)], start=(k == 0), stop=(k == KD - 1))
                                    mm.then_inc(q_psum_ready, 1)
                                if hp >= 1:
                                    g = hp - 1
                                    pe.wait_ge(q_ready, HP * n + (g + 1) + START)
                                    if g >= 2:
                                        pe.wait_ge(o_ready, HP * n + (g - 1) + START)
                                    nc.tensor.matmul(den_ps[g % 2][:], ksum[:, g], q_elu[:, g % 2], start=True, stop=True).then_inc(den_ready, 1)
                                    nc.tensor.matmul(num_ps[g % 2][:], kv[:, g], q_elu[:, g % 2], start=True, stop=True).then_inc(num_ready, 1)
                            for hp in range(HP):
                                pe.wait_ge(o_ready, HP * n + (hp + 1) + START)
                                for m in range(KD):
                                    mm = nc.tensor.matmul(acc[m][:], wo[:, hp, P * m:P * m + P], o[:, hp], start=(hp == 0), stop=(hp == HP - 1))
                            mm.then_inc(wo_ready, 1)
                            norm.tensor(pe, 3 * n, z, z_ready, 3 * n + 1, mean_ps[:], var_ps[:])
                            pe.wait_ge(ln1_ready, 2 * n + 2 + START)
                            for m in range(KF):
                                if m >= 4:
                                    pe.wait_ge(hidden_ready, KF * n + (m - 3) + START)
                                for k in range(KD):
                                    mm = nc.tensor.matmul(h_ps[m % 4][:], w1[:, k, P * m:P * m + P], y[:, k], start=(k == 0), stop=(k == KD - 1))
                                mm.then_inc(h_psum_ready, 1)
                            for f in range(KF):
                                pe.wait_ge(hidden_ready, KF * n + (f + 1) + START)
                                for m in range(KD):
                                    mm = nc.tensor.matmul(acc[m][:], w2[:, f, P * m:P * m + P], hidden[:, f], start=(f == 0), stop=(f == KF - 1))
                            mm.then_inc(w2_ready, 1)
                            norm.tensor(pe, 3 * n + 1, z, z_ready, 3 * n + 2, mean_ps[:], var_ps[:])
                            norm.tensor(pe, 3 * n + 2, z, z_ready, 3 * n + 3, mean_ps[:], var_ps[:])

                    @block.scalar
                    def _(act):
                        with act.Fori(0, NBLK) as i:
                            n = i + NBLK * b
                            for hp in range(HP):
                                act.wait_ge(q_psum_ready, HP * n + (hp + 1) + START)
                                if hp >= 2:
                                    act.wait_ge(q_ready, HP * n + (hp - 1) + START)
                                nc.scalar.activation(q_exp[:, hp % 2], q_ps[hp % 2][:], ACT.Exp, bias=bq[:, hp:hp + 1]).then_inc(q_exp_ready, 1)
                                nc.scalar.activation(q_relu[:, hp % 2], q_ps[hp % 2][:], ACT.Relu, bias=bq[:, hp:hp + 1]).then_inc(q_relu_ready, 1)
                            norm.scalar(act, 3 * n, var_ps[:])
                            for m in range(KF):
                                act.wait_ge(h_psum_ready, KF * n + (m + 1) + START)
                                nc.scalar.activation(hidden[:, m], h_ps[m % 4][:], ACT.Gelu, bias=b1[:, m:m + 1]).then_inc(hidden_ready, 1)
                            norm.scalar(act, 3 * n + 1, var_ps[:])
                            norm.scalar(act, 3 * n + 2, var_ps[:])

                    @block.vector
                    def _(dve):
                        with dve.Fori(0, NBLK) as i:
                            n = i + NBLK * b
                            x_block = x[:, :, b, bass.ds(PAD + i * BLK, BLK)]
                            for hp in range(HP + 1):
                                if hp < HP:
                                    dve.wait_ge(q_exp_ready, HP * n + (hp + 1) + START)
                                    dve.wait_ge(q_relu_ready, HP * n + (hp + 1) + START)
                                    if hp >= 2:
                                        dve.wait_ge(num_ready, HP * n + (hp - 1) + START)
                                    nc.vector.scalar_tensor_tensor(q_elu[:, hp % 2], q_exp[:, hp % 2], 1.0, q_relu[:, hp % 2],
                                                                   ALU.min, ALU.add).then_inc(q_ready, 1)
                                if hp >= 1:
                                    g = hp - 1
                                    dve.wait_ge(den_ready, HP * n + (g + 1) + START)
                                    nc.vector.tensor_scalar(den[:, g % 2], den_ps[g % 2][:], 1e-6, None, ALU.add).then_inc(inv_ready, 1)
                                    dve.wait_ge(inv_ready, 2 * HP * n + (2 * g + 1) + START)
                                    nc.vector.reciprocal(den[:, g % 2], den[:, g % 2]).then_inc(inv_ready, 1)
                                    dve.wait_ge(inv_ready, 2 * HP * n + (2 * g + 2) + START)
                                    dve.wait_ge(num_ready, HP * n + (g + 1) + START)
                                    nc.vector.tensor_tensor(o[:, g], num_ps[g % 2][:], den[:, g % 2], ALU.mult).then_inc(o_ready, 1)
                            dve.wait_ge(wo_ready, n + 1 + START)
                            for m in range(KD):
                                last = nc.vector.scalar_tensor_tensor(z[:, m], acc[m][:], bo[:, m:m + 1], x_block[:, m], ALU.add, ALU.add)
                            last.then_inc(z_ready, 1)
                            dve.wait_ge(z_ready, 3 * n + 1 + START)
                            norm.vector(dve, 3 * n, z, y[:], mean_ps[:])
                            dve.wait_ge(norm.done, 3 * n + 1 + START)
                            for m in range(KD):
                                nc.vector.tensor_scalar(y[:, m], y[:, m], g1[:, m:m + 1], be1[:, m:m + 1], ALU.mult, ALU.add).then_inc(ln1_ready, 1)
                            dve.wait_ge(w2_ready, n + 1 + START)
                            dve.wait_ge(ln1_ready, 2 * n + 2 + START)
                            for m in range(KD):
                                last = nc.vector.scalar_tensor_tensor(z[:, m], acc[m][:], b2[:, m:m + 1], y[:, m], ALU.add, ALU.add)
                            last.then_inc(z_ready, 1)
                            norm.vector(dve, 3 * n + 1, z, y[:], mean_ps[:])
                            dve.wait_ge(norm.done, 3 * n + 2 + START)
                            for m in range(KD):
                                nc.vector.tensor_scalar(y[:, m], y[:, m], g2[:, m:m + 1], be2[:, m:m + 1], ALU.mult, ALU.add).then_inc(ln2_ready, 1)
                            dve.wait_ge(ln2_ready, 2 * n + 2 + START)
                            nc.vector.tensor_tensor(z[:], y[:], x_block, ALU.add).then_inc(z_ready, 1)
                            norm.vector(dve, 3 * n + 2, z, x_block, mean_ps[:])
                            dve.wait_ge(norm.done, 3 * n + 3 + START)
                            dve.sem_inc(x_written, 1)

        ctx.preset()
        for b in range(NB):
            kv_pass(b)
            block_pass(b)


def experts(nc, io, x, ones):
    with Phase(nc) as ctx:
        def sem(name):
            return ctx.semaphore(name)

        def sb(name, shape):
            return ctx.enter_context(nc.sbuf_tensor(name, shape, F32))

        SH = NE
        KE = FE // P
        wg, wu = sb("expert_gate", [P, NE + 1, KD, FE]), sb("expert_up", [P, NE + 1, KD, FE])
        wd = sb("expert_down", [P, NE + 1, KE, D])
        router, ident = sb("router", [P, KD, NE]), sb("ident", [P, P])
        rank = sb("rank", [P, 4, NE])
        pick = sb("pick", [NE, NE, P])
        logit_rows = sb("logit_rows", [NE, BLK])
        top, first = sb("top", [P, 4]), sb("first", [P, 4])
        hit, share = sb("hit", [P, 4, NE]), sb("share", [P, 4, NE])
        share_rows = sb("share_rows", [NE, BLK])
        xe = sb("xe", [P, 2, KD, BLK])
        silu, act_in = sb("silu", [P, 2, BLK]), sb("expert_hidden", [P, KE, BLK])
        z, y = sb("moe_z", [P, KD, BLK]), sb("moe_y", [P, KD, BLK])
        norm = Norm(nc, ctx, "moe_norm", ones)
        bank = [ctx.enter_context(nc.psum_tensor(f"moe_bank{j}", [P, BLK], F32)) for j in range(8)]
        gate_ps, up_ps, acc, spread_ps, small_ps = bank[0:2], bank[2:4], bank[4:6], bank[6], bank[7]

        weights_in, eps_ready = sem("moe_weights_in"), sem("moe_eps_ready")
        logits_ready, rows_ready, turned, top_ready = sem("logits_ready"), sem("rows_ready"), sem("turned"), sem("top_ready")
        route_step, score_ready, share_ready = sem("route_step"), sem("score_ready"), sem("share_ready")
        share_turned, share_rows_ready = sem("share_turned"), sem("share_rows_ready")
        spread_ready, xe_ready = sem("spread_ready"), sem("xe_ready")
        gate_ready, up_ready, silu_ready, hidden_ready = sem("gate_ready"), sem("up_ready"), sem("silu_ready"), sem("expert_hidden_ready")
        down_done, acc_ready, z_ready, x_written = sem("down_done"), sem("expert_acc_ready"), sem("moe_z_ready"), sem("moe_x_written")
        stored = sem("moe_stored")
        score = sb("score", [P, 4])
        ORDER = [SH] + list(range(NE))
        NX = len(ORDER)

        ctx.preset()
        with nc.Block() as block:
            @block.sync
            def _(sp):
                for dst, name in ((router, "router"), (ident, "ident"), (rank, "rank"), (pick, "pick")):
                    sp.dma_start(dst[:], io[name]).then_inc(weights_in, 16)
                for e in ORDER:
                    for dst, name in ((wg, "expert_gate"), (wu, "expert_up"), (wd, "expert_down")):
                        sp.dma_start(dst[:, e], io[name][:, e]).then_inc(weights_in, 16)
                with sp.Fori(0, NB * NBLK) as n:
                    sp.wait_ge(x_written, n + 1 + START)
                    sp.dma_start(io["x2"][:, :, bass.ds(2 * CH + n * BLK, BLK)], y[:]).then_inc(stored, 16)
                for edge in (0, 2 * CH + NB * T):
                    sp.dma_start(io["x2"][:, :, edge:edge + 2 * CH], y[:, :, 0:2 * CH]).then_inc(stored, 16)
                sp.wait_ge(stored, 16 * (NB * NBLK + 2) + START)

            @block.gpsimd
            def _(pool):
                nc.gpsimd.memset(norm.eps[:], 1e-5).then_inc(eps_ready, 1)

            @block.tensor
            def _(pe):
                pe.wait_ge(weights_in, 16 * (4 + 3 * NX) + START)
                with pe.Fori(0, NB) as b, pe.Fori(0, NBLK) as i:
                    n = i + NBLK * b
                    xb = [x[:, k, :, :].rearrange("p b t -> p (b t)")[:, bass.ds(PAD + b * (PAD + T) + i * BLK, BLK)] for k in range(KD)]
                    pe.wait_ge(x_written, n + START)
                    for k in range(KD):
                        mm = nc.tensor.matmul(small_ps[0:NE, :], router[:, k], xb[k], start=(k == 0), stop=(k == KD - 1))
                    mm.then_inc(logits_ready, 1)
                    for j, e in enumerate(ORDER):
                        if j == 1:
                            pe.wait_ge(rows_ready, n + 1 + START)
                            for s in range(4):
                                mm = nc.tensor.matmul(small_ps[:, NE * s:NE * s + NE], logit_rows[:, P * s:P * s + P], ident[0:NE, 0:NE], start=True, stop=True)
                            mm.then_inc(turned, 1)
                            pe.wait_ge(share_ready, n + 1 + START)
                            for s in range(4):
                                mm = nc.tensor.transpose(small_ps[0:NE, P * s:P * s + P], share[:, s], ident[:])
                            mm.then_inc(share_turned, 1)
                            pe.wait_ge(share_rows_ready, n + 1 + START)
                            nc.tensor.matmul(spread_ps[:], pick[:, e], share_rows[:], start=True, stop=True).then_inc(spread_ready, 1)
                        if j >= 1:
                            pe.wait_ge(xe_ready, NE * n + j + START)
                            if j < NE:
                                nc.tensor.matmul(spread_ps[:], pick[:, ORDER[j + 1]], share_rows[:], start=True, stop=True).then_inc(spread_ready, 1)
                        src = xb if e == SH else [xe[:, j % 2, k] for k in range(KD)]
                        for m in range(KE):
                            c = (NX * n + j) * KE + m
                            if j or m >= 2:
                                pe.wait_ge(hidden_ready, c - 1 + START)
                            for k in range(KD):
                                mm = nc.tensor.matmul(gate_ps[m % 2][:], wg[:, e, k, P * m:P * m + P], src[k], start=(k == 0), stop=(k == KD - 1))
                            mm.then_inc(gate_ready, 1)
                            for k in range(KD):
                                mm = nc.tensor.matmul(up_ps[m % 2][:], wu[:, e, k, P * m:P * m + P], src[k], start=(k == 0), stop=(k == KD - 1))
                            mm.then_inc(up_ready, 1)
                        for f in range(KE):
                            pe.wait_ge(hidden_ready, (NX * n + j) * KE + (f + 1) + START)
                            for m in range(KD):
                                mm = nc.tensor.matmul(acc[m][:], wd[:, e, f, P * m:P * m + P], act_in[:, f],
                                                      start=(j == 0 and f == 0), stop=(j == NX - 1 and f == KE - 1))
                        mm.then_inc(down_done, 1)
                    norm.tensor(pe, n, z, z_ready, n + 1, small_ps[:], spread_ps[:])

            @block.scalar
            def _(act):
                act.wait_ge(eps_ready, 1 + START)
                with act.Fori(0, NB) as b, act.Fori(0, NBLK) as i:
                    n = i + NBLK * b
                    for j in range(NX):
                        if j == 1:
                            act.wait_ge(top_ready, n + 1 + START)
                            nc.scalar.activation(score[:], top[:], ACT.Sigmoid).then_inc(score_ready, 1)
                        for m in range(KE):
                            c = (NX * n + j) * KE + m
                            act.wait_ge(gate_ready, c + 1 + START)
                            if j or m >= 2:
                                act.wait_ge(hidden_ready, c - 1 + START)
                            nc.scalar.activation(silu[:, m % 2], gate_ps[m % 2][:], ACT.Silu).then_inc(silu_ready, 1)
                    norm.scalar(act, n, spread_ps[:])

            @block.vector
            def _(dve):
                dve.wait_ge(weights_in, 16 * (4 + 3 * NX) + START)
                with dve.Fori(0, NB) as b, dve.Fori(0, NBLK) as i:
                    n = i + NBLK * b
                    x_block = x[:].rearrange("p k b t -> p k (b t)")[:, :, bass.ds(PAD + b * (PAD + T) + i * BLK, BLK)]
                    dve.wait_ge(logits_ready, n + 1 + START)
                    nc.vector.tensor_copy(logit_rows[:], small_ps[0:NE, :]).then_inc(rows_ready, 1)
                    for j in range(NX):
                        if j == 1:
                            logits = small_ps[:, 0:4 * NE].rearrange("p (s e) -> p s e", e=NE)
                            dve.wait_ge(turned, n + 1 + START)
                            nc.vector.tensor_reduce(top[:], logits, AX_X, ALU.max).then_inc(top_ready, 1)
                            dve.wait_ge(top_ready, n + 1 + START)
                            nc.vector.tensor_tensor(hit[:], logits, top[:].unsqueeze(2).broadcast_to([P, 4, NE]), ALU.is_equal).then_inc(route_step, 1)
                            dve.wait_ge(route_step, 4 * n + 1 + START)
                            nc.vector.tensor_tensor(hit[:], hit[:], rank[:], ALU.mult).then_inc(route_step, 1)
                            dve.wait_ge(route_step, 4 * n + 2 + START)
                            nc.vector.tensor_reduce(first[:], hit[:], AX_X, ALU.max).then_inc(route_step, 1)
                            dve.wait_ge(route_step, 4 * n + 3 + START)
                            nc.vector.tensor_tensor(hit[:], hit[:], first[:].unsqueeze(2).broadcast_to([P, 4, NE]), ALU.is_equal).then_inc(route_step, 1)
                            dve.wait_ge(route_step, 4 * n + 4 + START)
                            dve.wait_ge(score_ready, n + 1 + START)
                            nc.vector.tensor_tensor(share[:], hit[:], score[:].unsqueeze(2).broadcast_to([P, 4, NE]), ALU.mult).then_inc(share_ready, 1)
                            dve.wait_ge(share_turned, n + 1 + START)
                            nc.vector.tensor_copy(share_rows[:], small_ps[0:NE, :]).then_inc(share_rows_ready, 1)

                        def input_of(j):
                            dve.wait_ge(spread_ready, NE * n + j + START)
                            if j >= 3:
                                dve.wait_ge(down_done, NX * n + (j - 1) + START)
                            nc.vector.tensor_tensor(xe[:, j % 2], x_block, spread_ps[:].unsqueeze(1).broadcast_to([P, KD, BLK]),
                                                    ALU.mult).then_inc(xe_ready, 1)

                        if j == 1:
                            input_of(1)
                        for m in range(KE):
                            c = (NX * n + j) * KE + m
                            if m == 2 and 1 <= j < NE:
                                input_of(j + 1)
                            dve.wait_ge(silu_ready, c + 1 + START)
                            dve.wait_ge(up_ready, c + 1 + START)
                            if m == 0 and j:
                                dve.wait_ge(down_done, NX * n + j + START)
                            nc.vector.tensor_tensor(act_in[:, m], up_ps[m % 2][:], silu[:, m % 2], ALU.mult).then_inc(hidden_ready, 1)
                    dve.wait_ge(down_done, NX * n + NX + START)
                    for m in range(KD):
                        last = nc.vector.tensor_tensor(z[:, m], acc[m][:], x_block[:, m], ALU.add)
                    last.then_inc(z_ready, 1)
                    dve.wait_ge(stored, 16 * n + START)
                    norm.vector(dve, n, z, y[:], small_ps[:])
                    dve.wait_ge(norm.done, n + 1 + START)
                    dve.sem_inc(x_written, 1)


def delta_rule(nc, io, ones):
    CB = 2
    TB = CB * CH
    NT = T // TB
    NBLOCKS = NB * NT
    G4 = HP // 2
    LEVELS = (32, 16, 8)
    LIMIT = float(np.exp(12.0))

    with Phase(nc) as ctx:
        def sem(name):
            return ctx.semaphore("d_" + name)

        def sb(name, shape):
            return ctx.enter_context(nc.sbuf_tensor("d_" + name, shape, F32))

        wq, wk, wv, wa = (sb(w, [P, KD, FF]) for w in ("wq", "wk", "wv", "wa"))
        wb, u1, u2 = sb("wb", [P, KD, H]), sb("u1", [P, KD, DH]), sb("u2", [DH, D])
        wo, head_norm = sb("wo", [P, HP, D]), sb("head_norm", [P, HP])
        cols = sb("cols", [P, 2 + 8 + 2 + 8 + 2 + 1 + 1])
        norm_w, conv_w, conv_b, a_b = cols[:, 0:2], cols[:, 2:10], cols[:, 10:12], cols[:, 12:20]
        u2_b, u1_b, b_b = cols[:, 20:22], cols[0:DH, 22:23], cols[0:H, 23:24]
        pick = sb("pick", [H, HP, P])
        gather = sb("gather", [P, HP, H])
        ident = sb("ident", [P, P])
        masks = sb("masks", [P, 6, 2, CH])
        q_masks = sb("q_masks", [P, 3, CH])
        carry_on = sb("carry_on", [P, HP * CH])
        goes_on = sb("goes_on", [P, NBLOCKS + 1])
        eps = sb("eps", [P, 2])

        xb, x_res = sb("xb", [P, KD, TB]), sb("x_res", [P, KD, TB])
        std = sb("std", [P, TB])
        hn, h = sb("hn", [P, KD, 3 + TB]), sb("h", [P, KD, TB])
        square, conv = h, h
        rows = sb("rows", [H, 3, TB])
        yT = sb("yT", [P, HP // 2, 2, TB])
        u_hid = sb("u_hid", [DH, TB])
        q2, k2, kb2, n2, v2_ = ([sb(f"{w}{j}", [P, CB, HP, CH]) for j in range(2)] for w in ("q", "k", "kb", "n", "v"))
        gate2 = [sb(f"gate{j}", [P, KD, TB]) for j in range(2)]
        ex = sb("ex", [P, 5, G4, CH])
        exs = sb("exs", [P, 2, 2, G4, CH])
        g_last = sb("g_last", [P, CB, 2, G4])
        lhs = sb("lhs", [P, 2, 4, G4, P])
        rhs = sb("rhs", [P, 2, 4, G4, 2, CH])
        kG, qG, kH = sb("kG", [P, 2, G4, P]), sb("qG", [P, 2, G4, P]), sb("kH", [P, 2, G4, P])
        U = sb("U", [P, 2, 6, G4, P])
        Tm, V, Y = sb("Tm", [P, 2, G4, P]), sb("V", [P, 2, G4, P]), sb("Y", [P, 2, G4, P])
        QK = U[:, :, 0]
        B, W, S = (sb(w, [P, 2, G4 + 1, CH]) for w in ("B", "W", "S"))
        yn = sb("yn", [P, 2, G4, CH])
        ss = sb("ss", [P, 2, G4])
        qk_part = [rhs[:, :, 3, :, 0], rhs[:, :, 3, :, 1], yn]
        bank = [[ctx.enter_context(nc.psum_tensor(f"d_bank{g}{j}", [P, BLK], F32)) for j in range(3)] for g in range(2)]
        f0, f1 = (ctx.enter_context(nc.psum_tensor(f"d_f{j}", [P, BLK], F32)) for j in range(2))

        once = """weights_in cleared wo_scaled x_in res_in x_used square var std rstd head hn conv_a h k_ps q_ps a_ps b_ps v_ps z_sum a_exp
            a_min a_log n raw sq sum_ps norms norm_inv k_ready q_ready kb_ready b_rows spread_k spread_q spread_b v_ready
            out_ps u1_ps u_hid u2_ps gate_ready gated stored reset yt_ps yt_sb""".split()
        of_groups = """pool_d ex_neg exps lvl_in state_in prod u_ready qk_part y_ps y_sb dt_ps dv_ps t_sb v_ps2 v_sb v2 vd_sb kt_ps kt_sb r_ps b_sb
            w_ps w_sb o_ps s_ps s_mul s_sb ysq ss y_std ss_inv yn""".split()
        s = {name: sem(name) for name in once}
        s |= {name: (sem(name + "0"), sem(name + "1")) for name in of_groups}
        N_CLEARED, N_WEIGHTS = 16, 17

        def pairs(t):
            return t[:].rearrange("p (h c) -> p h c", h=G4)

        def few(t):
            return pairs(t)[:, :, 0:CH]

        def by_chunk(t, half):
            return t[:, :, G4 * half:G4 * half + G4].rearrange("p c h t -> p h c t")

        def projected(t):
            return t[:].rearrange("p (h c t) -> p h c t", h=G4, c=CB)

        def flat(t):
            return t[:].rearrange("p c h t -> p (c h t)")

        ctx.preset()
        with nc.Block() as block:
            @block.sync
            def _(sp):
                for dst, name in ((cols, "d_cols"), (wa, "d_wa"), (wk, "d_wk"), (wq, "d_wq"), (wv, "d_wv"), (wb, "d_wb"), (pick, "d_pick"),
                                  (gather, "d_gather"), (ident, "ident"), (masks, "d_masks"), (q_masks, "d_q_masks"), (wo, "d_wo"),
                                  (head_norm, "d_head_norm"), (u1, "d_u1"), (u2, "d_u2"), (carry_on, "d_carry_on"), (goes_on, "d_goes_on")):
                    sp.dma_start(dst[:], io[name]).then_inc(s["weights_in"], 16)

                def store(n, place):
                    sp.wait_ge(s["gated"], 2 * n + 2 + START)
                    sp.dma_start(io["mid"][:, :, place], x_res[:]).then_inc(s["stored"], 16)

                sp.dma_start(xb[:], io["x2"][:, :, TB:2 * TB]).then_inc(s["x_in"], 16)
                sp.dma_start(x_res[:], io["x2"][:, :, 0:TB]).then_inc(s["res_in"], 16)
                with sp.Fori(0, NBLOCKS) as n:
                    here, after = bass.ds(n * TB + TB, TB), bass.ds(n * TB + 2 * TB, TB)
                    sp.wait_ge(s["hn"], n + 1 + START)
                    sp.wait_ge(s["u1_ps"], n + 1 + START)
                    sp.dma_start(xb[:], io["x2"][:, :, after]).then_inc(s["x_in"], 16)
                    store(n, here)
                    sp.wait_ge(s["stored"], 16 * n + 16 + START)
                    sp.dma_start(x_res[:], io["x2"][:, :, here]).then_inc(s["res_in"], 16)
                store(NBLOCKS, bass.ds(NBLOCKS * TB + TB, TB))
                sp.wait_ge(s["stored"], 16 * (NBLOCKS + 1) + START)

            @block.gpsimd
            def _(pool):
                for t in (lhs, rhs, kG, qG, kH, B, W, yT, hn, gate2[1], yn):
                    nc.gpsimd.memset(t[:], 0.0).then_inc(s["cleared"], 1)
                nc.gpsimd.memset(eps[:, 0:1], 1e-6).then_inc(s["cleared"], 1)
                nc.gpsimd.memset(eps[:, 1:2], 0.0).then_inc(s["cleared"], 1)
                nc.gpsimd.memset(u_hid[:], 0.0).then_inc(s["cleared"], 1)
                nc.gpsimd.memset(ss[:], 0.0).then_inc(s["cleared"], 1)
                nc.gpsimd.memset(std[:], 0.0).then_inc(s["cleared"], 1)
                pool.wait_ge(s["cleared"], N_CLEARED + START)
                pool.wait_ge(s["weights_in"], 16 * N_WEIGHTS + START)

                def squares(m, p):
                    pool.wait_ge(s["raw"], 4 * m + 4 + START)
                    nc.gpsimd.tensor_tensor(kb2[p][:], k2[p][:], k2[p][:], ALU.mult).then_inc(s["sq"], 1)
                    nc.gpsimd.tensor_tensor(v2_[p][:], q2[p][:], q2[p][:], ALU.mult).then_inc(s["sq"], 1)

                def exponents(u, m, p, c, g):
                    hs = slice(G4 * g, G4 * g + G4)
                    if c == 0:
                        pool.wait_ge(s["n"], 2 * m + 2 + START)
                    pool.wait_ge(s["lvl_in"][1 - g], u + g + START)
                    nn = n2[p][:, c, hs].rearrange("p h t -> p (h t)")
                    for l, half in enumerate(LEVELS):
                        nv = nn.rearrange("p (m u t) -> p m u t", u=2, t=half)
                        ev = ex[:, l].rearrange("p h t -> p (h t)").rearrange("p (m u t) -> p m u t", u=2, t=half)
                        mid_n = nv[:, :, 0, half - 1:half].broadcast_to([P, G4 * CH // (2 * half), half])
                        nc.gpsimd.tensor_tensor(ev[:, :, 0], nv[:, :, 0], mid_n, ALU.subtract)
                        nc.gpsimd.tensor_tensor(ev[:, :, 1], mid_n, nv[:, :, 1], ALU.subtract)
                    nv = nn.rearrange("p (m t) -> p m t", t=CH)
                    nc.gpsimd.tensor_tensor(exs[:, g, 0], nv, nv[:, :, CH - 1:CH].broadcast_to([P, G4, CH]), ALU.subtract)
                    nv = nn.rearrange("p (m t) -> p m t", t=8)
                    nc.gpsimd.tensor_tensor(ex[:, 3].rearrange("p h t -> p (h t)").rearrange("p (m t) -> p m t", t=8),
                                            nv[:, :, 3:4].broadcast_to([P, G4 * 8, 8]), nv, ALU.subtract).then_inc(s["pool_d"][g], 1)

                def state_factors(u, m, p, c, g):
                    hs = slice(G4 * g, G4 * g + G4)
                    pool.wait_ge(s["kb_ready"], 2 * m + 2 + START)
                    pool.wait_ge(s["exps"][g], u + 1 + START)
                    pool.wait_ge(s["s_ps"][g], u + START)
                    parts = [(dst, src, l, head) for head in range(2) for dst, src, l in ((kG, k2, 1), (qG, q2, 1), (kH, kb2, 0))]
                    for j, (dst, src, l, head) in enumerate(parts):
                        r = slice(DH * head, DH * head + DH)
                        nc.gpsimd.tensor_tensor(dst[r, g, :, r], src[p][r, c, hs], exs[r, g, l], ALU.mult).then_inc(s["state_in"][g], 1)
                        pool.wait_ge(s["state_in"][g], 6 * u + (j + 1) + START)

                squares(0, 0)
                exponents(0, 0, 0, 0, 0)
                exponents(0, 0, 0, 0, 1)
                with pool.Fori(0, NBLOCKS // 2) as i:
                    for p in range(2):
                        n = 2 * i + p
                        for c in range(CB):
                            u = n * CB + c
                            for g in range(2):
                                pool.wait_ge(s["u_ready"][g], 6 * u + 1 + START)
                                nc.gpsimd.tensor_tensor(V[:, g], ident[:].unsqueeze(1).broadcast_to([P, G4, P]), U[:, g, 0], ALU.subtract).then_inc(s["v2"][g], 1)
                            if c == 1:
                                squares(n + 1, 1 - p)
                            for g in range(2):
                                state_factors(u, n, p, c, g)
                            for g in range(2):
                                if c == 0:
                                    exponents(u + 1, n, p, 1, g)
                                else:
                                    exponents(u + 1, n + 1, 1 - p, 0, g)
                            for g in range(2):
                                pool.wait_ge(s["o_ps"][g], u + 1 + START)
                                nc.gpsimd.tensor_tensor(S[:, g, 0:G4], S[:, g, 0:G4], g_last[:, c, g].unsqueeze(2).broadcast_to([P, G4, CH]),
                                                        ALU.mult).then_inc(s["s_mul"][g], 1)

            @block.scalar
            def _(act):
                act.wait_ge(s["cleared"], N_CLEARED + START)
                act.wait_ge(s["weights_in"], 16 * N_WEIGHTS + START)

                def x_squares(m):
                    act.wait_ge(s["x_in"], 16 * m + 16 + START)
                    act.wait_ge(s["v_ps"], 2 * m + START)
                    nc.scalar.activation(square[:], xb[:], ACT.Square).then_inc(s["square"], 1)

                def x_std(m):
                    act.wait_ge(s["var"], m + 1 + START)
                    act.wait_ge(s["u1_ps"], m + 1 + START)
                    nc.scalar.activation(std[:], f1[:, 0:TB], ACT.Sqrt, bias=eps[:, 0:1]).then_inc(s["std"], 1)

                def gate_hidden(m):
                    act.wait_ge(s["u1_ps"], m + 1 + START)
                    nc.scalar.activation(u_hid[:], f1[0:DH, TB:2 * TB], ACT.Silu, bias=u1_b).then_inc(s["u_hid"], 1)

                def conv_silu(m):
                    act.wait_ge(s["conv_a"], m + 1 + START)
                    for kk in range(KD):
                        last = nc.scalar.activation(h[:, kk], conv[:, kk], ACT.Silu, bias=conv_b[:, kk:kk + 1])
                    last.then_inc(s["h"], 1)

                def gates(m, p):
                    act.wait_ge(s["u2_ps"], m + 1 + START)
                    for kk in range(KD):
                        last = nc.scalar.activation(gate2[p][:, kk], f0[:, TB * kk:TB * kk + TB], ACT.Sigmoid, bias=u2_b[:, kk:kk + 1])
                    last.then_inc(s["gate_ready"], 1)

                def decay_exp(m, p):
                    act.wait_ge(s["z_sum"], 2 * m + 2 + START)
                    nc.scalar.activation(n2[p][:], n2[p][:], ACT.Exp, scale=-1.0).then_inc(s["a_exp"], 1)

                def decay_log(m, p):
                    act.wait_ge(s["a_min"], m + 1 + START)
                    nc.scalar.activation(n2[p][:], n2[p][:], ACT.Ln, bias=1.0).then_inc(s["a_log"], 1)

                def raw(m, dst, ready):
                    for half in range(2):
                        act.wait_ge(s[ready], 2 * m + (half + 1) + START)
                        nc.scalar.copy(by_chunk(dst, half), projected([f0, f1][half])).then_inc(s["raw"], 1)

                def betas(m):
                    act.wait_ge(s["b_ps"], m + 1 + START)
                    nc.scalar.activation(rows[:, 2], f0[0:H, 0:TB], ACT.Sigmoid, bias=b_b).then_inc(s["b_rows"], 1)

                def norms(m):
                    act.wait_ge(s["sum_ps"], m + 1 + START)
                    nc.scalar.activation(rows[:, 0:2], f1[0:H, 0:2 * TB].rearrange("p (a t) -> p a t", a=2), ACT.Sqrt, bias=eps[0:H, 1:2]).then_inc(s["norms"], 1)

                def values(m, p):
                    for c in range(CB):
                        act.wait_ge(s["v_ps"], 2 * m + (c + 1) + START)
                        nc.scalar.copy(v2_[p][:, c], [f0, f1][c][:].rearrange("p (h t) -> p h t", h=HP)).then_inc(s["v_ready"], 1)

                def exponentials(u, p, c, g):
                    hs = slice(G4 * g, G4 * g + G4)
                    act.wait_ge(s["pool_d"][g], u + 1 + START)
                    nc.scalar.activation(ex[:, 4], ex[:, 3], ACT.Exp, scale=-1.0).then_inc(s["ex_neg"][g], 1)
                    nc.scalar.activation(ex[:, 0:3], ex[:, 0:3], ACT.Exp)
                    nc.scalar.activation(exs[:, g, 0], exs[:, g, 0], ACT.Exp)
                    act.wait_ge(s["ex_neg"][g], u + 1 + START)
                    nc.scalar.activation(ex[:, 3], ex[:, 3], ACT.Exp)
                    nc.scalar.activation(exs[:, g, 1], n2[p][:, c, hs], ACT.Exp, scale=-1.0).then_inc(s["exps"][g], 1)

                x_squares(0)
                x_std(0)
                gate_hidden(0)
                gates(0, 0)
                conv_silu(0)
                decay_exp(0, 0)
                raw(0, k2[0], "k_ps")
                raw(0, q2[0], "q_ps")
                decay_log(0, 0)
                betas(0)
                norms(0)
                values(0, 0)
                exponentials(0, 0, 0, 0)
                exponentials(0, 0, 0, 1)
                with act.Fori(0, NBLOCKS // 2) as i:
                    for p in range(2):
                        n = 2 * i + p
                        m = n + 1
                        for c in range(CB):
                            u = n * CB + c
                            if c == 0:
                                x_squares(m)
                            for j in range(1, 6):
                                for g in range(2):
                                    act.wait_ge(s["y_ps"][g], 6 * u + (j + 1) + START)
                                    nc.scalar.copy(Y[:, g], pairs(bank[g][1])).then_inc(s["y_sb"][g], 1)
                                if c == 0:
                                    if j == 1:
                                        x_std(m)
                                        gate_hidden(m)
                                        exponentials(u + 1, p, 1, 0)
                                    if j == 2:
                                        conv_silu(m)
                                        gates(m, 1 - p)
                                    if j == 3:
                                        exponentials(u + 1, p, 1, 1)
                                    if j == 4:
                                        decay_exp(m, 1 - p)
                                        raw(m, k2[1 - p], "k_ps")
                                    if j == 5:
                                        raw(m, q2[1 - p], "q_ps")
                                        decay_log(m, 1 - p)
                                else:
                                    if j == 1:
                                        betas(m)
                                        norms(m)
                                    if j == 4:
                                        exponentials(u + 1, 1 - p, 0, 0)
                                    if j == 5:
                                        values(m, 1 - p)
                                for g in range(2):
                                    if j < 5:
                                        act.wait_ge(s["v_ps2"][g], 4 * u + j + START)
                                        nc.scalar.copy(V[:, g], pairs(bank[g][2])).then_inc(s["v_sb"][g], 1)
                            for g in range(2):
                                act.wait_ge(s["kt_ps"][g], u + 1 + START)
                                nc.scalar.copy(kH[:, g], pairs(bank[g][0])).then_inc(s["kt_sb"][g], 1)
                            if c == 1:
                                exponentials(u + 1, 1 - p, 0, 1)
                            for g in range(2):
                                act.wait_ge(s["w_ps"][g], u + 1 + START)
                                nc.scalar.copy(W[:, g, 0:G4], few(bank[g][0])).then_inc(s["w_sb"][g], 1)
                            for g in range(2):
                                act.wait_ge(s["o_ps"][g], u + 1 + START)
                                nc.scalar.activation(yn[:, g], few(bank[g][2]), ACT.Square).then_inc(s["ysq"][g], 1)
                            for g in range(2):
                                act.wait_ge(s["ss"][g], u + 1 + START)
                                nc.scalar.activation(ss[:, g], ss[:, g], ACT.Sqrt, scale=1.0 / DH, bias=eps[:, 0:1]).then_inc(s["y_std"][g], 1)

            @block.vector
            def _(dve):
                dve.wait_ge(s["cleared"], N_CLEARED + START)
                dve.wait_ge(s["weights_in"], 16 * N_WEIGHTS + START)
                nc.vector.tensor_tensor(wo[:], wo[:], head_norm[:].unsqueeze(2).broadcast_to([P, HP, D]), ALU.mult).then_inc(s["wo_scaled"], 1)

                def norm_and_conv(m):
                    nc.vector.tensor_scalar(hn[:, :, 0:3], hn[:, :, TB:TB + 3], goes_on[:, bass.ds(m, 1)], None, ALU.mult).then_inc(s["head"], 1)
                    dve.wait_ge(s["std"], m + 1 + START)
                    nc.vector.reciprocal(std[:], std[:]).then_inc(s["rstd"], 1)
                    dve.wait_ge(s["rstd"], m + 1 + START)
                    dve.wait_ge(s["head"], 4 * m + 1 + START)
                    for kk in range(KD):
                        last = nc.vector.scalar_tensor_tensor(hn[:, kk, 3:], xb[:, kk], norm_w[:, kk:kk + 1], std[:], ALU.mult, ALU.mult)
                    last.then_inc(s["hn"], 1)
                    dve.wait_ge(s["hn"], m + 1 + START)
                    for tap in range(4):
                        for kk in range(KD):
                            w = conv_w[:, 4 * kk + tap:4 * kk + tap + 1]
                            if tap == 0:
                                last = nc.vector.tensor_scalar(conv[:, kk], hn[:, kk, 0:TB], w, None, ALU.mult)
                            else:
                                last = nc.vector.scalar_tensor_tensor(conv[:, kk], hn[:, kk, tap:tap + TB], w, conv[:, kk], ALU.mult, ALU.add)
                        last.then_inc(s["head" if tap < 3 else "conv_a"], 1)
                        if tap < 3:
                            dve.wait_ge(s["head"], 4 * m + (tap + 2) + START)
                    dve.wait_ge(s["conv_a"], m + 1 + START)

                def decay_logits(m, p):
                    for half in range(2):
                        dve.wait_ge(s["a_ps"], 2 * m + (half + 1) + START)
                        nc.vector.tensor_tensor(by_chunk(n2[p], half), projected([f0, f1][half]),
                                                a_b[:, G4 * half:G4 * half + G4].unsqueeze(2).unsqueeze(3).broadcast_to([P, G4, CB, CH]), ALU.add).then_inc(s["z_sum"], 1)

                def decay_min(m, p):
                    dve.wait_ge(s["a_exp"], m + 1 + START)
                    nc.vector.tensor_scalar(n2[p][:], n2[p][:], LIMIT, None, ALU.min).then_inc(s["a_min"], 1)

                def decay_sum(m, p):
                    dve.wait_ge(s["a_log"], m + 1 + START)
                    for c in range(CB):
                        part = n2[p][:, c].rearrange("p h t -> p (h t)")
                        nc.vector.tensor_tensor_scan(part, carry_on[:], part, 0.0, ALU.mult, ALU.add).then_inc(s["n"], 1)

                def norm_rows(m):
                    dve.wait_ge(s["norms"], m + 1 + START)
                    nc.vector.tensor_scalar(rows[:, 0:2], rows[:, 0:2], 1e-6, None, ALU.add).then_inc(s["norm_inv"], 1)
                    dve.wait_ge(s["norm_inv"], 2 * m + 1 + START)
                    nc.vector.reciprocal(rows[:, 0:2], rows[:, 0:2]).then_inc(s["norm_inv"], 1)

                def scaled(m, dst, src, spread, done):
                    for half in range(2):
                        dve.wait_ge(s[spread], 2 * m + (half + 1) + START)
                        nc.vector.tensor_tensor(by_chunk(dst, half), by_chunk(src, half), projected([f0, f1][half]), ALU.mult).then_inc(s[done], 1)
                    dve.wait_ge(s[done], 2 * m + 2 + START)

                def level_factors(u, p, c, g):
                    hs = slice(G4 * g, G4 * g + G4)
                    k, q, kb = k2[p], q2[p], kb2[p]
                    dve.wait_ge(s["exps"][g], u + 1 + START)
                    dve.wait_ge(s["qk_part"][g], 5 * u + START)
                    for l, half in enumerate(LEVELS):
                        def lv(t):
                            return t.rearrange("p h (m u t) -> p h m u t", u=2, t=half)
                        e = lv(ex[:, l])
                        for j, t in ((0, k), (1, q)):
                            nc.vector.tensor_tensor(lv(rhs[:, g, l, :, j])[:, :, :, 1], lv(t[:, c, hs])[:, :, :, 1], e[:, :, :, 1], ALU.mult)
                        for head in range(2):
                            r = slice(DH * head, DH * head + DH)
                            nc.vector.tensor_tensor(lv(lhs[r, g, l, :, r])[:, :, :, 0], lv(kb[r, c, hs])[:, :, :, 0], e[r, :, :, 0], ALU.mult)
                    for j, t in ((0, k), (1, q)):
                        nc.vector.tensor_tensor(rhs[:, g, 3, :, j], t[:, c, hs], ex[:, 3], ALU.mult)
                    for head in range(2):
                        r = slice(DH * head, DH * head + DH)
                        nc.vector.tensor_tensor(lhs[r, g, 3, :, r], kb[r, c, hs], ex[r, 4], ALU.mult)
                    nc.vector.tensor_copy(g_last[:, c, g], exs[:, g, 1, :, CH - 1]).then_inc(s["lvl_in"][g], 1)

                def q_side(bk):
                    return bk[:].rearrange("p (h a t) -> p h a t", h=G4, a=2)[:, :, 1]

                def masked(g, j, m):
                    src = bank[g][j][:].rearrange("p (h a t) -> p h a t", h=G4, a=2)[:, :, 0].unsqueeze(2).broadcast_to([P, G4, 2, CH])
                    dst = U[:, g, m].rearrange("p h (a t) -> p h a t", a=2)
                    return nc.vector.tensor_tensor(dst, src, masks[:, m].unsqueeze(1).broadcast_to([P, G4, 2, CH]), ALU.mult)

                def products(u, g, j):
                    dve.wait_ge(s["prod"][g], 4 * u + (j + 1) + START)
                    for m in ((0, 1, 2), (3,), (4,))[j]:
                        masked(g, j, m).then_inc(s["u_ready"][g], 1)
                    nc.vector.tensor_tensor(qk_part[j][:, g], q_side(bank[g][j]), q_masks[:, j].unsqueeze(1).broadcast_to([P, G4, CH]),
                                            ALU.mult).then_inc(s["qk_part"][g], 1)

                def first_inverse(u, g):
                    dve.wait_ge(s["y_ps"][g], 6 * u + 1 + START)
                    nc.vector.tensor_tensor(Tm[:, g], ident[:].unsqueeze(1).broadcast_to([P, G4, P]), pairs(bank[g][1]), ALU.subtract).then_inc(s["t_sb"][g], 1)
                    dve.wait_ge(s["prod"][g], 4 * u + 4 + START)
                    masked(g, 0, 5)
                    dve.wait_ge(s["qk_part"][g], 5 * u + 3 + START)
                    nc.vector.tensor_tensor(qk_part[2][:, g], q_side(bank[g][0]), qk_part[2][:, g], ALU.add).then_inc(s["u_ready"][g], 1)

                def put_qk_together(u, g):
                    nc.vector.tensor_tensor(qk_part[1][:, g], qk_part[1][:, g], qk_part[0][:, g], ALU.add).then_inc(s["qk_part"][g], 1)
                    dve.wait_ge(s["v2"][g], u + 1 + START)
                    dve.wait_ge(s["qk_part"][g], 5 * u + 4 + START)
                    dve.wait_ge(s["u_ready"][g], 6 * u + 6 + START)
                    for head in range(2):
                        r = slice(DH * head, DH * head + DH)
                        last = nc.vector.tensor_tensor(QK[r, g, :, r], qk_part[1][r, g], qk_part[2][r, g], ALU.add)
                    last.then_inc(s["qk_part"][g], 1)

                def turned_out(u, c):
                    dve.wait_ge(s["yt_ps"], u + 1 + START)
                    nc.vector.tensor_copy(yT[:, :, :, CH * c:CH * c + CH], f1[:].rearrange("p (a h t) -> p a h t", a=HP // 2, h=2)).then_inc(s["yt_sb"], 1)

                def finish(n, p):
                    dve.wait_ge(s["out_ps"], n + 1 + START)
                    dve.wait_ge(s["gate_ready"], n + START)
                    nc.vector.tensor_tensor(gate2[1 - p][:], f0[:, 0:KD * TB].rearrange("p (k t) -> p k t", k=KD), gate2[1 - p][:], ALU.mult).then_inc(s["gated"], 1)
                    dve.wait_ge(s["gated"], 2 * n + 1 + START)
                    dve.wait_ge(s["res_in"], 16 * n + 16 + START)
                    nc.vector.tensor_tensor(x_res[:], x_res[:], gate2[1 - p][:], ALU.add).then_inc(s["gated"], 1)

                norm_and_conv(0)
                decay_logits(0, 0)
                decay_min(0, 0)
                decay_sum(0, 0)
                norm_rows(0)
                scaled(0, k2[0], k2[0], "spread_k", "k_ready")
                scaled(0, q2[0], q2[0], "spread_q", "q_ready")
                scaled(0, kb2[0], k2[0], "spread_b", "kb_ready")
                level_factors(0, 0, 0, 0)
                level_factors(0, 0, 0, 1)
                with dve.Fori(0, NB) as b:
                    nc.vector.memset(S[:], 0.0).then_inc(s["reset"], 1)
                    with dve.Fori(0, NT // 2) as i:
                        for p in range(2):
                            n = NT * b + 2 * i + p
                            m = n + 1
                            for c in range(CB):
                                u = n * CB + c
                                for j in range(3):
                                    for g in range(2):
                                        products(u, g, j)
                                    if j == 1:
                                        turned_out(u, 1 - c)
                                for g in range(2):
                                    first_inverse(u, g)
                                for j in range(1, 6):
                                    for g in range(2):
                                        if j < 5:
                                            dve.wait_ge(s["dt_ps"][g], 4 * u + j + START)
                                            dve.wait_ge(s["t_sb"][g], 5 * u + j + START)
                                            nc.vector.tensor_tensor(Tm[:, g], Tm[:, g], pairs(bank[g][0]), ALU.subtract).then_inc(s["t_sb"][g], 1)
                                        else:
                                            dve.wait_ge(s["dv_ps"][g], u + 1 + START)
                                            nc.vector.tensor_tensor(V[:, g], V[:, g], pairs(bank[g][2]), ALU.subtract).then_inc(s["vd_sb"][g], 1)
                                    if j == 1:
                                        for g in range(2):
                                            put_qk_together(u, g)
                                    if c == 0:
                                        if j == 1:
                                            finish(n, p)
                                            norm_and_conv(m)
                                        if j == 2:
                                            level_factors(u + 1, p, 1, 0)
                                        if j == 3:
                                            level_factors(u + 1, p, 1, 1)
                                        if j == 4:
                                            decay_logits(m, 1 - p)
                                        if j == 5:
                                            decay_min(m, 1 - p)
                                    else:
                                        if j == 1:
                                            norm_rows(m)
                                        if j == 2:
                                            scaled(m, k2[1 - p], k2[1 - p], "spread_k", "k_ready")
                                        if j == 3:
                                            scaled(m, q2[1 - p], q2[1 - p], "spread_q", "q_ready")
                                        if j == 4:
                                            scaled(m, kb2[1 - p], k2[1 - p], "spread_b", "kb_ready")
                                        if j == 5:
                                            level_factors(u + 1, 1 - p, 0, 0)
                                for g in range(2):
                                    hs = slice(G4 * g, G4 * g + G4)
                                    dve.wait_ge(s["r_ps"][g], u + 1 + START)
                                    if g == 0:
                                        dve.wait_ge(s["v_ready"], 2 * n + 2 + START)
                                    nc.vector.tensor_tensor(B[:, g, 0:G4], v2_[p][:, c, hs], few(bank[g][1]), ALU.subtract).then_inc(s["b_sb"][g], 1)
                                if c == 0:
                                    decay_sum(m, 1 - p)
                                else:
                                    level_factors(u + 1, 1 - p, 0, 1)
                                for g in range(2):
                                    dve.wait_ge(s["s_mul"][g], u + 1 + START)
                                    dve.wait_ge(s["s_ps"][g], u + 1 + START)
                                    nc.vector.tensor_tensor(S[:, g, 0:G4], S[:, g, 0:G4], few(bank[g][1]), ALU.add).then_inc(s["s_sb"][g], 1)
                                    dve.wait_ge(s["ysq"][g], u + 1 + START)
                                    nc.vector.tensor_reduce(ss[:, g], yn[:, g], AX_X, ALU.add).then_inc(s["ss"][g], 1)
                                for g in range(2):
                                    dve.wait_ge(s["y_std"][g], u + 1 + START)
                                    nc.vector.reciprocal(ss[:, g], ss[:, g]).then_inc(s["ss_inv"][g], 1)
                                    dve.wait_ge(s["ss_inv"][g], u + 1 + START)
                                    nc.vector.tensor_tensor(yn[:, g], few(bank[g][2]), ss[:, g].unsqueeze(2).broadcast_to([P, G4, CH]), ALU.mult).then_inc(s["yn"][g], 1)
                turned_out(CB * NBLOCKS, 1)
                finish(NBLOCKS, 0)

            @block.tensor
            def _(pe):
                pe.wait_ge(s["cleared"], N_CLEARED + START)
                pe.wait_ge(s["weights_in"], 16 * N_WEIGHTS + START)
                pe.wait_ge(s["wo_scaled"], 1 + START)

                def x_products(m):
                    pe.wait_ge(s["square"], m + 1 + START)
                    for kk in range(KD):
                        mm = nc.tensor.matmul(f1[:, 0:TB], ones[:], square[:, kk], start=(kk == 0), stop=(kk == KD - 1))
                    mm.then_inc(s["var"], 1)
                    for kk in range(KD):
                        mm = nc.tensor.matmul(f1[0:DH, TB:2 * TB], u1[:, kk], xb[:, kk], start=(kk == 0), stop=(kk == KD - 1))
                    mm.then_inc(s["u1_ps"], 1)

                def gate_products(m):
                    pe.wait_ge(s["u_hid"], m + 1 + START)
                    for kk in range(KD):
                        mm = nc.tensor.matmul(f0[:, TB * kk:TB * kk + TB], u2[:, P * kk:P * kk + P], u_hid[:], start=True, stop=True)
                    mm.then_inc(s["u2_ps"], 1)

                def project(w, done):
                    for half in range(2):
                        for j in range(G4):
                            hp = G4 * half + j
                            for kk in range(KD):
                                mm = nc.tensor.matmul([f0, f1][half][:, P * j:P * j + P], w[:, kk, P * hp:P * hp + P], h[:, kk],
                                                      start=(kk == 0), stop=(kk == KD - 1))
                        mm.then_inc(s[done], 1)

                def decays(m):
                    pe.wait_ge(s["h"], m + 1 + START)
                    pe.wait_ge(s["gate_ready"], m + 1 + START)
                    pe.wait_ge(s["std"], m + 1 + START)
                    project(wa, "a_ps")

                def keys(m):
                    pe.wait_ge(s["z_sum"], 2 * m + 2 + START)
                    project(wk, "k_ps")

                def queries(m):
                    pe.wait_ge(s["raw"], 4 * m + 2 + START)
                    project(wq, "q_ps")

                def betas(m):
                    pe.wait_ge(s["raw"], 4 * m + 4 + START)
                    for kk in range(KD):
                        mm = nc.tensor.matmul(f0[0:H, 0:TB], wb[:, kk], h[:, kk], start=(kk == 0), stop=(kk == KD - 1))
                    mm.then_inc(s["b_ps"], 1)

                def norm_sums(m, p):
                    pe.wait_ge(s["sq"], 2 * m + 2 + START)
                    for j, t in ((0, kb2[p]), (1, v2_[p])):
                        for hp in range(HP):
                            mm = nc.tensor.matmul(f1[0:H, TB * j:TB * j + TB], gather[:, hp], t[:, :, hp], start=(hp == 0), stop=(hp == HP - 1))
                    mm.then_inc(s["sum_ps"], 1)

                def spread(m, j, done, free, count):
                    pe.wait_ge(s[free], count + START)
                    for half in range(2):
                        for hp in range(G4):
                            mm = nc.tensor.matmul([f0, f1][half][:, P * hp:P * hp + P], pick[:, G4 * half + hp], rows[:, j], start=True, stop=True)
                        mm.then_inc(s[done], 1)

                def spread_k(m):
                    pe.wait_ge(s["b_rows"], m + 1 + START)
                    spread(m, 0, "spread_k", "norm_inv", 2 * m + 2)

                def spread_q(m):
                    spread(m, 1, "spread_q", "k_ready", 2 * m + 2)

                def spread_b(m):
                    spread(m, 2, "spread_b", "q_ready", 2 * m + 2)

                def values(m):
                    pe.wait_ge(s["kb_ready"], 2 * m + 2 + START)
                    for c in range(CB):
                        for head in range(2):
                            r = slice(DH * head, DH * head + DH)
                            for kk in range(KD):
                                mm = nc.tensor.matmul([f0, f1][c][r, :], h[:, kk, CH * c:CH * c + CH],
                                                      wv[:, kk].rearrange("p (h a t) -> p h a t", a=2, t=DH)[:, :, head],
                                                      start=(kk == 0), stop=(kk == KD - 1))
                        mm.then_inc(s["v_ps"], 1)

                def turn_out(u, n, c):
                    if c == 0:
                        pe.wait_ge(s["v_ready"], 2 * n + 2 + START)
                    else:
                        pe.wait_ge(s["raw"], 4 * n + 8 + START)
                    for g in range(2):
                        pe.wait_ge(s["yn"][g], u + START)
                        for a in range(2):
                            mm = nc.tensor.transpose(f1[:, 2 * P * g + P * a:2 * P * g + P * a + P],
                                                     yn[:, g, 2 * a:2 * a + 2].rearrange("p h t -> p (h t)"), ident[:])
                    mm.then_inc(s["yt_ps"], 1)

                def output(n):
                    pe.wait_ge(s["yt_sb"], CB * n + 1 + START)
                    for m in range(KD):
                        for a in range(HP // 2):
                            for head in range(2):
                                mm = nc.tensor.matmul(f0[:, TB * m:TB * m + TB], wo[:, 2 * a + head, P * m:P * m + P], yT[:, a, head],
                                                      start=(a == 0 and head == 0), stop=(a == HP // 2 - 1 and head == 1))
                    mm.then_inc(s["out_ps"], 1)

                x_products(0)
                gate_products(0)
                decays(0)
                keys(0)
                queries(0)
                betas(0)
                norm_sums(0, 0)
                spread_k(0)
                spread_q(0)
                spread_b(0)
                values(0)
                with pe.Fori(0, NB) as b, pe.Fori(0, NT // 2) as i:
                    for p in range(2):
                        n = NT * b + 2 * i + p
                        m = n + 1
                        for c in range(CB):
                            u = n * CB + c
                            for j in range(4):
                                if j == 2:
                                    turn_out(u, n, c)
                                if j == 3 and c == 0:
                                    output(n)
                                    x_products(m)
                                if j == 3 and c == 1:
                                    pe.wait_ge(s["yt_sb"], u + 1 + START)
                                    norm_sums(m, 1 - p)
                                for g in range(2):
                                    if j == 0:
                                        pe.wait_ge(s["lvl_in"][g], u + 1 + START)
                                        pe.wait_ge(s["w_sb"][g], u + START)
                                    elif j == 1:
                                        pe.wait_ge(s["s_sb"][g], u + START)
                                    elif j == 2:
                                        pe.wait_ge(s["yn"][g], u + START)
                                    else:
                                        pe.wait_ge(s["u_ready"][g], 6 * u + 4 + START)
                                        pe.wait_ge(s["qk_part"][g], 5 * u + 2 + START)
                                        for hp in range(G4):
                                            mm = nc.tensor.transpose(bank[g][1][:, P * hp:P * hp + P], U[:, g, 0, hp], ident[:])
                                        mm.then_inc(s["y_ps"][g], 1)
                                    for hp in range(G4):
                                        mm = nc.tensor.matmul(bank[g][j % 3][:, P * hp:P * hp + P], lhs[:, g, 3 - j, hp],
                                                              rhs[:, g, 3 - j, hp].rearrange("p a t -> p (a t)"), start=True, stop=True)
                                    mm.then_inc(s["prod"][g], 1)
                            for j in range(1, 6):
                                for g in range(2):
                                    pe.wait_ge(s["u_ready"][g], 6 * u + (j + 1) + START)
                                    pe.wait_ge(s["t_sb"][g], 5 * u + j + START)
                                    for hp in range(G4):
                                        mm = nc.tensor.matmul(bank[g][1][:, P * hp:P * hp + P], U[:, g, j, hp], Tm[:, g, hp], start=True, stop=True)
                                    mm.then_inc(s["y_ps"][g], 1)
                                for g in range(2):
                                    pe.wait_ge(s["y_sb"][g], 5 * u + j + START)
                                    if j == 1:
                                        pe.wait_ge(s["v2"][g], u + 1 + START)
                                        pe.wait_ge(s["qk_part"][g], 5 * u + 3 + START)
                                        pe.wait_ge(s["u_ready"][g], 6 * u + 6 + START)
                                    else:
                                        pe.wait_ge(s["v_sb"][g], 4 * u + (j - 1) + START)
                                    if j < 5:
                                        for hp in range(G4):
                                            mm = nc.tensor.matmul(bank[g][0][:, P * hp:P * hp + P], V[:, g, hp], Y[:, g, hp], start=True, stop=True)
                                        mm.then_inc(s["dt_ps"][g], 1)
                                    else:
                                        for hp in range(G4):
                                            mm = nc.tensor.matmul(bank[g][2][:, P * hp:P * hp + P], Y[:, g, hp], V[:, g, hp], start=True, stop=True)
                                        mm.then_inc(s["dv_ps"][g], 1)
                                if c == 0:
                                    if j == 2:
                                        pe.wait_ge(s["gated"], 2 * n + 2 + START)
                                        gate_products(m)
                                    if j == 3:
                                        decays(m)
                                    if j == 4:
                                        keys(m)
                                    if j == 5:
                                        queries(m)
                                else:
                                    if j == 2:
                                        spread_k(m)
                                    if j == 3:
                                        spread_q(m)
                                    if j == 4:
                                        spread_b(m)
                                    if j == 5:
                                        values(m)
                                for g in range(2):
                                    if j < 5:
                                        pe.wait_ge(s["t_sb"][g], 5 * u + (j + 1) + START)
                                        for hp in range(G4):
                                            mm = nc.tensor.transpose(bank[g][2][:, P * hp:P * hp + P], Tm[:, g, hp], ident[:])
                                        mm.then_inc(s["v_ps2"][g], 1)
                            for g in range(2):
                                pe.wait_ge(s["state_in"][g], 6 * u + 6 + START)
                                for hp in range(G4):
                                    mm = nc.tensor.transpose(bank[g][0][:, P * hp:P * hp + P], kH[:, g, hp], ident[:])
                                mm.then_inc(s["kt_ps"][g], 1)
                            for g in range(2):
                                if g == 0:
                                    pe.wait_ge(s["reset"], b + 1 + START)
                                pe.wait_ge(s["s_sb"][g], u + START)
                                for hp in range(G4):
                                    mm = nc.tensor.matmul(bank[g][1][:, P * hp:P * hp + P], kG[:, g, hp], S[:, g, hp:hp + 2], start=True, stop=True)
                                mm.then_inc(s["r_ps"][g], 1)
                            if c == 0:
                                betas(m)
                            for g in range(2):
                                pe.wait_ge(s["b_sb"][g], u + 1 + START)
                                pe.wait_ge(s["vd_sb"][g], u + 1 + START)
                                pe.wait_ge(s["kt_sb"][g], u + 1 + START)
                                for hp in range(G4):
                                    mm = nc.tensor.matmul(bank[g][0][:, P * hp:P * hp + P], V[:, g, hp], B[:, g, hp:hp + 2], start=True, stop=True)
                                mm.then_inc(s["w_ps"][g], 1)
                            for g in range(2):
                                pe.wait_ge(s["w_sb"][g], u + 1 + START)
                                for hp in range(G4):
                                    nc.tensor.matmul(bank[g][2][:, P * hp:P * hp + P], qG[:, g, hp], S[:, g, hp:hp + 2], start=True, stop=False)
                                    mm = nc.tensor.matmul(bank[g][2][:, P * hp:P * hp + P], QK[:, g, hp], W[:, g, hp:hp + 2], start=False, stop=True)
                                mm.then_inc(s["o_ps"][g], 1)
                                for hp in range(G4):
                                    mm = nc.tensor.matmul(bank[g][1][:, P * hp:P * hp + P], kH[:, g, hp], W[:, g, hp:hp + 2], start=True, stop=True)
                                mm.then_inc(s["s_ps"][g], 1)
                turn_out(CB * NBLOCKS, NBLOCKS, 0)
                output(NBLOCKS)


def delta_feed_forward(nc, io, x, ones):
    with Phase(nc) as ctx:
        def sem(name):
            return ctx.semaphore("f_" + name)

        def sb(name, shape):
            return ctx.enter_context(nc.sbuf_tensor("f_" + name, shape, F32))

        w1, w3, w2 = sb("w1", [P, KD, FF]), sb("w3", [P, KD, FF]), sb("w2", [P, KF, D])
        norm_w = sb("norm_w", [P, KD])
        mid, y2, z = sb("mid", [P, 2, KD, BLK]), sb("y2", [P, KD, BLK]), sb("z", [P, KD, BLK])
        silu, hidden = sb("silu", [P, 2, BLK]), sb("hidden", [P, KF, BLK])
        rms = Norm(nc, ctx, "f_rms", ones, centred=False)
        norm = Norm(nc, ctx, "f_norm", ones)
        bank = [ctx.enter_context(nc.psum_tensor(f"f_bank{j}", [P, BLK], F32)) for j in range(8)]
        gate_ps, up_ps, acc, mean_ps, var_ps = bank[0:2], bank[2:4], bank[4:6], bank[6], bank[7]
        weights_in, eps_ready, mid_in = sem("weights_in"), sem("eps_ready"), [sem("mid_in0"), sem("mid_in1")]
        x_in, padded = [sem("x_in0"), sem("x_in1")], sem("padded")
        x_old = sb("x_old", [P, 2, KD, BLK])
        y2_ready, gate_done, up_done, silu_ready, hidden_ready = sem("y2_ready"), sem("gate_done"), sem("up_done"), sem("silu_ready"), sem("hidden_ready")
        down_done, z_ready = sem("down_done"), sem("z_ready")
        sum_ready = [sem("sum_ready0"), sem("sum_ready1")]
        HB = NBLK // 2

        ctx.preset()
        with nc.Block() as block:
            @block.sync
            def _(sp):
                for dst, name in ((w1, "f_w1"), (w3, "f_w3"), (w2, "f_w2"), (norm_w, "f_norm_w")):
                    sp.dma_start(dst[:], io[name]).then_inc(weights_in, 16)
                with sp.Fori(0, NB) as b, sp.Fori(0, HB) as i:
                    for half in range(2):
                        sp.wait_ge(sum_ready[half], i + HB * b + START)
                        start = 2 * CH + b * T + (2 * i + half) * BLK
                        sp.dma_start(mid[:, half], io["mid"][:, :, bass.ds(start + 2 * CH, BLK)]).then_inc(mid_in[half], 16)
                        sp.dma_start(x_old[:, half], io["x2"][:, :, bass.ds(start, BLK)]).then_inc(x_in[half], 16)

            @block.gpsimd
            def _(pool):
                nc.gpsimd.memset(norm.eps[:], 1e-5).then_inc(eps_ready, 1)
                nc.gpsimd.memset(x[:, :, :, 0:PAD], 0.0).then_inc(padded, 1)
                nc.gpsimd.memset(rms.eps[:], 1e-6).then_inc(eps_ready, 1)

            @block.tensor
            def _(pe):
                pe.wait_ge(weights_in, 16 * 4 + START)
                with pe.Fori(0, NB) as b, pe.Fori(0, HB) as i:
                    for half in range(2):
                        n = 2 * i + half + NBLK * b
                        rms.tensor(pe, n, None, None, None, mean_ps[:], var_ps[:])
                        pe.wait_ge(y2_ready, KD * n + KD + START)
                        for m in range(KF):
                            c = KF * n + m
                            if m >= 2:
                                pe.wait_ge(hidden_ready, c - 1 + START)
                            for w, dst, done in ((w1, gate_ps, gate_done), (w3, up_ps, up_done)):
                                for k in range(KD):
                                    mm = nc.tensor.matmul(dst[m % 2][:], w[:, k, P * m:P * m + P], y2[:, k], start=(k == 0), stop=(k == KD - 1))
                                mm.then_inc(done, 1)
                        for f in range(KF):
                            pe.wait_ge(hidden_ready, KF * n + (f + 1) + START)
                            for m in range(KD):
                                mm = nc.tensor.matmul(acc[m][:], w2[:, f, P * m:P * m + P], hidden[:, f], start=(f == 0), stop=(f == KF - 1))
                        mm.then_inc(down_done, 1)
                        norm.tensor(pe, n, z, z_ready, n + 1, mean_ps[:], var_ps[:])

            @block.scalar
            def _(act):
                act.wait_ge(eps_ready, 2 + START)
                with act.Fori(0, NB) as b, act.Fori(0, HB) as i:
                    for half in range(2):
                        n = 2 * i + half + NBLK * b
                        rms.scalar(act, n, var_ps[:], mid[:, half], mid_in[half], 16 * (i + HB * b + 1))
                        for m in range(KF):
                            c = KF * n + m
                            act.wait_ge(gate_done, c + 1 + START)
                            if m >= 2:
                                act.wait_ge(hidden_ready, c - 1 + START)
                            nc.scalar.activation(silu[:, m % 2], gate_ps[m % 2][:], ACT.Silu).then_inc(silu_ready, 1)
                        norm.scalar(act, n, var_ps[:])

            @block.vector
            def _(dve):
                dve.wait_ge(weights_in, 16 * 4 + START)
                with dve.Fori(0, NB) as b, dve.Fori(0, HB) as i:
                    for half in range(2):
                        n = 2 * i + half + NBLK * b
                        start = b * (PAD + T) + PAD + (2 * i + half) * BLK
                        x_block = x[:].rearrange("p k b t -> p k (b t)")[:, :, bass.ds(start, BLK)]
                        dve.wait_ge(mid_in[half], 16 * (i + HB * b + 1) + START)
                        rms.vector(dve, n, mid[:, half], y2[:], mean_ps[:])
                        dve.wait_ge(rms.done, n + 1 + START)
                        for k in range(KD):
                            nc.vector.tensor_scalar(y2[:, k], y2[:, k], norm_w[:, k:k + 1], None, ALU.mult).then_inc(y2_ready, 1)
                        for m in range(KF):
                            c = KF * n + m
                            dve.wait_ge(silu_ready, c + 1 + START)
                            dve.wait_ge(up_done, c + 1 + START)
                            nc.vector.tensor_tensor(hidden[:, m], up_ps[m % 2][:], silu[:, m % 2], ALU.mult).then_inc(hidden_ready, 1)
                        dve.wait_ge(x_in[half], 16 * (i + HB * b + 1) + START)
                        nc.vector.tensor_tensor(z[:], x_old[:, half], mid[:, half], ALU.add).then_inc(sum_ready[half], 1)
                        dve.wait_ge(down_done, n + 1 + START)
                        dve.wait_ge(sum_ready[half], i + HB * b + 1 + START)
                        for m in range(KD):
                            last = nc.vector.tensor_tensor(z[:, m], acc[m][:], z[:, m], ALU.add)
                        last.then_inc(z_ready, 1)
                        dve.wait_ge(z_ready, n + 1 + START)
                        norm.vector(dve, n, z, x_block, mean_ps[:])
                        dve.wait_ge(norm.done, n + 1 + START)


def channel_mix(nc, io, x, ones):
    with Phase(nc) as ctx:
        def sem(name):
            return ctx.semaphore(name)

        def sb(name, shape):
            return ctx.enter_context(nc.sbuf_tensor(name, shape, F32))

        wr, wk, wv = sb("mix_wr", [P, KD, D]), sb("mix_wk", [P, KD, D]), sb("mix_wv", [P, KD, D])
        mu = sb("mu", [P, 2 * KD])
        step, xr, xk = sb("mix_step", [P, KD, BLK]), sb("xr", [P, KD, BLK]), sb("xk", [P, KD, BLK])
        r, k_relu, k_act = sb("mix_r", [P, KD, BLK]), sb("k_relu", [P, KD, BLK]), sb("k_act", [P, KD, BLK])
        z, y = sb("mix_z", [P, KD, BLK]), sb("mix_y", [P, 2, KD, BLK])
        norm = Norm(nc, ctx, "mix_norm", ones)
        bank = [ctx.enter_context(nc.psum_tensor(f"mix_bank{j}", [P, BLK], F32)) for j in range(8)]
        r_ps, k_ps, v_ps, mean_ps, var_ps = bank[0:2], bank[2:4], bank[4:6], bank[6], bank[7]

        weights_in, eps_ready = sem("mix_weights_in"), sem("mix_eps_ready")
        step_ready, xk_ready, xr_ready = sem("mix_step_ready"), sem("xk_ready"), sem("xr_ready")
        k_done, r_done, v_done = sem("mix_k_done"), sem("mix_r_done"), sem("mix_v_done")
        relu_ready, r_ready, k_act_ready, gated, z_ready = sem("relu_ready"), sem("mix_r_ready"), sem("k_act_ready"), sem("gated"), sem("mix_z_ready")
        stored, written = [sem("out_stored0"), sem("out_stored1")], sem("out_written")
        HB = NBLK // 2

        ctx.preset()
        with nc.Block() as block:
            @block.sync
            def _(sp):
                for dst, name in ((wr, "mix_wr"), (wk, "mix_wk"), (wv, "mix_wv"), (mu, "mu")):
                    sp.dma_start(dst[:], io[name]).then_inc(weights_in, 16)
                with sp.Fori(0, NB) as b, sp.Fori(0, HB) as i:
                    for half in range(2):
                        n = 2 * i + half + NBLK * b
                        sp.wait_ge(written, n + 1 + START)
                        sp.dma_start(io["out"][:, :, b, bass.ds((2 * i + half) * BLK, BLK)], y[:, half]).then_inc(stored[half], 16)
                for half in range(2):
                    sp.wait_ge(stored[half], 16 * NB * HB + START)

            @block.gpsimd
            def _(pool):
                nc.gpsimd.memset(norm.eps[:], 1e-5).then_inc(eps_ready, 1)
                with pool.Fori(0, NB) as b, pool.Fori(0, HB) as i:
                    for half in range(2):
                        n = 2 * i + half + NBLK * b
                        pool.wait_ge(relu_ready, n + 1 + START)
                        nc.gpsimd.tensor_tensor(k_act[:], k_relu[:], k_relu[:], ALU.mult).then_inc(k_act_ready, 1)

            @block.tensor
            def _(pe):
                pe.wait_ge(weights_in, 16 * 4 + START)
                with pe.Fori(0, NB) as b, pe.Fori(0, HB) as i:
                    for half in range(2):
                        n = 2 * i + half + NBLK * b
                        for dst, w, src, ready, done in ((k_ps, wk, xk, xk_ready, k_done), (r_ps, wr, xr, xr_ready, r_done)):
                            pe.wait_ge(ready, KD * (n + 1) + START)
                            pe.wait_ge(gated, n + START)
                            for m in range(KD):
                                for k in range(KD):
                                    mm = nc.tensor.matmul(dst[m][:], w[:, k, P * m:P * m + P], src[:, k], start=(k == 0), stop=(k == KD - 1))
                            mm.then_inc(done, 1)
                        pe.wait_ge(k_act_ready, n + 1 + START)
                        for m in range(KD):
                            for k in range(KD):
                                mm = nc.tensor.matmul(v_ps[m][:], wv[:, k, P * m:P * m + P], k_act[:, k], start=(k == 0), stop=(k == KD - 1))
                        mm.then_inc(v_done, 1)
                        norm.tensor(pe, n, z, z_ready, n + 1, mean_ps[:], var_ps[:])

            @block.scalar
            def _(act):
                act.wait_ge(eps_ready, 1 + START)
                with act.Fori(0, NB) as b, act.Fori(0, HB) as i:
                    for half in range(2):
                        n = 2 * i + half + NBLK * b
                        act.wait_ge(k_done, n + 1 + START)
                        act.wait_ge(k_act_ready, n + START)
                        act.wait_ge(v_done, n + START)
                        for m in range(KD):
                            last = nc.scalar.activation(k_relu[:, m], k_ps[m][:], ACT.Relu)
                        last.then_inc(relu_ready, 1)
                        act.wait_ge(r_done, n + 1 + START)
                        for m in range(KD):
                            last = nc.scalar.activation(r[:, m], r_ps[m][:], ACT.Sigmoid)
                        last.then_inc(r_ready, 1)
                        norm.scalar(act, n, var_ps[:])

            @block.vector
            def _(dve):
                dve.wait_ge(weights_in, 16 * 4 + START)
                with dve.Fori(0, NB) as b, dve.Fori(0, HB) as i:
                    for half in range(2):
                        n = 2 * i + half + NBLK * b
                        start = b * (PAD + T) + PAD + (2 * i + half) * BLK
                        tokens = x[:].rearrange("p k b t -> p k (b t)")
                        now, before = tokens[:, :, bass.ds(start, BLK)], tokens[:, :, bass.ds(start - 1, BLK)]
                        nc.vector.tensor_tensor(step[:], now, before, ALU.subtract).then_inc(step_ready, 1)
                        dve.wait_ge(step_ready, n + 1 + START)
                        dve.wait_ge(r_done, n + START)
                        for dst, col, ready in ((xk, KD, xk_ready), (xr, 0, xr_ready)):
                            for k in range(KD):
                                nc.vector.scalar_tensor_tensor(dst[:, k], step[:, k], mu[:, col + k:col + k + 1], before[:, k],
                                                               ALU.mult, ALU.add).then_inc(ready, 1)
                        dve.wait_ge(v_done, n + 1 + START)
                        dve.wait_ge(r_ready, n + 1 + START)
                        for m in range(KD):
                            last = nc.vector.tensor_tensor(r[:, m], v_ps[m][:], r[:, m], ALU.mult)
                        last.then_inc(gated, 1)
                        dve.wait_ge(gated, n + 1 + START)
                        nc.vector.tensor_tensor(z[:], r[:], now, ALU.add).then_inc(z_ready, 1)
                        dve.wait_ge(stored[half], 16 * (i + HB * b) + START)
                        norm.vector(dve, n, z, y[:, half], mean_ps[:])
                        dve.wait_ge(norm.done, n + 1 + START)
                        dve.sem_inc(written, 1)


def host_layout(inputs):
    a = {k: np.asarray(v) for k, v in inputs.items()}

    def rows(w):
        return np.ascontiguousarray(w.reshape(-1, P, w.shape[-1]).transpose(1, 0, 2))

    def cols(*vs):
        return np.ascontiguousarray(np.concatenate([v.reshape(-1, P).T for v in vs], axis=1))

    def spread(v):
        return np.ascontiguousarray(np.broadcast_to(v.reshape(1, -1), (P, v.size)))

    out = {"x": np.ascontiguousarray(a["L0_attn_src"].reshape(NB, T, KD, P).transpose(3, 2, 0, 1))}
    for k, n in (("wq", "Wq"), ("wk", "Wk"), ("wv", "Wv"), ("wo", "Wo"), ("w1", "W1"), ("w2", "W2")):
        out[k] = rows(a["L0_attn_" + n])
    out["bk"], out["bv"] = spread(a["L0_attn_bk"]), spread(a["L0_attn_bv"])
    out["l0_cols"] = cols(*(a["L0_attn_" + n] for n in ("bq", "b1", "bo", "b2", "g1", "be1", "g2", "be2")))
    head = np.arange(P) // DH
    out["pair_mask"] = (head[:, None] == head[None, :]).astype(np.float32)
    out["ident"] = np.eye(P, dtype=np.float32)
    out["router"] = rows(a["L0_ffn_gate_w"].T)
    for name, w in (("gate", "gate"), ("up", "up"), ("down", "down")):
        every = np.concatenate([a["L0_ffn_r_" + w], a["L0_ffn_shared_" + w][None]]).transpose(0, 2, 1)
        out["expert_" + name] = np.ascontiguousarray(np.stack([rows(w) for w in every], axis=1))
    out["rank"] = np.ascontiguousarray(np.broadcast_to(NE - np.arange(NE, dtype=np.float32), (P, 4, NE)))
    out["pick"] = np.ascontiguousarray(np.broadcast_to(np.eye(NE, dtype=np.float32)[:, :, None], (NE, NE, P)))
    for k in ("r", "k", "v"):
        out["mix_w" + k] = rows(a["L1_ffn_W_" + k].T)
    out["mu"] = cols(a["L1_ffn_mu_r"], a["L1_ffn_mu_k"])
    A = {k[8:]: v for k, v in a.items() if k.startswith("L1_attn_")}
    for name, w in (("wq", "q_w"), ("wk", "k_w"), ("wv", "v_w"), ("wa", "alpha_w"), ("wb", "beta_w"), ("u1", "u1_w")):
        out["d_" + name] = rows(A[w])
    out["d_u2"] = np.ascontiguousarray(A["u2_w"])
    conv = A["conv_w"].reshape(KD, P, 4).transpose(1, 0, 2).reshape(P, 4 * KD)
    u1_b, b_b = np.zeros((P, 1), np.float32), np.zeros((P, 1), np.float32)
    u1_b[:DH, 0], b_b[:H, 0] = A["u1_b"], A["beta_b"]
    out["d_cols"] = np.ascontiguousarray(np.concatenate(
        [cols(A["norm_in_w"]), conv, cols(A["conv_b"], A["alpha_b"], A["u2_b"]), u1_b, b_b], axis=1))
    def by_two_pairs(t):
        t = t.reshape(HP // 2, 2, 2, DH, -1).transpose(1, 3, 0, 2, 4)
        return np.ascontiguousarray(t.reshape(P, HP, -1))
    out["d_wo"] = by_two_pairs(A["out_w"])
    out["d_head_norm"] = by_two_pairs(A["head_norm_w"])[:, :, 0].copy()
    pair_head = (2 * np.arange(HP)[:, None] + head[None, :])
    out["d_pick"] = (np.arange(H)[:, None, None] == pair_head[None]).astype(np.float32)
    for w in ("w1", "w3", "w2"):
        out["f_" + w] = rows(A["ff_" + w])
    out["f_norm_w"] = cols(A["ff_norm_w"])
    out["d_gather"] = np.ascontiguousarray(out["d_pick"].transpose(2, 1, 0))
    blocks = np.arange(NB * T // (2 * CH) + 1)
    out["d_goes_on"] = np.ascontiguousarray(np.broadcast_to((blocks % (T // (2 * CH)) > 0).astype(np.float32), (P, blocks.size)))
    t = np.arange(CH)
    j, i = t[:, None], t[None, :]
    masks = np.zeros((2, CH, 6, 2, CH), np.float32)
    for m in range(6):
        s = 1 << m
        ok = (j // (2 * s) == i // (2 * s)) & (j // s % 2 == 0) & (i // s % 2 == 1)
        for w in range(2):
            masks[w, :, m, w] = ok
    out["d_masks"] = masks.reshape(P, 6, 2, CH)
    q_masks = np.stack([(j // 8 == i // 8) & (j <= i)] + [(j // (2 * s) == i // (2 * s)) & (j // s % 2 == 0) & (i // s % 2 == 1) for s in (8, 16)], axis=1)
    out["d_q_masks"] = np.concatenate([q_masks, q_masks]).astype(np.float32)
    out["d_carry_on"] = np.ascontiguousarray(np.broadcast_to((t > 0).astype(np.float32), (P, HP, CH)).reshape(P, HP * CH))
    return out


def kernel(**inputs):
    import concourse.bacc as bacc
    from concourse.bass_utils import run_bass_kernel_spmd as run

    nc = bacc.Bacc("TRN2", target_bir_lowering=False, num_devices=1)
    arrays = {f"in_{k}": v for k, v in host_layout(inputs).items()}
    io = {k[3:]: nc.dram_tensor(k, a.shape, F32, kind="ExternalInput").ap() for k, a in arrays.items()}
    io["out"] = nc.dram_tensor("out", (P, KD, NB, T), F32, kind="ExternalOutput").ap()
    for name in ("x2", "mid"):
        io[name] = nc.dram_tensor(name, (P, KD, NB * T + 4 * CH), F32).ap()
    decoder_program(nc, io)
    got = run(nc, [arrays], core_ids=[0]).results[0]["out"]
    return np.ascontiguousarray(np.transpose(got, (2, 3, 1, 0)).reshape(NB, T, D))
```

```python
from contextlib import ExitStack

import numpy as np

import concourse.bass as bass
from concourse import mybir

F32 = mybir.dt.float32
ACT = mybir.ActivationFunctionType
ALU = mybir.AluOpType
AX_X = mybir.AxisListType.X

P = 128
NB, T = 2, 2048
D = 256
KD = D // P
H, DH = 16, 64
HP = H // 2
FF = 1024
KF = FF // P
NE, FE = 8, 512
BLK = 512
NBLK = T // BLK
CH = 64
START = 1
PAD = 4


class Phase(ExitStack):

    def __init__(self, nc):
        super().__init__()
        self.nc, self.semaphores, self.started = nc, [], []
        self.callback(lambda: nc.clear_and_free_semaphores(self.semaphores))

    def semaphore(self, name, start=START):
        self.semaphores.append(self.nc.alloc_semaphore(name))
        if start:
            self.started.append(self.semaphores[-1])
        return self.semaphores[-1]

    def preset(self):
        nc = self.nc
        engines = (nc.sync, nc.gpsimd, nc.scalar, nc.vector, nc.tensor)
        for n, s in enumerate(self.started):
            engines[n % len(engines)].sem_inc(s, START)
        nc.all_engine_barrier()


def decoder_program(nc, io):
    with ExitStack() as ctx:
        ones = ctx.enter_context(nc.sbuf_tensor("mean_ones", [P, P], F32))
        ones_ready = ctx.enter_context(nc.semaphore("ones_ready"))
        with nc.Block() as block:
            @block.gpsimd
            def _(pool):
                nc.gpsimd.memset(ones[:], 1.0 / D).then_inc(ones_ready, 1)
                pool.wait_ge(ones_ready, 1)

        def x_in_sbuf(name):
            return nc.sbuf_tensor(name, [P, KD, NB, PAD + T], F32)

        with x_in_sbuf("x_first") as x:
            linear_attention(nc, io, x, ones)
            nc.all_engine_barrier()
            experts(nc, io, x, ones)
            nc.all_engine_barrier()
        delta_rule(nc, io, ones)
        nc.all_engine_barrier()
        with x_in_sbuf("x_last") as x:
            delta_feed_forward(nc, io, x, ones)
            nc.all_engine_barrier()
            channel_mix(nc, io, x, ones)


class Norm:

    def __init__(self, nc, ctx, name, ones, centred=True, buffers=True):
        self.nc, self.name, self.ones, self.centred = nc, name, ones, centred
        sem = lambda s: ctx.semaphore(f"{name}_{s}")
        self.mean_ready, self.centre_ready = sem("mean_ready"), sem("centre_ready")
        self.square_ready, self.var_ready, self.rstd_ready = sem("square_ready"), sem("var_ready"), sem("rstd_ready")
        self.std_ready, self.done = sem("std_ready"), sem("done")
        if buffers:
            self.allocate(ctx)

    def allocate(self, ctx):
        def sb(name, shape):
            return ctx.enter_context(self.nc.sbuf_tensor(f"{self.name}_{name}", shape, F32))

        self.square, self.centre = sb("square", [P, KD, BLK]), sb("centre", [P, KD, BLK])
        self.std, self.rstd, self.eps = sb("std", [P, BLK]), sb("rstd", [P, BLK]), sb("eps", [P, 1])

    def tensor_mean(self, pe, z, z_ready, z_value, mean_psum):
        pe.wait_ge(z_ready, z_value + START)
        for k in range(KD):
            mm = self.nc.tensor.matmul(mean_psum, self.ones[:], z[:, k], start=(k == 0), stop=(k == KD - 1))
        mm.then_inc(self.mean_ready, 1)

    def tensor_var(self, pe, n, var_psum):
        pe.wait_ge(self.square_ready, n + 1 + START)
        for k in range(KD):
            mm = self.nc.tensor.matmul(var_psum, self.ones[:], self.square[:, k], start=(k == 0), stop=(k == KD - 1))
        mm.then_inc(self.var_ready, 1)

    def tensor(self, pe, n, z, z_ready, z_value, mean_psum, var_psum):
        if self.centred:
            self.tensor_mean(pe, z, z_ready, z_value, mean_psum)
        self.tensor_var(pe, n, var_psum)

    def scalar_square(self, act, n, z=None, z_ready=None, z_value=None):
        if self.centred:
            act.wait_ge(self.centre_ready, n + 1 + START)
            z = self.centre
        else:
            act.wait_ge(z_ready, z_value + START)
        self.nc.scalar.activation(self.square[:], z[:], ACT.Square).then_inc(self.square_ready, 1)

    def scalar_std(self, act, n, var_psum):
        act.wait_ge(self.var_ready, n + 1 + START)
        act.wait_ge(self.rstd_ready, n + START)
        self.nc.scalar.activation(self.std[:], var_psum, ACT.Sqrt, bias=self.eps[:]).then_inc(self.std_ready, 1)

    def scalar(self, act, n, var_psum, z=None, z_ready=None, z_value=None):
        self.scalar_square(act, n, z, z_ready, z_value)
        self.scalar_std(act, n, var_psum)

    def vector_centre(self, dve, n, z, mean_psum):
        dve.wait_ge(self.mean_ready, n + 1 + START)
        self.nc.vector.tensor_tensor(self.centre[:], z[:], mean_psum.unsqueeze(1).broadcast_to([P, KD, BLK]),
                                     ALU.subtract).then_inc(self.centre_ready, 1)

    def vector_out(self, dve, n, z, out):
        nc = self.nc
        dve.wait_ge(self.std_ready, n + 1 + START)
        nc.vector.reciprocal(self.rstd[:], self.std[:]).then_inc(self.rstd_ready, 1)
        dve.wait_ge(self.rstd_ready, n + 1 + START)
        nc.vector.tensor_tensor(out, z[:], self.rstd[:].unsqueeze(1).broadcast_to([P, KD, BLK]),
                                ALU.mult).then_inc(self.done, 1)

    def vector(self, dve, n, z, out, mean_psum):
        if self.centred:
            self.vector_centre(dve, n, z, mean_psum)
            z = self.centre
        self.vector_out(dve, n, z, out)


def linear_attention(nc, io, x, ones):
    with Phase(nc) as ctx:
        def sem(name):
            return ctx.semaphore(name)

        def sb(name, shape):
            return ctx.enter_context(nc.sbuf_tensor(name, shape, F32))

        def ps(name, shape):
            return ctx.enter_context(nc.psum_tensor(name, shape, F32))

        wq, wk, wv = sb("wq", [P, KD, FF]), sb("wk", [P, KD, FF]), sb("wv", [P, KD, FF])
        wo, w1, w2 = sb("wo", [P, HP, D]), sb("w1", [P, KD, FF]), sb("w2", [P, KF, D])
        bk, bv = sb("bk", [P, FF]), sb("bv", [P, FF])
        cols = sb("l0_columns", [P, 8 + 8 + 2 * 6])
        bq, b1 = cols[:, 0:8], cols[:, 8:16]
        bo, b2, g1, be1, g2, be2 = (cols[:, 16 + 2 * j:18 + 2 * j] for j in range(6))
        pair_mask = sb("pair_mask", [P, P])
        zeros = sb("zeros", [P, BLK])
        gather, pick = sb("head_gather", [P, HP, H]), sb("head_pick", [H, HP, P])
        x_tile = sb("x_tile", [P, 2, KD, P])
        k_raw, k_exp, k_elu = sb("k_raw", [P, FF]), sb("k_exp", [P, FF]), sb("k_elu", [P, FF])
        v_one = sb("v_one", [P, HP, P + 1])
        kv, ksum = sb("kv", [P, HP, P]), sb("ksum", [P, HP, H])
        q_exp, q_relu, q_elu = sb("q_exp", [P, 2, BLK]), sb("q_relu", [P, 2, BLK]), sb("q_elu", [P, 2, BLK])
        den = sb("den", [H, BLK])
        o = sb("o", [P, HP, BLK])
        z, y = sb("z", [P, KD, BLK]), sb("y", [P, KD, BLK])
        hidden = o
        norm = Norm(nc, ctx, "l0_norm", ones)

        first_in, x_in, x_padded = sem("l0_first_in"), sem("l0_x_in"), sem("l0_x_padded")
        weights_in, cleared = sem("l0_weights_in"), sem("l0_cleared")
        tile_in, k_psum_ready, v_psum_ready = [sem("tile_in0"), sem("tile_in1")], sem("k_psum_ready"), sem("v_psum_ready")
        k_raw_ready, k_exp_ready, k_min_ready = sem("k_raw_ready"), sem("k_exp_ready"), sem("k_min_ready")
        k_ready, v_ready, kv_added = sem("k_ready"), sem("v_ready"), sem("kv_added")
        kv_summed, kv_ready = sem("kv_summed"), sem("kv_ready")
        q_psum_ready, q_exp_ready, q_relu_ready, q_ready = sem("q_psum_ready"), sem("q_exp_ready"), sem("q_relu_ready"), sem("q_ready")
        num_ready, den_ready, inv_ready, o_ready = sem("num_ready"), sem("den_ready"), sem("inv_ready"), sem("o_ready")
        num_copied, spread_ready = sem("num_copied"), sem("spread_ready")
        wo_ready, z_ready, ln1_ready = sem("wo_ready"), sem("z_ready"), sem("ln1_ready")
        h_psum_ready, hidden_ready, w2_ready = sem("h_psum_ready"), sem("hidden_ready"), sem("w2_ready")
        ln2_ready = sem("ln2_ready")

        NT = T // P

        def kv_pass(b):
            with ExitStack() as cp:
                k_ps = cp.enter_context(nc.psum_tensor(f"k_ps{b}", [P, FF], F32))
                v_ps = cp.enter_context(nc.psum_tensor(f"v_ps{b}", [P, FF], F32))
                kv_ps = cp.enter_context(nc.psum_tensor(f"kv_ps{b}", [P, 3, BLK], F32))
                W = P + 1

                def pair(hp):
                    return kv_ps[:, hp // 3, W * (hp % 3):W * (hp % 3) + W]

                with nc.Block() as block:
                    @block.sync
                    def _(sp):
                        if b == 0:
                            for dst, name in ((wk, "wk"), (wv, "wv"), (bk, "bk"), (bv, "bv"), (gather, "d_gather"), (pair_mask, "pair_mask")):
                                sp.dma_start(dst[:], io[name]).then_inc(first_in, 16)
                        for slot in range(2):
                            sp.dma_start(x_tile[:, slot], io["x"][:, :, b, P * slot:P * slot + P]).then_inc(tile_in[slot], 16)
                        with sp.Fori(0, NT // 2 - 1) as i:
                            for slot in range(2):
                                sp.wait_ge(v_psum_ready, 2 * i + (slot + 1) + NT * b + START)
                                sp.dma_start(x_tile[:, slot], io["x"][:, :, b, bass.ds((2 * i + slot) * P + 2 * P, P)]).then_inc(tile_in[slot], 16)
                        if b == 0:
                            sp.wait_ge(weights_in, 16 * 6 + START)
                            sp.wait_ge(x_in, 16 * KD + START)
                            sp.wait_ge(x_padded, 1 + START)

                    @block.gpsimd
                    def _(pool):
                        if b == 0:
                            nc.gpsimd.memset(x[:, :, :, 0:PAD], 0.0).then_inc(x_padded, 1)
                            nc.gpsimd.memset(norm.eps[:], 1e-5).then_inc(cleared, 1)
                            nc.gpsimd.memset(zeros[:], 0.0).then_inc(cleared, 1)
                            nc.gpsimd.memset(v_one[:, :, P:W], 1.0).then_inc(cleared, 1)

                    @block.scalar
                    def _(act):
                        if b == 0:
                            act.wait_ge(first_in, 16 * 6 + START)
                            for dst, name in ((cols, "l0_cols"), (pick, "d_pick"), (wq, "wq"), (wo, "wo"), (w1, "w1"), (w2, "w2")):
                                nc.scalar.dma_start(dst[:], io[name]).then_inc(weights_in, 16)
                            for k in range(KD):
                                nc.scalar.dma_start(x[:, k, :, PAD:], io["x"][:, k]).then_inc(x_in, 16)
                        with act.Fori(0, NT) as t:
                            act.wait_ge(k_raw_ready, t + (NT * b + 1) + START)
                            act.wait_ge(k_ready, t + NT * b + START)
                            nc.scalar.activation(k_exp[:], k_raw[:], ACT.Exp).then_inc(k_exp_ready, 1)

                    @block.vector
                    def _(dve):
                        if b == 0:
                            dve.wait_ge(first_in, 16 * 6 + START)
                            dve.wait_ge(cleared, 3 + START)
                        with dve.Fori(0, NT) as t:
                            n = t + NT * b
                            dve.wait_ge(k_psum_ready, n + 1 + START)
                            dve.wait_ge(k_ready, n + START)
                            nc.vector.tensor_tensor(k_raw[:], k_ps[:], bk[:], ALU.add).then_inc(k_raw_ready, 1)
                            dve.wait_ge(k_exp_ready, n + 1 + START)
                            nc.vector.tensor_scalar(k_exp[:], k_exp[:], 1.0, None, ALU.min).then_inc(k_min_ready, 1)
                            dve.wait_ge(k_min_ready, n + 1 + START)
                            dve.wait_ge(kv_added, n + START)
                            nc.vector.scalar_tensor_tensor(k_elu[:], k_raw[:], 0.0, k_exp[:], ALU.max, ALU.add).then_inc(k_ready, 1)
                            dve.wait_ge(v_psum_ready, n + 1 + START)
                            nc.vector.tensor_tensor(v_one[:, :, 0:P], v_ps[:].rearrange("p (h c) -> p h c", c=P),
                                                    bv[:].rearrange("p (h c) -> p h c", c=P), ALU.add).then_inc(v_ready, 1)
                        dve.wait_ge(kv_summed, b + 1 + START)
                        for hp in range(HP):
                            nc.vector.tensor_tensor(kv[:, hp], pair(hp)[:, 0:P], pair_mask[:], ALU.mult).then_inc(kv_ready, 1)
                            nc.vector.tensor_scalar(ksum[:, hp], gather[:, hp], pair(hp)[:, P:W], None, ALU.mult).then_inc(kv_ready, 1)
                        dve.wait_ge(kv_ready, 2 * HP * (b + 1) + START)

                    @block.tensor
                    def _(pe):
                        if b == 0:
                            pe.wait_ge(first_in, 16 * 6 + START)
                            pe.wait_ge(cleared, 3 + START)
                        for j in range(3):
                            nc.tensor.matmul(kv_ps[:, j, 0:3 * W], zeros[:, 0:P], zeros[:, 0:3 * W], start=True, stop=False,
                                             skip_group_check=True)

                        def project(w, ps, slot, done):
                            for half in range(2):
                                for k in range(KD):
                                    mm = nc.tensor.matmul(ps[:, BLK * half:BLK * half + BLK], x_tile[:, slot, k],
                                                          w[:, k, BLK * half:BLK * half + BLK], start=(k == 0), stop=(k == KD - 1))
                            mm.then_inc(done, 1)

                        def add_tile(n):
                            pe.wait_ge(v_ready, n + 1 + START)
                            pe.wait_ge(k_ready, n + 1 + START)
                            for hp in range(HP):
                                mm = nc.tensor.matmul(pair(hp), k_elu[:, P * hp:P * hp + P], v_one[:, hp], start=False, stop=False,
                                                      skip_group_check=True)
                            mm.then_inc(kv_added, 1)

                        def tile_step(t, slot, turn):
                            n = t + NT * b
                            pe.wait_ge(tile_in[slot], 16 * turn + (NT // 2 * 16 * b + 16) + START)
                            pe.wait_ge(k_raw_ready, n + START)
                            project(wk, k_ps, slot, k_psum_ready)
                            if not isinstance(t, int) or t:
                                add_tile(n - 1)
                            project(wv, v_ps, slot, v_psum_ready)

                        tile_step(0, 0, 0)
                        with pe.Fori(0, NT // 2 - 1) as i:
                            tile_step(2 * i + 1, 1, i)
                            tile_step(2 * i + 2, 0, i + 1)
                        tile_step(NT - 1, 1, NT // 2 - 1)
                        add_tile(NT * b + NT - 1)
                        for j in range(3):
                            mm = nc.tensor.matmul(kv_ps[:, j, 0:3 * W], zeros[:, 0:P], zeros[:, 0:3 * W], start=False, stop=True,
                                                  skip_group_check=True)
                        mm.then_inc(kv_summed, 1)

        def block_pass(b):
            with ExitStack() as cp:
                bank = [cp.enter_context(nc.psum_tensor(f"l0_bank{b}_{j}", [P, BLK], F32)) for j in range(8)]
                q_ps, num_ps, spread_ps, acc = bank[0:2], bank[2:4], bank[4:6], bank[6:8]
                den_ps, h_ps = bank[4], bank[0:4]
                first_mean, first_var, last_mean, last_var = bank[4], bank[5], acc[0], acc[1]

                def every_block(engine, block, last_norms):
                    block(0, NBLK * b, False)
                    with engine.Fori(1, NBLK) as i:
                        block(i, i + NBLK * b, True)
                    for part in range(4):
                        last_norms(NBLK, NBLK * (b + 1), part)

                with nc.Block() as block:
                    @block.tensor
                    def _(pe):
                        def last_norms(i, n, part):
                            if part % 2 == 0:
                                norm.tensor_mean(pe, z, z_ready, 3 * n - 1 + part // 2, last_mean[:])
                            else:
                                norm.tensor_var(pe, 3 * n - 2 + part // 2, last_var[:])

                        def one_block(i, n, tail):
                            for hp in range(HP + 1):
                                if hp < HP:
                                    if hp >= 2:
                                        pe.wait_ge(q_exp_ready, HP * n + (hp - 1) + START)
                                        pe.wait_ge(q_relu_ready, HP * n + (hp - 1) + START)
                                    for k in range(KD):
                                        mm = nc.tensor.matmul(q_ps[hp % 2][:], wq[:, k, P * hp:P * hp + P],
                                                              x[:, k, b, bass.ds(PAD + i * BLK, BLK)], start=(k == 0), stop=(k == KD - 1))
                                    mm.then_inc(q_psum_ready, 1)
                                if tail and hp in (1, 3, 5, 7):
                                    last_norms(i, n, hp // 2)
                                if hp >= 1:
                                    g = hp - 1
                                    pe.wait_ge(q_ready, HP * n + (g + 1) + START)
                                    mm = nc.tensor.matmul(den_ps[0:H, :], ksum[:, g], q_elu[:, g % 2], start=(g == 0), stop=(g == HP - 1))
                                    if g == HP - 1:
                                        mm.then_inc(den_ready, 1)
                                    if g >= 2:
                                        pe.wait_ge(num_copied, HP * n + (g - 1) + START)
                                    nc.tensor.matmul(num_ps[g % 2][:], kv[:, g], q_elu[:, g % 2], start=True, stop=True).then_inc(num_ready, 1)
                            pe.wait_ge(inv_ready, 2 * n + 2 + START)
                            for hp in range(HP + 1):
                                if hp < HP:
                                    if hp >= 2:
                                        pe.wait_ge(o_ready, HP * n + (hp - 1) + START)
                                    nc.tensor.matmul(spread_ps[hp % 2][:], pick[:, hp], den[:], start=True, stop=True).then_inc(spread_ready, 1)
                                if hp >= 1:
                                    if hp == 1 and tail:
                                        pe.wait_ge(norm.done, 3 * n + START)
                                    pe.wait_ge(o_ready, HP * n + hp + START)
                                    for m in range(KD):
                                        mm = nc.tensor.matmul(acc[m][:], wo[:, hp - 1, P * m:P * m + P], o[:, hp - 1], start=(hp == 1), stop=(hp == HP))
                            mm.then_inc(wo_ready, 1)
                            norm.tensor(pe, 3 * n, z, z_ready, 3 * n + 1, first_mean[:], first_var[:])
                            pe.wait_ge(ln1_ready, 2 * n + 2 + START)
                            for m in range(KF):
                                if m >= 4:
                                    pe.wait_ge(hidden_ready, KF * n + (m - 3) + START)
                                for k in range(KD):
                                    mm = nc.tensor.matmul(h_ps[m % 4][:], w1[:, k, P * m:P * m + P], y[:, k], start=(k == 0), stop=(k == KD - 1))
                                mm.then_inc(h_psum_ready, 1)
                            for f in range(KF):
                                pe.wait_ge(hidden_ready, KF * n + (f + 1) + START)
                                for m in range(KD):
                                    mm = nc.tensor.matmul(acc[m][:], w2[:, f, P * m:P * m + P], hidden[:, f], start=(f == 0), stop=(f == KF - 1))
                            mm.then_inc(w2_ready, 1)

                        every_block(pe, one_block, last_norms)

                    @block.scalar
                    def _(act):
                        def last_norms(i, n, part):
                            if part % 2 == 0:
                                norm.scalar_square(act, 3 * n - 2 + part // 2)
                            else:
                                norm.scalar_std(act, 3 * n - 2 + part // 2, last_var[:])

                        def one_block(i, n, tail):
                            for hp in range(HP + 1):
                                if hp < HP:
                                    act.wait_ge(q_psum_ready, HP * n + (hp + 1) + START)
                                    if hp >= 2:
                                        act.wait_ge(q_ready, HP * n + (hp - 1) + START)
                                    nc.scalar.activation(q_exp[:, hp % 2], q_ps[hp % 2][:], ACT.Exp, bias=bq[:, hp:hp + 1]).then_inc(q_exp_ready, 1)
                                    nc.scalar.activation(q_relu[:, hp % 2], q_ps[hp % 2][:], ACT.Relu, bias=bq[:, hp:hp + 1]).then_inc(q_relu_ready, 1)
                                if tail and hp in (1, 3, 5, 7):
                                    last_norms(i, n, hp // 2)
                                if hp >= 1:
                                    act.wait_ge(num_ready, HP * n + hp + START)
                                    nc.scalar.copy(o[:, hp - 1], num_ps[(hp - 1) % 2][:]).then_inc(num_copied, 1)
                            norm.scalar(act, 3 * n, first_var[:])
                            for m in range(KF):
                                act.wait_ge(h_psum_ready, KF * n + (m + 1) + START)
                                nc.scalar.activation(hidden[:, m], h_ps[m % 4][:], ACT.Gelu, bias=b1[:, m:m + 1]).then_inc(hidden_ready, 1)

                        every_block(act, one_block, last_norms)

                    @block.vector
                    def _(dve):
                        def affine(gain, shift, ready):
                            for m in range(KD):
                                nc.vector.tensor_scalar(y[:, m], y[:, m], gain[:, m:m + 1], shift[:, m:m + 1], ALU.mult, ALU.add).then_inc(ready, 1)

                        def second_sum(n):
                            dve.wait_ge(w2_ready, n + START)
                            for m in range(KD):
                                last = nc.vector.scalar_tensor_tensor(z[:, m], acc[m][:], b2[:, m:m + 1], y[:, m], ALU.add, ALU.add)
                            last.then_inc(z_ready, 1)

                        def last_norms(i, n, part):
                            x_before = x[:, :, b, bass.ds(PAD - BLK + i * BLK, BLK)]
                            if part == 0:
                                norm.vector_centre(dve, 3 * n - 2, z, last_mean[:])
                            elif part == 1:
                                norm.vector_out(dve, 3 * n - 2, norm.centre, y[:])
                                dve.wait_ge(norm.done, 3 * n - 1 + START)
                                affine(g2, be2, ln2_ready)
                                dve.wait_ge(ln2_ready, 2 * n + START)
                                nc.vector.tensor_tensor(z[:], y[:], x_before, ALU.add).then_inc(z_ready, 1)
                            elif part == 2:
                                norm.vector_centre(dve, 3 * n - 1, z, last_mean[:])
                            else:
                                norm.vector_out(dve, 3 * n - 1, norm.centre, x_before)
                                dve.wait_ge(norm.done, 3 * n + START)

                        def one_block(i, n, tail):
                            x_block = x[:, :, b, bass.ds(PAD + i * BLK, BLK)]
                            for hp in range(HP):
                                dve.wait_ge(q_exp_ready, HP * n + (hp + 1) + START)
                                dve.wait_ge(q_relu_ready, HP * n + (hp + 1) + START)
                                if hp >= 2:
                                    dve.wait_ge(num_ready, HP * n + (hp - 1) + START)
                                nc.vector.scalar_tensor_tensor(q_elu[:, hp % 2], q_exp[:, hp % 2], 1.0, q_relu[:, hp % 2],
                                                               ALU.min, ALU.add).then_inc(q_ready, 1)
                                if tail and hp in (0, 3, 4, 7):
                                    last_norms(i, n, (0, 3, 4, 7).index(hp))
                            dve.wait_ge(den_ready, n + 1 + START)
                            nc.vector.tensor_scalar(den[:], den_ps[0:H, :], 1e-6, None, ALU.add).then_inc(inv_ready, 1)
                            dve.wait_ge(inv_ready, 2 * n + 1 + START)
                            nc.vector.reciprocal(den[:], den[:]).then_inc(inv_ready, 1)
                            for g in range(HP):
                                dve.wait_ge(num_copied, HP * n + (g + 1) + START)
                                dve.wait_ge(spread_ready, HP * n + (g + 1) + START)
                                nc.vector.tensor_tensor(o[:, g], spread_ps[g % 2][:], o[:, g], ALU.mult).then_inc(o_ready, 1)
                            dve.wait_ge(wo_ready, n + 1 + START)
                            for m in range(KD):
                                last = nc.vector.scalar_tensor_tensor(z[:, m], acc[m][:], bo[:, m:m + 1], x_block[:, m], ALU.add, ALU.add)
                            last.then_inc(z_ready, 1)
                            dve.wait_ge(z_ready, 3 * n + 1 + START)
                            norm.vector(dve, 3 * n, z, y[:], first_mean[:])
                            dve.wait_ge(norm.done, 3 * n + 1 + START)
                            affine(g1, be1, ln1_ready)
                            dve.wait_ge(ln1_ready, 2 * n + 2 + START)
                            second_sum(n + 1)

                        every_block(dve, one_block, last_norms)

        ctx.preset()
        for b in range(NB):
            kv_pass(b)
            block_pass(b)


def experts(nc, io, x, ones):
    NT = NB * T // P
    TB = T // P
    NR = NT + NE
    KE = FE // P
    W = D + NE
    RES = 2 * CH

    def batch_major(t):
        return t[:].rearrange("p k b t -> p k (b t)")

    with Phase(nc) as ctx:
        def sem(name):
            return ctx.semaphore("c_" + name)

        def buffers(scope):
            return lambda name, shape, dtype=F32: scope.enter_context(nc.sbuf_tensor("c_" + name, shape, dtype))

        sb = buffers(ctx)
        ident, place, owner = sb("ident", [P, P]), sb("place", [P, NT], mybir.dt.uint32), sb("owner", [P, NR], mybir.dt.uint32)
        bank = [ctx.enter_context(nc.psum_tensor(f"c_bank{j}", [P, BLK], F32)) for j in range(8)]
        small_in, weights_in, shared_in, zeroed, filled = (sem(n) for n in ("small_in", "weights_in", "shared_in", "zeroed", "filled"))
        scattered, gathered = ctx.semaphore("c_scattered", start=0), [ctx.semaphore(f"c_gathered{b}", start=0) for b in range(NB)]
        tile_copied, tile_turned, row_copied = sem("tile_copied"), sem("tile_turned"), sem("row_copied")
        step, counted, score_ready, scaled = sem("step"), sem("counted"), sem("score_ready"), sem("scaled")
        gate_done, up_done, silu_ready, hidden_ready, down_done, added = (sem(n) for n in ("gate_done", "up_done", "silu_ready", "hidden_ready", "down_done", "added"))
        rows_in, out_stored = [sem("rows_in0"), sem("rows_in1")], [sem("out_stored0"), sem("out_stored1")]
        r_turned, r_copied, r_gate, r_up, r_silu, r_hidden = (sem(n) for n in ("r_turned", "r_copied", "r_gate", "r_up", "r_silu", "r_hidden"))
        r_hid_turned, r_hid_copied, r_down, r_out = (sem(n) for n in ("r_hid_turned", "r_hid_copied", "r_down", "r_out"))
        y_copied, y_turned, z_ready, written, stored, eps_ready = (sem(n) for n in ("y_copied", "y_turned", "z_ready", "written", "stored", "eps_ready"))
        norm = Norm(nc, ctx, "c_norm", ones, buffers=False)
        ctx.preset()
        with ExitStack() as weights:
            ws = buffers(weights)
            wg, wu, wd = ws("gate", [P, NE + 1, KD, FE]), ws("up", [P, NE + 1, KD, FE]), ws("down", [P, NE + 1, KE, D])

            with ExitStack() as scope:
                s1 = buffers(scope)
                router, before, rank = s1("router", [P, KD, NE]), s1("before", [P, P]), s1("rank", [P, NE])
                consts = s1("consts", [P, NE * NT + NE * NT + NR + NE])
                keep = consts[:, 0:NE * NT]
                steps = consts[:, NE * NT:2 * NE * NT].rearrange("p (e t) -> p e t", t=NT)
                tiles = consts[:, 2 * NE * NT:2 * NE * NT + NR]
                one = consts[:, 2 * NE * NT + NR:]
                zeros = s1("zeros", [P, D])
                x_tile, row = s1("x_tile", [P, 2, KD, P]), s1("row", [P, NT, W])
                top, first, score = s1("top", [P, NT]), s1("first", [P, NT]), s1("score", [P, NT])
                hit_te, hit, total = s1("hit_te", [P, NT, NE]), s1("hit", [P, NE, NT]), s1("total", [P, NE, NT])
                cum, over = s1("cum", [P, NE, NT]), s1("over", [P, NE * NR])
                need, ends = s1("need", [P, NE]), s1("ends", [P, NE])
                silu, hidden = s1("silu", [P, 2, BLK]), s1("hidden", [P, KE, BLK])
                PLACED = 18

                with nc.Block() as block:
                    @block.sync
                    def _(sp):
                        for dst, name in ((router, "router"), (ident, "ident"), (before, "c_before"), (rank, "c_rank"), (consts, "c_consts")):
                            sp.dma_start(dst[:], io[name]).then_inc(small_in, 16)
                        for dst, name in ((wg, "expert_gate"), (wu, "expert_up"), (wd, "expert_down")):
                            sp.dma_start(dst[:, NE], io[name][:, NE]).then_inc(shared_in, 16)
                        for e in range(NE):
                            for dst, name in ((wg, "expert_gate"), (wu, "expert_up"), (wd, "expert_down")):
                                sp.dma_start(dst[:, e], io[name][:, e]).then_inc(weights_in, 16)
                        sp.wait_ge(zeroed, 1 + START)
                        sp.dma_start(io["sorted_in"].rearrange("(n p) c -> p n c", p=P),
                                     zeros[:].unsqueeze(1).broadcast_to([P, NR + 1, D])).then_inc(filled, 16)
                        sp.dma_start(io["sorted_out"][0:P, :], zeros[:]).then_inc(filled, 16)
                        sp.wait_ge(weights_in, 16 * 3 * NE + START)

                    @block.gpsimd
                    def _(pool):
                        nc.gpsimd.memset(zeros[:], 0.0).then_inc(zeroed, 1)
                        pool.wait_ge(row_copied, NT + START)
                        pool.wait_ge(score_ready, 1 + START)
                        nc.gpsimd.tensor_tensor(row[:, :, 0:D], row[:, :, 0:D], score[:].unsqueeze(2).broadcast_to([P, NT, D]), ALU.mult).then_inc(scaled, 1)
                        pool.wait_ge(filled, 2 * 16 + START)
                        pool.wait_ge(step, PLACED + START)
                        pool.wait_ge(scaled, 1 + START)
                        for t in range(NT):
                            nc.gpsimd.indirect_dma_start(io["sorted_in"][:, :], bass.IndirectOffsetOnAxis(ap=place[:, t:t + 1], axis=0),
                                                         row[:, t, 0:D], None).then_inc(scattered, 16)
                        pool.wait_ge(scattered, 16 * NT)

                    @block.tensor
                    def _(pe):
                        pe.wait_ge(small_in, 16 * 5 + START)
                        with pe.Fori(0, NT // 2) as i:
                            for slot in range(2):
                                t = 2 * i + slot
                                pe.wait_ge(tile_copied, t + 1 + START)
                                if slot == 0:
                                    pe.wait_ge(row_copied, t + START)
                                for k in range(KD):
                                    nc.tensor.transpose(bank[slot][:, P * k:P * k + P], x_tile[:, slot, k], ident[:])
                                for k in range(KD):
                                    mm = nc.tensor.matmul(bank[slot][:, D:W], x_tile[:, slot, k], router[:, k], start=(k == 0), stop=(k == KD - 1))
                                mm.then_inc(tile_turned, 1)

                        pe.wait_ge(step, 5 + START)
                        nc.tensor.matmul(bank[2][:, 0:NE * NT], before[:], hit[:].rearrange("p e t -> p (e t)"), start=True, stop=True)
                        nc.tensor.matmul(bank[3][:, 0:NE * NT], ones[:], hit[:].rearrange("p e t -> p (e t)"), start=True, stop=True).then_inc(counted, 1)
                        pe.wait_ge(shared_in, 16 * 3 + START)
                        with pe.Fori(0, NB) as b, pe.Fori(0, NBLK) as i:
                            n = i + NBLK * b
                            here = bass.ds(PAD + b * (PAD + T) + i * BLK, BLK)
                            for m in range(KE):
                                c = KE * n + m
                                if m >= 2:
                                    pe.wait_ge(hidden_ready, c - 1 + START)
                                for w, dst, done in ((wg, bank[0:2], gate_done), (wu, bank[4:6], up_done)):
                                    for k in range(KD):
                                        mm = nc.tensor.matmul(dst[m % 2][:], w[:, NE, k, P * m:P * m + P], batch_major(x)[:, k, here],
                                                              start=(k == 0), stop=(k == KD - 1))
                                    mm.then_inc(done, 1)
                            pe.wait_ge(added, n + START)
                            for f in range(KE):
                                pe.wait_ge(hidden_ready, KE * n + (f + 1) + START)
                                for m in range(KD):
                                    mm = nc.tensor.matmul(bank[6 + m][:], wd[:, NE, f, P * m:P * m + P], hidden[:, f], start=(f == 0), stop=(f == KE - 1))
                            mm.then_inc(down_done, 1)

                    @block.scalar
                    def _(act):
                        with act.Fori(0, NT // 2) as i:
                            for slot in range(2):
                                t = 2 * i + slot
                                act.wait_ge(tile_turned, t + 1 + START)
                                nc.scalar.copy(row[:, bass.ds(t, 1)].rearrange("p a c -> p (a c)"), bank[slot][:, 0:W]).then_inc(row_copied, 1)
                        act.wait_ge(step, 1 + START)
                        nc.scalar.activation(score[:], top[:], ACT.Sigmoid).then_inc(score_ready, 1)
                        with act.Fori(0, NB * NBLK) as n:
                            for m in range(KE):
                                c = KE * n + m
                                act.wait_ge(gate_done, c + 1 + START)
                                if m >= 2:
                                    act.wait_ge(hidden_ready, c - 1 + START)
                                nc.scalar.activation(silu[:, m % 2], bank[m % 2][:], ACT.Silu).then_inc(silu_ready, 1)

                    @block.vector
                    def _(dve):
                        with dve.Fori(0, NB) as b, dve.Fori(0, TB // 2) as i:
                            for slot in range(2):
                                t = TB * b + 2 * i + slot
                                if slot == 0:
                                    dve.wait_ge(tile_turned, t + START)
                                nc.vector.tensor_copy(x_tile[:, slot], batch_major(x)[:, :, bass.ds(PAD + b * (PAD + T) + (2 * i + slot) * P, P)]).then_inc(tile_copied, 1)
                        dve.wait_ge(small_in, 16 * 5 + START)
                        dve.wait_ge(row_copied, NT + START)
                        done = [0]

                        def then(op):
                            op.then_inc(step, 1)
                            done[0] += 1
                            dve.wait_ge(step, done[0] + START)

                        def over_tiles(v):
                            return v.unsqueeze(2).broadcast_to([P, NE, NT])

                        logits = row[:, :, D:W]
                        tt, red = nc.vector.tensor_tensor, nc.vector.tensor_reduce
                        then(red(top[:], logits, AX_X, ALU.max))
                        then(tt(hit_te[:], logits, top[:].unsqueeze(2).broadcast_to([P, NT, NE]), ALU.is_equal))
                        then(tt(hit_te[:], hit_te[:], rank[:].unsqueeze(1).broadcast_to([P, NT, NE]), ALU.mult))
                        then(red(first[:], hit_te[:], AX_X, ALU.max))
                        then(tt(hit[:].rearrange("p e t -> p t e"), hit_te[:], first[:].unsqueeze(2).broadcast_to([P, NT, NE]), ALU.is_equal))
                        dve.wait_ge(counted, 1 + START)
                        then(nc.vector.tensor_scalar(total[:].rearrange("p e t -> p (e t)"), bank[3][:, 0:NE * NT], float(D), None, ALU.mult))
                        then(nc.vector.tensor_tensor_scan(cum[:].rearrange("p e t -> p (e t)"), keep, total[:].rearrange("p e t -> p (e t)"), 0.0, ALU.mult, ALU.add))
                        ov = over[:, 0:NE * NT].rearrange("p (e t) -> p e t", t=NT)
                        then(tt(ov, cum[:, :, NT - 1:NT].broadcast_to([P, NE, NT]), steps, ALU.is_gt))
                        then(red(need[:], ov, AX_X, ALU.add))
                        then(nc.vector.tensor_tensor_scan(ends[:], one, need[:], 0.0, ALU.mult, ALU.add))
                        then(tt(cum[:], cum[:], total[:], ALU.subtract))
                        then(tt(cum[:], cum[:], bank[2][:, 0:NE * NT].rearrange("p (e t) -> p e t", t=NT), ALU.add))
                        then(tt(need[:], ends[:], need[:], ALU.subtract))
                        then(nc.vector.tensor_scalar(need[:], need[:], 1.0, float(P), ALU.add, ALU.mult))
                        then(tt(cum[:], cum[:], over_tiles(need[:]), ALU.add))
                        then(tt(cum[:], cum[:], hit[:], ALU.mult))
                        then(red(first[:], cum[:].rearrange("p e t -> p t e"), AX_X, ALU.add))
                        then(nc.vector.tensor_copy(place[:], first[:]))
                        ov = over[:].rearrange("p (n e) -> p n e", e=NE)
                        assert done[0] == PLACED
                        then(tt(ov, ends[:].unsqueeze(1).broadcast_to([P, NR, NE]), tiles.unsqueeze(2).broadcast_to([P, NR, NE]), ALU.is_lt))
                        number = cum[:].rearrange("p e t -> p (e t)")[:, 0:NR]
                        then(red(number, ov, AX_X, ALU.add))
                        then(nc.vector.tensor_scalar(number, number, float(NE - 1), None, ALU.min))
                        then(nc.vector.tensor_copy(owner[:], number))
                        with dve.Fori(0, NB) as b, dve.Fori(0, NBLK) as i:
                            n = i + NBLK * b
                            xb = batch_major(x)[:, :, bass.ds(PAD + b * (PAD + T) + i * BLK, BLK)]
                            for m in range(KE):
                                c = KE * n + m
                                dve.wait_ge(silu_ready, c + 1 + START)
                                dve.wait_ge(up_done, c + 1 + START)
                                if m == 0:
                                    dve.wait_ge(down_done, n + START)
                                nc.vector.tensor_tensor(hidden[:, m], bank[4 + m % 2][:], silu[:, m % 2], ALU.mult).then_inc(hidden_ready, 1)
                            dve.wait_ge(down_done, n + 1 + START)
                            for m in range(KD):
                                last = nc.vector.tensor_tensor(xb[:, m], bank[6 + m][:], xb[:, m], ALU.add)
                            last.then_inc(added, 1)

            with ExitStack() as scope:
                s2 = buffers(scope)
                r_in, r_xT, r_sl = s2("r_in", [P, 2, D]), s2("r_xT", [P, 2, KD, P]), s2("r_sl", [P, 2, FE])
                r_hid, r_hT, r_y = s2("r_hid", [P, 2, FE]), s2("r_hT", [P, 2, KE, P]), s2("r_y", [P, 2, D])
                g_ps, u_ps, y_ps, turn_ps, hid_ps = bank[0:2], bank[2:4], bank[4:6], bank[6], bank[7]
                HR = NR // 2

                with nc.Block() as block:
                    @block.sync
                    def _(sp):
                        for slot in range(2):
                            sp.dma_start(r_in[:, slot], io["sorted_in"][P * slot + P:P * slot + 2 * P, :]).then_inc(rows_in[slot], 16)
                        with sp.Fori(0, HR - 1) as i:
                            for slot in range(2):
                                sp.wait_ge(r_turned, 2 * i + (slot + 1) + START)
                                sp.dma_start(r_in[:, slot], io["sorted_in"][bass.ds((2 * i + slot) * P + 3 * P, P), :]).then_inc(rows_in[slot], 16)

                    @block.tensor
                    def _(pe):
                        def turn(n, slot, i):
                            pe.wait_ge(rows_in[slot], 16 * i + 16 + START)
                            pe.wait_ge(r_copied, n + START)
                            for k in range(KD):
                                mm = nc.tensor.transpose(turn_ps[:, P * k:P * k + P], r_in[:, slot, P * k:P * k + P], ident[:])
                            mm.then_inc(r_turned, 1)

                        def expert(n):
                            at = slice(n, n + 1) if isinstance(n, int) else bass.ds(n, 1)
                            return pe.value_load(owner[0:1, at], min_val=0, max_val=NE - 1)

                        def gate_up(n, slot):
                            e = expert(n)
                            pe.wait_ge(r_copied, n + 1 + START)
                            if not isinstance(n, int) or n >= 2:
                                pe.wait_ge(r_hidden, n - 1 + START)
                            for w, dst, done in ((wg, g_ps, r_gate), (wu, u_ps, r_up)):
                                for k in range(KD):
                                    mm = nc.tensor.matmul(dst[slot][:], r_xT[:, slot, k], w[:, bass.ds(e, 1), k].rearrange("p a f -> p (a f)"),
                                                          start=(k == 0), stop=(k == KD - 1))
                                mm.then_inc(done, 1)

                        def down(n, slot):
                            e = expert(n)
                            pe.wait_ge(r_hidden, n + 1 + START)
                            pe.wait_ge(r_hid_copied, n + START)
                            for f in range(KE):
                                mm = nc.tensor.transpose(hid_ps[:, P * f:P * f + P], r_hid[:, slot, P * f:P * f + P], ident[:])
                            mm.then_inc(r_hid_turned, 1)
                            pe.wait_ge(r_hid_copied, n + 1 + START)
                            pe.wait_ge(r_out, n + START)
                            for f in range(KE):
                                mm = nc.tensor.matmul(y_ps[slot][:, 0:D], r_hT[:, slot, f], wd[:, bass.ds(e, 1), f].rearrange("p a f -> p (a f)"),
                                                      start=(f == 0), stop=(f == KE - 1))
                            mm.then_inc(r_down, 1)

                        turn(0, 0, 0)
                        gate_up(0, 0)
                        turn(1, 1, 0)
                        with pe.Fori(0, HR - 1) as i:
                            gate_up(2 * i + 1, 1)
                            turn(2 * i + 2, 0, i + 1)
                            down(2 * i, 0)
                            gate_up(2 * i + 2, 0)
                            turn(2 * i + 3, 1, i + 1)
                            down(2 * i + 1, 1)
                        gate_up(NR - 1, 1)
                        down(NR - 2, 0)
                        down(NR - 1, 1)

                    @block.scalar
                    def _(act):
                        def copy_rows(n, slot):
                            act.wait_ge(r_turned, n + 1 + START)
                            if not isinstance(n, int) or n >= 2:
                                act.wait_ge(r_up, n - 1 + START)
                            nc.scalar.copy(r_xT[:, slot], turn_ps[:, 0:D].rearrange("p (k t) -> p k t", k=KD)).then_inc(r_copied, 1)

                        def gate(n, slot):
                            act.wait_ge(r_gate, n + 1 + START)
                            if not isinstance(n, int) or n >= 2:
                                act.wait_ge(r_hidden, n - 1 + START)
                            nc.scalar.activation(r_sl[:, slot], g_ps[slot][:], ACT.Silu).then_inc(r_silu, 1)

                        def out(n, slot, i):
                            act.wait_ge(r_down, n + 1 + START)
                            act.wait_ge(out_stored[slot], 16 * i + START)
                            nc.scalar.copy(r_y[:, slot], y_ps[slot][:, 0:D]).then_inc(r_out, 1)
                            place = bass.ds(n * P + P, P) if not isinstance(n, int) else slice(n * P + P, n * P + 2 * P)
                            act.wait_ge(r_out, n + 1 + START)
                            nc.scalar.dma_start(io["sorted_out"][place, :], r_y[:, slot]).then_inc(out_stored[slot], 16)

                        copy_rows(0, 0)
                        gate(0, 0)
                        copy_rows(1, 1)
                        with act.Fori(0, HR - 1) as i:
                            gate(2 * i + 1, 1)
                            copy_rows(2 * i + 2, 0)
                            out(2 * i, 0, i)
                            gate(2 * i + 2, 0)
                            copy_rows(2 * i + 3, 1)
                            out(2 * i + 1, 1, i)
                        gate(NR - 1, 1)
                        out(NR - 2, 0, HR - 1)
                        out(NR - 1, 1, HR - 1)
                        for slot in range(2):
                            act.wait_ge(out_stored[slot], 16 * HR + START)

                    @block.vector
                    def _(dve):
                        def product(n, slot):
                            dve.wait_ge(r_silu, n + 1 + START)
                            dve.wait_ge(r_up, n + 1 + START)
                            if not isinstance(n, int) or n >= 2:
                                dve.wait_ge(r_hid_turned, n - 1 + START)
                            nc.vector.tensor_tensor(r_hid[:, slot], r_sl[:, slot], u_ps[slot][:], ALU.mult).then_inc(r_hidden, 1)

                        def turned(n, slot):
                            dve.wait_ge(r_hid_turned, n + 1 + START)
                            if not isinstance(n, int) or n >= 2:
                                dve.wait_ge(r_down, n + START)
                            nc.vector.tensor_copy(r_hT[:, slot], hid_ps[:].rearrange("p (k t) -> p k t", k=KE)).then_inc(r_hid_copied, 1)

                        product(0, 0)
                        with dve.Fori(0, HR - 1) as i:
                            product(2 * i + 1, 1)
                            turned(2 * i, 0)
                            product(2 * i + 2, 0)
                            turned(2 * i + 1, 1)
                        product(NR - 1, 1)
                        turned(NR - 2, 0)
                        turned(NR - 1, 1)

        with ExitStack() as scope:
            s3 = buffers(scope)
            norm.allocate(scope)
            back, tile = s3("back", [P, NT, D]), s3("back_tile", [P, 4, D])
            z, y = s3("z", [P, KD, BLK]), s3("y", [P, KD, BLK])
            with nc.Block() as block:
                @block.gpsimd
                def _(pool):
                    nc.gpsimd.memset(norm.eps[:], 1e-5).then_inc(eps_ready, 1)
                    for t in range(NT):
                        nc.gpsimd.indirect_dma_start(back[:, t], None, io["sorted_out"][:, :],
                                                     bass.IndirectOffsetOnAxis(ap=place[:, t:t + 1], axis=0)).then_inc(gathered[t // TB], 16)

                @block.sync
                def _(sp):
                    with sp.Fori(0, NB * NBLK) as n:
                        sp.wait_ge(written, n + 1 + START)
                        sp.dma_start(io["x2"][:, :, bass.ds(RES + n * BLK, BLK)], y[:]).then_inc(stored, 16)
                    for edge in (0, RES + NB * T):
                        sp.dma_start(io["x2"][:, :, edge:edge + 2 * CH], y[:, :, 0:2 * CH]).then_inc(stored, 16)
                    sp.wait_ge(stored, 16 * (NB * NBLK + 2) + START)

                @block.tensor
                def _(pe):
                    with pe.Fori(0, NB * NBLK) as n:
                        pe.wait_ge(y_copied, n + 1 + START)
                        pe.wait_ge(z_ready, n + START)
                        for m in range(KD):
                            for t in range(4):
                                mm = nc.tensor.transpose(bank[m][:, P * t:P * t + P], tile[:, t, P * m:P * m + P], ident[:])
                        mm.then_inc(y_turned, 1)
                        norm.tensor(pe, n, z, z_ready, n + 1, bank[2][:], bank[3][:])

                @block.scalar
                def _(act):
                    act.wait_ge(eps_ready, 1 + START)
                    for b in range(NB):
                        act.wait_ge(gathered[b], 16 * TB)
                        with act.Fori(0, NBLK) as i:
                            n = i + NBLK * b
                            act.wait_ge(y_turned, n + START)
                            nc.scalar.copy(tile[:], back[:, bass.ds(4 * i + TB * b, 4)]).then_inc(y_copied, 1)
                            norm.scalar(act, n, bank[3][:])

                @block.vector
                def _(dve):
                    with dve.Fori(0, NB) as b, dve.Fori(0, NBLK) as i:
                        n = i + NBLK * b
                        xb = batch_major(x)[:, :, bass.ds(PAD + b * (PAD + T) + i * BLK, BLK)]
                        dve.wait_ge(y_turned, n + 1 + START)
                        for m in range(KD):
                            last = nc.vector.tensor_tensor(z[:, m], bank[m][:], xb[:, m], ALU.add)
                        last.then_inc(z_ready, 1)
                        dve.wait_ge(z_ready, n + 1 + START)
                        dve.wait_ge(stored, 16 * n + START)
                        norm.vector(dve, n, z, y[:], bank[2][:])
                        dve.wait_ge(norm.done, n + 1 + START)
                        dve.sem_inc(written, 1)


def delta_rule(nc, io, ones):
    CB = 2
    TB = CB * CH
    NT = T // TB
    NBLOCKS = NB * NT
    G4 = HP // 2
    LEVELS = (32, 16, 8)
    LIMIT = float(np.exp(12.0))

    with Phase(nc) as ctx:
        def sem(name):
            return ctx.semaphore("d_" + name)

        def sb(name, shape):
            return ctx.enter_context(nc.sbuf_tensor("d_" + name, shape, F32))

        wq, wk, wv, wa = (sb(w, [P, KD, FF]) for w in ("wq", "wk", "wv", "wa"))
        wb, u1, u2 = sb("wb", [P, KD, H]), sb("u1", [P, KD, DH]), sb("u2", [DH, D])
        wo, head_norm = sb("wo", [P, HP, D]), sb("head_norm", [P, HP])
        cols = sb("cols", [P, 2 + 8 + 2 + 8 + 2 + 1 + 1])
        norm_w, conv_w, conv_b, a_b = cols[:, 0:2], cols[:, 2:10], cols[:, 10:12], cols[:, 12:20]
        u2_b, u1_b, b_b = cols[:, 20:22], cols[0:DH, 22:23], cols[0:H, 23:24]
        pick = sb("pick", [H, HP, P])
        gather = sb("gather", [P, HP, H])
        ident = sb("ident", [P, P])
        masks = sb("masks", [P, 6, 2, CH])
        q_masks = sb("q_masks", [P, 3, CH])
        carry_on = sb("carry_on", [P, HP * CH])
        goes_on = sb("goes_on", [P, NBLOCKS + 1])
        eps = sb("eps", [P, 2])

        xb, x_res = sb("xb", [P, KD, TB]), sb("x_res", [P, KD, TB])
        std = sb("std", [P, TB])
        hn, h = sb("hn", [P, KD, 3 + TB]), sb("h", [P, KD, TB])
        square, conv = h, h
        rows = sb("rows", [H, 3, TB])
        yT = sb("yT", [P, HP // 2, 2, TB])
        u_hid = sb("u_hid", [DH, TB])
        q2, k2, kb2, n2, v2_ = ([sb(f"{w}{j}", [P, CB, HP, CH]) for j in range(2)] for w in ("q", "k", "kb", "n", "v"))
        gate2 = [sb(f"gate{j}", [P, KD, TB]) for j in range(2)]
        ex = sb("ex", [P, 5, G4, CH])
        exs = sb("exs", [P, 2, 2, G4, CH])
        g_last = sb("g_last", [P, CB, 2, G4])
        lhs = sb("lhs", [P, 2, 4, G4, P])
        rhs = sb("rhs", [P, 2, 4, G4, 2, CH])
        kG, qG, kH = sb("kG", [P, 2, G4, P]), sb("qG", [P, 2, G4, P]), sb("kH", [P, 2, G4, P])
        U = sb("U", [P, 2, 6, G4, P])
        Tm, V, Y = sb("Tm", [P, 2, G4, P]), sb("V", [P, 2, G4, P]), sb("Y", [P, 2, G4, P])
        QK = U[:, :, 0]
        B, W, S = (sb(w, [P, 2, G4 + 1, CH]) for w in ("B", "W", "S"))
        yn = sb("yn", [P, 2, G4, CH])
        ss = sb("ss", [P, 2, G4])
        qk_part = [rhs[:, :, 3, :, 0], rhs[:, :, 3, :, 1], yn]
        bank = [[ctx.enter_context(nc.psum_tensor(f"d_bank{g}{j}", [P, BLK], F32)) for j in range(3)] for g in range(2)]
        f0, f1 = (ctx.enter_context(nc.psum_tensor(f"d_f{j}", [P, BLK], F32)) for j in range(2))

        once = """weights_in cleared wo_scaled x_in res_in square var std rstd head hn conv_a h k_ps q_ps a_ps b_ps v_ps z_sum a_exp
            a_min a_log n raw sq sum_ps norms norm_inv k_ready q_ready kb_ready b_rows spread_k spread_q spread_b v_ready
            out_ps u1_ps u_hid u2_ps gate_ready gated stored reset yt_ps yt_sb""".split()
        of_groups = """pool_d ex_neg exps lvl_in state_in prod u_ready qk_part y_ps y_sb dt_ps dv_ps t_sb v_ps2 v_sb v2 vd_sb kt_ps kt_sb r_ps b_sb
            w_ps w_sb o_ps s_ps s_mul s_sb ysq ss y_std ss_inv yn""".split()
        s = {name: sem(name) for name in once}
        s |= {name: (sem(name + "0"), sem(name + "1")) for name in of_groups}
        N_CLEARED, N_WEIGHTS = 16, 17

        def pairs(t):
            return t[:].rearrange("p (h c) -> p h c", h=G4)

        def few(t):
            return pairs(t)[:, :, 0:CH]

        def by_chunk(t, half):
            return t[:, :, G4 * half:G4 * half + G4].rearrange("p c h t -> p h c t")

        def projected(t):
            return t[:].rearrange("p (h c t) -> p h c t", h=G4, c=CB)

        def flat(t):
            return t[:].rearrange("p c h t -> p (c h t)")

        ctx.preset()
        with nc.Block() as block:
            @block.sync
            def _(sp):
                for dst, name in ((cols, "d_cols"), (wa, "d_wa"), (wk, "d_wk"), (wq, "d_wq"), (wv, "d_wv"), (wb, "d_wb"), (pick, "d_pick"),
                                  (gather, "d_gather"), (ident, "ident"), (masks, "d_masks"), (q_masks, "d_q_masks"), (wo, "d_wo"),
                                  (head_norm, "d_head_norm"), (u1, "d_u1"), (u2, "d_u2"), (carry_on, "d_carry_on"), (goes_on, "d_goes_on")):
                    sp.dma_start(dst[:], io[name]).then_inc(s["weights_in"], 16)

                def store(n, place):
                    sp.wait_ge(s["gated"], 2 * n + 2 + START)
                    sp.dma_start(io["mid"][:, :, place], x_res[:]).then_inc(s["stored"], 16)

                sp.dma_start(xb[:], io["x2"][:, :, TB:2 * TB]).then_inc(s["x_in"], 16)
                sp.dma_start(x_res[:], io["x2"][:, :, 0:TB]).then_inc(s["res_in"], 16)
                with sp.Fori(0, NBLOCKS) as n:
                    here, after = bass.ds(n * TB + TB, TB), bass.ds(n * TB + 2 * TB, TB)
                    sp.wait_ge(s["hn"], n + 1 + START)
                    sp.wait_ge(s["u1_ps"], n + 1 + START)
                    sp.dma_start(xb[:], io["x2"][:, :, after]).then_inc(s["x_in"], 16)
                    store(n, here)
                    sp.wait_ge(s["stored"], 16 * n + 16 + START)
                    sp.dma_start(x_res[:], io["x2"][:, :, here]).then_inc(s["res_in"], 16)
                store(NBLOCKS, bass.ds(NBLOCKS * TB + TB, TB))
                sp.wait_ge(s["stored"], 16 * (NBLOCKS + 1) + START)

            @block.gpsimd
            def _(pool):
                for t in (lhs, rhs, kG, qG, kH, B, W, yT, hn, gate2[1], yn):
                    nc.gpsimd.memset(t[:], 0.0).then_inc(s["cleared"], 1)
                nc.gpsimd.memset(eps[:, 0:1], 1e-6).then_inc(s["cleared"], 1)
                nc.gpsimd.memset(eps[:, 1:2], 0.0).then_inc(s["cleared"], 1)
                nc.gpsimd.memset(u_hid[:], 0.0).then_inc(s["cleared"], 1)
                nc.gpsimd.memset(ss[:], 0.0).then_inc(s["cleared"], 1)
                nc.gpsimd.memset(std[:], 0.0).then_inc(s["cleared"], 1)
                pool.wait_ge(s["cleared"], N_CLEARED + START)
                pool.wait_ge(s["weights_in"], 16 * N_WEIGHTS + START)

                def squares(m, p):
                    pool.wait_ge(s["raw"], 4 * m + 4 + START)
                    nc.gpsimd.tensor_tensor(kb2[p][:], k2[p][:], k2[p][:], ALU.mult).then_inc(s["sq"], 1)
                    nc.gpsimd.tensor_tensor(v2_[p][:], q2[p][:], q2[p][:], ALU.mult).then_inc(s["sq"], 1)

                def exponents(u, m, p, c, g):
                    hs = slice(G4 * g, G4 * g + G4)
                    if c == 0:
                        pool.wait_ge(s["n"], 2 * m + 2 + START)
                    pool.wait_ge(s["lvl_in"][1 - g], u + g + START)
                    nn = n2[p][:, c, hs].rearrange("p h t -> p (h t)")
                    for l, half in enumerate(LEVELS):
                        nv = nn.rearrange("p (m u t) -> p m u t", u=2, t=half)
                        ev = ex[:, l].rearrange("p h t -> p (h t)").rearrange("p (m u t) -> p m u t", u=2, t=half)
                        mid_n = nv[:, :, 0, half - 1:half].broadcast_to([P, G4 * CH // (2 * half), half])
                        nc.gpsimd.tensor_tensor(ev[:, :, 0], nv[:, :, 0], mid_n, ALU.subtract)
                        nc.gpsimd.tensor_tensor(ev[:, :, 1], mid_n, nv[:, :, 1], ALU.subtract)
                    nv = nn.rearrange("p (m t) -> p m t", t=CH)
                    nc.gpsimd.tensor_tensor(exs[:, g, 0], nv, nv[:, :, CH - 1:CH].broadcast_to([P, G4, CH]), ALU.subtract)
                    nv = nn.rearrange("p (m t) -> p m t", t=8)
                    nc.gpsimd.tensor_tensor(ex[:, 3].rearrange("p h t -> p (h t)").rearrange("p (m t) -> p m t", t=8),
                                            nv[:, :, 3:4].broadcast_to([P, G4 * 8, 8]), nv, ALU.subtract).then_inc(s["pool_d"][g], 1)

                def state_factors(u, m, p, c, g):
                    hs = slice(G4 * g, G4 * g + G4)
                    pool.wait_ge(s["kb_ready"], 2 * m + 2 + START)
                    pool.wait_ge(s["exps"][g], u + 1 + START)
                    pool.wait_ge(s["s_ps"][g], u + START)
                    parts = [(dst, src, l, head) for head in range(2) for dst, src, l in ((kG, k2, 1), (qG, q2, 1), (kH, kb2, 0))]
                    for j, (dst, src, l, head) in enumerate(parts):
                        r = slice(DH * head, DH * head + DH)
                        nc.gpsimd.tensor_tensor(dst[r, g, :, r], src[p][r, c, hs], exs[r, g, l], ALU.mult).then_inc(s["state_in"][g], 1)
                        pool.wait_ge(s["state_in"][g], 6 * u + (j + 1) + START)

                squares(0, 0)
                exponents(0, 0, 0, 0, 0)
                exponents(0, 0, 0, 0, 1)
                with pool.Fori(0, NBLOCKS // 2) as i:
                    for p in range(2):
                        n = 2 * i + p
                        for c in range(CB):
                            u = n * CB + c
                            for g in range(2):
                                pool.wait_ge(s["u_ready"][g], 6 * u + 1 + START)
                                nc.gpsimd.tensor_tensor(V[:, g], ident[:].unsqueeze(1).broadcast_to([P, G4, P]), U[:, g, 0], ALU.subtract).then_inc(s["v2"][g], 1)
                            for g in range(2):
                                state_factors(u, n, p, c, g)
                            for g in range(2):
                                if c == 0:
                                    exponents(u + 1, n, p, 1, g)
                                else:
                                    exponents(u + 1, n + 1, 1 - p, 0, g)
                            for g in range(2):
                                pool.wait_ge(s["o_ps"][g], u + 1 + START)
                                nc.gpsimd.tensor_tensor(S[:, g, 0:G4], S[:, g, 0:G4], g_last[:, c, g].unsqueeze(2).broadcast_to([P, G4, CH]),
                                                        ALU.mult).then_inc(s["s_mul"][g], 1)
                            if c == 0:
                                squares(n + 1, 1 - p)

            @block.scalar
            def _(act):
                act.wait_ge(s["cleared"], N_CLEARED + START)
                act.wait_ge(s["weights_in"], 16 * N_WEIGHTS + START)

                def x_squares(m):
                    act.wait_ge(s["x_in"], 16 * m + 16 + START)
                    act.wait_ge(s["v_ps"], 2 * m + START)
                    nc.scalar.activation(square[:], xb[:], ACT.Square).then_inc(s["square"], 1)

                def x_std(m):
                    act.wait_ge(s["var"], m + 1 + START)
                    act.wait_ge(s["u1_ps"], m + 1 + START)
                    nc.scalar.activation(std[:], f1[:, 0:TB], ACT.Sqrt, bias=eps[:, 0:1]).then_inc(s["std"], 1)

                def gate_hidden(m):
                    act.wait_ge(s["u1_ps"], m + 1 + START)
                    nc.scalar.activation(u_hid[:], f1[0:DH, TB:2 * TB], ACT.Silu, bias=u1_b).then_inc(s["u_hid"], 1)

                def conv_silu(m):
                    act.wait_ge(s["conv_a"], m + 1 + START)
                    for kk in range(KD):
                        last = nc.scalar.activation(h[:, kk], conv[:, kk], ACT.Silu, bias=conv_b[:, kk:kk + 1])
                    last.then_inc(s["h"], 1)

                def gates(m, p):
                    act.wait_ge(s["u2_ps"], m + 1 + START)
                    for kk in range(KD):
                        last = nc.scalar.activation(gate2[p][:, kk], f0[:, TB * kk:TB * kk + TB], ACT.Sigmoid, bias=u2_b[:, kk:kk + 1])
                    last.then_inc(s["gate_ready"], 1)

                def decay_exp(m, p):
                    act.wait_ge(s["z_sum"], 2 * m + 2 + START)
                    nc.scalar.activation(n2[p][:], n2[p][:], ACT.Exp, scale=-1.0).then_inc(s["a_exp"], 1)

                def decay_log(m, p):
                    act.wait_ge(s["a_min"], m + 1 + START)
                    nc.scalar.activation(n2[p][:], n2[p][:], ACT.Ln, bias=1.0).then_inc(s["a_log"], 1)

                def raw(m, dst, ready):
                    for half in range(2):
                        act.wait_ge(s[ready], 2 * m + (half + 1) + START)
                        nc.scalar.copy(by_chunk(dst, half), projected([f0, f1][half])).then_inc(s["raw"], 1)

                def betas(m):
                    act.wait_ge(s["b_ps"], m + 1 + START)
                    nc.scalar.activation(rows[:, 2], f0[0:H, 0:TB], ACT.Sigmoid, bias=b_b).then_inc(s["b_rows"], 1)

                def norms(m):
                    act.wait_ge(s["sum_ps"], m + 1 + START)
                    nc.scalar.activation(rows[:, 0:2], f1[0:H, 0:2 * TB].rearrange("p (a t) -> p a t", a=2), ACT.Sqrt, bias=eps[0:H, 1:2]).then_inc(s["norms"], 1)

                def values(m, p):
                    for c in range(CB):
                        act.wait_ge(s["v_ps"], 2 * m + (c + 1) + START)
                        nc.scalar.copy(v2_[p][:, c], [f0, f1][c][:].rearrange("p (h t) -> p h t", h=HP)).then_inc(s["v_ready"], 1)

                def exponentials(u, p, c, g):
                    hs = slice(G4 * g, G4 * g + G4)
                    act.wait_ge(s["pool_d"][g], u + 1 + START)
                    nc.scalar.activation(ex[:, 4], ex[:, 3], ACT.Exp, scale=-1.0).then_inc(s["ex_neg"][g], 1)
                    nc.scalar.activation(ex[:, 0:3], ex[:, 0:3], ACT.Exp)
                    nc.scalar.activation(exs[:, g, 0], exs[:, g, 0], ACT.Exp)
                    act.wait_ge(s["ex_neg"][g], u + 1 + START)
                    nc.scalar.activation(ex[:, 3], ex[:, 3], ACT.Exp)
                    nc.scalar.activation(exs[:, g, 1], n2[p][:, c, hs], ACT.Exp, scale=-1.0).then_inc(s["exps"][g], 1)

                x_squares(0)
                x_std(0)
                gate_hidden(0)
                gates(0, 0)
                conv_silu(0)
                decay_exp(0, 0)
                raw(0, k2[0], "k_ps")
                raw(0, q2[0], "q_ps")
                decay_log(0, 0)
                betas(0)
                norms(0)
                values(0, 0)
                exponentials(0, 0, 0, 0)
                exponentials(0, 0, 0, 1)
                with act.Fori(0, NBLOCKS // 2) as i:
                    for p in range(2):
                        n = 2 * i + p
                        m = n + 1
                        for c in range(CB):
                            u = n * CB + c
                            if c == 0:
                                x_squares(m)
                            for j in range(1, 6):
                                for g in range(2):
                                    act.wait_ge(s["y_ps"][g], 6 * u + (j + 1) + START)
                                    nc.scalar.copy(Y[:, g], pairs(bank[g][1])).then_inc(s["y_sb"][g], 1)
                                if c == 0:
                                    if j == 1:
                                        x_std(m)
                                        gate_hidden(m)
                                        exponentials(u + 1, p, 1, 0)
                                    if j == 2:
                                        conv_silu(m)
                                        gates(m, 1 - p)
                                    if j == 3:
                                        exponentials(u + 1, p, 1, 1)
                                    if j == 4:
                                        decay_exp(m, 1 - p)
                                        raw(m, k2[1 - p], "k_ps")
                                    if j == 5:
                                        raw(m, q2[1 - p], "q_ps")
                                        decay_log(m, 1 - p)
                                else:
                                    if j == 1:
                                        betas(m)
                                        norms(m)
                                    if j == 4:
                                        exponentials(u + 1, 1 - p, 0, 0)
                                    if j == 5:
                                        values(m, 1 - p)
                                for g in range(2):
                                    if j < 5:
                                        act.wait_ge(s["v_ps2"][g], 4 * u + j + START)
                                        nc.scalar.copy(V[:, g], pairs(bank[g][2])).then_inc(s["v_sb"][g], 1)
                            for g in range(2):
                                act.wait_ge(s["kt_ps"][g], u + 1 + START)
                                nc.scalar.copy(kH[:, g], pairs(bank[g][0])).then_inc(s["kt_sb"][g], 1)
                            for g in range(2):
                                act.wait_ge(s["w_ps"][g], u + 1 + START)
                                nc.scalar.copy(W[:, g, 0:G4], few(bank[g][0])).then_inc(s["w_sb"][g], 1)
                            if c == 1:
                                exponentials(u + 1, 1 - p, 0, 1)
                            for g in range(2):
                                act.wait_ge(s["o_ps"][g], u + 1 + START)
                                nc.scalar.activation(yn[:, g], few(bank[g][2]), ACT.Square).then_inc(s["ysq"][g], 1)
                            for g in range(2):
                                act.wait_ge(s["ss"][g], u + 1 + START)
                                nc.scalar.activation(ss[:, g], ss[:, g], ACT.Sqrt, scale=1.0 / DH, bias=eps[:, 0:1]).then_inc(s["y_std"][g], 1)

            @block.vector
            def _(dve):
                dve.wait_ge(s["cleared"], N_CLEARED + START)
                dve.wait_ge(s["weights_in"], 16 * N_WEIGHTS + START)
                nc.vector.tensor_tensor(wo[:], wo[:], head_norm[:].unsqueeze(2).broadcast_to([P, HP, D]), ALU.mult).then_inc(s["wo_scaled"], 1)

                def norm_and_conv(m):
                    nc.vector.tensor_scalar(hn[:, :, 0:3], hn[:, :, TB:TB + 3], goes_on[:, bass.ds(m, 1)], None, ALU.mult).then_inc(s["head"], 1)
                    dve.wait_ge(s["std"], m + 1 + START)
                    nc.vector.reciprocal(std[:], std[:]).then_inc(s["rstd"], 1)
                    dve.wait_ge(s["rstd"], m + 1 + START)
                    dve.wait_ge(s["head"], 4 * m + 1 + START)
                    for kk in range(KD):
                        last = nc.vector.scalar_tensor_tensor(hn[:, kk, 3:], xb[:, kk], norm_w[:, kk:kk + 1], std[:], ALU.mult, ALU.mult)
                    last.then_inc(s["hn"], 1)
                    dve.wait_ge(s["hn"], m + 1 + START)
                    for tap in range(4):
                        for kk in range(KD):
                            w = conv_w[:, 4 * kk + tap:4 * kk + tap + 1]
                            if tap == 0:
                                last = nc.vector.tensor_scalar(conv[:, kk], hn[:, kk, 0:TB], w, None, ALU.mult)
                            else:
                                last = nc.vector.scalar_tensor_tensor(conv[:, kk], hn[:, kk, tap:tap + TB], w, conv[:, kk], ALU.mult, ALU.add)
                        last.then_inc(s["head" if tap < 3 else "conv_a"], 1)
                        if tap < 3:
                            dve.wait_ge(s["head"], 4 * m + (tap + 2) + START)
                    dve.wait_ge(s["conv_a"], m + 1 + START)

                def decay_logits(m, p):
                    for half in range(2):
                        dve.wait_ge(s["a_ps"], 2 * m + (half + 1) + START)
                        nc.vector.tensor_tensor(by_chunk(n2[p], half), projected([f0, f1][half]),
                                                a_b[:, G4 * half:G4 * half + G4].unsqueeze(2).unsqueeze(3).broadcast_to([P, G4, CB, CH]), ALU.add).then_inc(s["z_sum"], 1)

                def decay_min(m, p):
                    dve.wait_ge(s["a_exp"], m + 1 + START)
                    nc.vector.tensor_scalar(n2[p][:], n2[p][:], LIMIT, None, ALU.min).then_inc(s["a_min"], 1)

                def decay_sum(m, p):
                    dve.wait_ge(s["a_log"], m + 1 + START)
                    for c in range(CB):
                        part = n2[p][:, c].rearrange("p h t -> p (h t)")
                        nc.vector.tensor_tensor_scan(part, carry_on[:], part, 0.0, ALU.mult, ALU.add).then_inc(s["n"], 1)

                def norm_rows(m):
                    dve.wait_ge(s["norms"], m + 1 + START)
                    nc.vector.tensor_scalar(rows[:, 0:2], rows[:, 0:2], 1e-6, None, ALU.add).then_inc(s["norm_inv"], 1)
                    dve.wait_ge(s["norm_inv"], 2 * m + 1 + START)
                    nc.vector.reciprocal(rows[:, 0:2], rows[:, 0:2]).then_inc(s["norm_inv"], 1)

                def scaled(m, dst, src, spread, done):
                    for half in range(2):
                        dve.wait_ge(s[spread], 2 * m + (half + 1) + START)
                        nc.vector.tensor_tensor(by_chunk(dst, half), by_chunk(src, half), projected([f0, f1][half]), ALU.mult).then_inc(s[done], 1)
                    dve.wait_ge(s[done], 2 * m + 2 + START)

                def level_factors(u, p, c, g):
                    hs = slice(G4 * g, G4 * g + G4)
                    k, q, kb = k2[p], q2[p], kb2[p]
                    dve.wait_ge(s["exps"][g], u + 1 + START)
                    dve.wait_ge(s["qk_part"][g], 5 * u + START)
                    for l, half in enumerate(LEVELS):
                        def lv(t):
                            return t.rearrange("p h (m u t) -> p h m u t", u=2, t=half)
                        e = lv(ex[:, l])
                        for j, t in ((0, k), (1, q)):
                            nc.vector.tensor_tensor(lv(rhs[:, g, l, :, j])[:, :, :, 1], lv(t[:, c, hs])[:, :, :, 1], e[:, :, :, 1], ALU.mult)
                        for head in range(2):
                            r = slice(DH * head, DH * head + DH)
                            nc.vector.tensor_tensor(lv(lhs[r, g, l, :, r])[:, :, :, 0], lv(kb[r, c, hs])[:, :, :, 0], e[r, :, :, 0], ALU.mult)
                    for j, t in ((0, k), (1, q)):
                        nc.vector.tensor_tensor(rhs[:, g, 3, :, j], t[:, c, hs], ex[:, 3], ALU.mult)
                    for head in range(2):
                        r = slice(DH * head, DH * head + DH)
                        nc.vector.tensor_tensor(lhs[r, g, 3, :, r], kb[r, c, hs], ex[r, 4], ALU.mult)
                    nc.vector.tensor_copy(g_last[:, c, g], exs[:, g, 1, :, CH - 1]).then_inc(s["lvl_in"][g], 1)

                def q_side(bk):
                    return bk[:].rearrange("p (h a t) -> p h a t", h=G4, a=2)[:, :, 1]

                def masked(g, j, m):
                    src = bank[g][j][:].rearrange("p (h a t) -> p h a t", h=G4, a=2)[:, :, 0].unsqueeze(2).broadcast_to([P, G4, 2, CH])
                    dst = U[:, g, m].rearrange("p h (a t) -> p h a t", a=2)
                    return nc.vector.tensor_tensor(dst, src, masks[:, m].unsqueeze(1).broadcast_to([P, G4, 2, CH]), ALU.mult)

                def products(u, g, j):
                    dve.wait_ge(s["prod"][g], 4 * u + (j + 1) + START)
                    for m in ((0, 1, 2), (3,), (4,))[j]:
                        masked(g, j, m).then_inc(s["u_ready"][g], 1)
                    nc.vector.tensor_tensor(qk_part[j][:, g], q_side(bank[g][j]), q_masks[:, j].unsqueeze(1).broadcast_to([P, G4, CH]),
                                            ALU.mult).then_inc(s["qk_part"][g], 1)

                def first_inverse(u, g):
                    dve.wait_ge(s["y_ps"][g], 6 * u + 1 + START)
                    nc.vector.tensor_tensor(Tm[:, g], ident[:].unsqueeze(1).broadcast_to([P, G4, P]), pairs(bank[g][1]), ALU.subtract).then_inc(s["t_sb"][g], 1)
                    dve.wait_ge(s["prod"][g], 4 * u + 4 + START)
                    masked(g, 0, 5)
                    dve.wait_ge(s["qk_part"][g], 5 * u + 3 + START)
                    nc.vector.tensor_tensor(qk_part[2][:, g], q_side(bank[g][0]), qk_part[2][:, g], ALU.add).then_inc(s["u_ready"][g], 1)

                def put_qk_together(u, g):
                    nc.vector.tensor_tensor(qk_part[1][:, g], qk_part[1][:, g], qk_part[0][:, g], ALU.add).then_inc(s["qk_part"][g], 1)
                    dve.wait_ge(s["v2"][g], u + 1 + START)
                    dve.wait_ge(s["qk_part"][g], 5 * u + 4 + START)
                    dve.wait_ge(s["u_ready"][g], 6 * u + 6 + START)
                    for head in range(2):
                        r = slice(DH * head, DH * head + DH)
                        last = nc.vector.tensor_tensor(QK[r, g, :, r], qk_part[1][r, g], qk_part[2][r, g], ALU.add)
                    last.then_inc(s["qk_part"][g], 1)

                def turned_out(u, c):
                    dve.wait_ge(s["yt_ps"], u + 1 + START)
                    nc.vector.tensor_copy(yT[:, :, :, CH * c:CH * c + CH], f1[:].rearrange("p (a h t) -> p a h t", a=HP // 2, h=2)).then_inc(s["yt_sb"], 1)

                def finish(n, p):
                    dve.wait_ge(s["out_ps"], n + 1 + START)
                    dve.wait_ge(s["gate_ready"], n + START)
                    nc.vector.tensor_tensor(gate2[1 - p][:], f0[:, 0:KD * TB].rearrange("p (k t) -> p k t", k=KD), gate2[1 - p][:], ALU.mult).then_inc(s["gated"], 1)
                    dve.wait_ge(s["gated"], 2 * n + 1 + START)
                    dve.wait_ge(s["res_in"], 16 * n + 16 + START)
                    nc.vector.tensor_tensor(x_res[:], x_res[:], gate2[1 - p][:], ALU.add).then_inc(s["gated"], 1)

                norm_and_conv(0)
                decay_logits(0, 0)
                decay_min(0, 0)
                decay_sum(0, 0)
                norm_rows(0)
                scaled(0, k2[0], k2[0], "spread_k", "k_ready")
                scaled(0, q2[0], q2[0], "spread_q", "q_ready")
                scaled(0, kb2[0], k2[0], "spread_b", "kb_ready")
                level_factors(0, 0, 0, 0)
                level_factors(0, 0, 0, 1)
                with dve.Fori(0, NB) as b:
                    nc.vector.memset(S[:], 0.0).then_inc(s["reset"], 1)
                    with dve.Fori(0, NT // 2) as i:
                        for p in range(2):
                            n = NT * b + 2 * i + p
                            m = n + 1
                            for c in range(CB):
                                u = n * CB + c
                                for j in range(3):
                                    for g in range(2):
                                        products(u, g, j)
                                    if j == 0:
                                        turned_out(u, 1 - c)
                                for g in range(2):
                                    first_inverse(u, g)
                                for j in range(1, 6):
                                    for g in range(2):
                                        if j < 5:
                                            dve.wait_ge(s["dt_ps"][g], 4 * u + j + START)
                                            dve.wait_ge(s["t_sb"][g], 5 * u + j + START)
                                            nc.vector.tensor_tensor(Tm[:, g], Tm[:, g], pairs(bank[g][0]), ALU.subtract).then_inc(s["t_sb"][g], 1)
                                        else:
                                            dve.wait_ge(s["dv_ps"][g], u + 1 + START)
                                            nc.vector.tensor_tensor(V[:, g], V[:, g], pairs(bank[g][2]), ALU.subtract).then_inc(s["vd_sb"][g], 1)
                                    if j == 1:
                                        for g in range(2):
                                            put_qk_together(u, g)
                                    if c == 0:
                                        if j == 1:
                                            finish(n, p)
                                            norm_and_conv(m)
                                        if j == 2:
                                            level_factors(u + 1, p, 1, 0)
                                        if j == 3:
                                            decay_logits(m, 1 - p)
                                        if j == 4:
                                            level_factors(u + 1, p, 1, 1)
                                        if j == 5:
                                            decay_min(m, 1 - p)
                                    else:
                                        if j == 1:
                                            norm_rows(m)
                                        if j == 2:
                                            scaled(m, k2[1 - p], k2[1 - p], "spread_k", "k_ready")
                                        if j == 3:
                                            scaled(m, q2[1 - p], q2[1 - p], "spread_q", "q_ready")
                                        if j == 4:
                                            scaled(m, kb2[1 - p], k2[1 - p], "spread_b", "kb_ready")
                                        if j == 5:
                                            level_factors(u + 1, 1 - p, 0, 0)
                                for g in range(2):
                                    hs = slice(G4 * g, G4 * g + G4)
                                    dve.wait_ge(s["r_ps"][g], u + 1 + START)
                                    if g == 0:
                                        dve.wait_ge(s["v_ready"], 2 * n + 2 + START)
                                    nc.vector.tensor_tensor(B[:, g, 0:G4], v2_[p][:, c, hs], few(bank[g][1]), ALU.subtract).then_inc(s["b_sb"][g], 1)
                                if c == 0:
                                    decay_sum(m, 1 - p)
                                else:
                                    level_factors(u + 1, 1 - p, 0, 1)
                                for g in range(2):
                                    dve.wait_ge(s["s_mul"][g], u + 1 + START)
                                    dve.wait_ge(s["s_ps"][g], u + 1 + START)
                                    nc.vector.tensor_tensor(S[:, g, 0:G4], S[:, g, 0:G4], few(bank[g][1]), ALU.add).then_inc(s["s_sb"][g], 1)
                                    dve.wait_ge(s["ysq"][g], u + 1 + START)
                                    nc.vector.tensor_reduce(ss[:, g], yn[:, g], AX_X, ALU.add).then_inc(s["ss"][g], 1)
                                for g in range(2):
                                    dve.wait_ge(s["y_std"][g], u + 1 + START)
                                    nc.vector.reciprocal(ss[:, g], ss[:, g]).then_inc(s["ss_inv"][g], 1)
                                    dve.wait_ge(s["ss_inv"][g], u + 1 + START)
                                    nc.vector.tensor_tensor(yn[:, g], few(bank[g][2]), ss[:, g].unsqueeze(2).broadcast_to([P, G4, CH]), ALU.mult).then_inc(s["yn"][g], 1)
                turned_out(CB * NBLOCKS, 1)
                finish(NBLOCKS, 0)

            @block.tensor
            def _(pe):
                pe.wait_ge(s["cleared"], N_CLEARED + START)
                pe.wait_ge(s["weights_in"], 16 * N_WEIGHTS + START)
                pe.wait_ge(s["wo_scaled"], 1 + START)

                def x_products(m):
                    pe.wait_ge(s["square"], m + 1 + START)
                    for kk in range(KD):
                        mm = nc.tensor.matmul(f1[:, 0:TB], ones[:], square[:, kk], start=(kk == 0), stop=(kk == KD - 1))
                    mm.then_inc(s["var"], 1)
                    for kk in range(KD):
                        mm = nc.tensor.matmul(f1[0:DH, TB:2 * TB], u1[:, kk], xb[:, kk], start=(kk == 0), stop=(kk == KD - 1))
                    mm.then_inc(s["u1_ps"], 1)

                def gate_products(m):
                    pe.wait_ge(s["u_hid"], m + 1 + START)
                    for kk in range(KD):
                        mm = nc.tensor.matmul(f0[:, TB * kk:TB * kk + TB], u2[:, P * kk:P * kk + P], u_hid[:], start=True, stop=True)
                    mm.then_inc(s["u2_ps"], 1)

                def project(w, done):
                    for half in range(2):
                        for j in range(G4):
                            hp = G4 * half + j
                            for kk in range(KD):
                                mm = nc.tensor.matmul([f0, f1][half][:, P * j:P * j + P], w[:, kk, P * hp:P * hp + P], h[:, kk],
                                                      start=(kk == 0), stop=(kk == KD - 1))
                        mm.then_inc(s[done], 1)

                def decays(m):
                    pe.wait_ge(s["h"], m + 1 + START)
                    pe.wait_ge(s["gate_ready"], m + 1 + START)
                    pe.wait_ge(s["std"], m + 1 + START)
                    project(wa, "a_ps")

                def keys(m):
                    pe.wait_ge(s["z_sum"], 2 * m + 2 + START)
                    project(wk, "k_ps")

                def queries(m):
                    pe.wait_ge(s["raw"], 4 * m + 2 + START)
                    project(wq, "q_ps")

                def betas(m):
                    pe.wait_ge(s["raw"], 4 * m + 4 + START)
                    for kk in range(KD):
                        mm = nc.tensor.matmul(f0[0:H, 0:TB], wb[:, kk], h[:, kk], start=(kk == 0), stop=(kk == KD - 1))
                    mm.then_inc(s["b_ps"], 1)

                def norm_sums(m, p):
                    pe.wait_ge(s["sq"], 2 * m + 2 + START)
                    for j, t in ((0, kb2[p]), (1, v2_[p])):
                        for hp in range(HP):
                            mm = nc.tensor.matmul(f1[0:H, TB * j:TB * j + TB], gather[:, hp], t[:, :, hp], start=(hp == 0), stop=(hp == HP - 1))
                    mm.then_inc(s["sum_ps"], 1)

                def spread(m, j, done, free, count):
                    pe.wait_ge(s[free], count + START)
                    for half in range(2):
                        for hp in range(G4):
                            mm = nc.tensor.matmul([f0, f1][half][:, P * hp:P * hp + P], pick[:, G4 * half + hp], rows[:, j], start=True, stop=True)
                        mm.then_inc(s[done], 1)

                def spread_k(m):
                    pe.wait_ge(s["b_rows"], m + 1 + START)
                    spread(m, 0, "spread_k", "norm_inv", 2 * m + 2)

                def spread_q(m):
                    spread(m, 1, "spread_q", "k_ready", 2 * m + 2)

                def spread_b(m):
                    spread(m, 2, "spread_b", "q_ready", 2 * m + 2)

                def values(m):
                    pe.wait_ge(s["kb_ready"], 2 * m + 2 + START)
                    for c in range(CB):
                        for head in range(2):
                            r = slice(DH * head, DH * head + DH)
                            for kk in range(KD):
                                mm = nc.tensor.matmul([f0, f1][c][r, :], h[:, kk, CH * c:CH * c + CH],
                                                      wv[:, kk].rearrange("p (h a t) -> p h a t", a=2, t=DH)[:, :, head],
                                                      start=(kk == 0), stop=(kk == KD - 1))
                        mm.then_inc(s["v_ps"], 1)

                def turn_out(u, n, c):
                    if c == 0:
                        pe.wait_ge(s["v_ready"], 2 * n + 2 + START)
                    else:
                        pe.wait_ge(s["raw"], 4 * n + 8 + START)
                    for g in range(2):
                        pe.wait_ge(s["yn"][g], u + START)
                        for a in range(2):
                            mm = nc.tensor.transpose(f1[:, 2 * P * g + P * a:2 * P * g + P * a + P],
                                                     yn[:, g, 2 * a:2 * a + 2].rearrange("p h t -> p (h t)"), ident[:])
                    mm.then_inc(s["yt_ps"], 1)

                def output(n):
                    pe.wait_ge(s["yt_sb"], CB * n + 1 + START)
                    for m in range(KD):
                        for a in range(HP // 2):
                            for head in range(2):
                                mm = nc.tensor.matmul(f0[:, TB * m:TB * m + TB], wo[:, 2 * a + head, P * m:P * m + P], yT[:, a, head],
                                                      start=(a == 0 and head == 0), stop=(a == HP // 2 - 1 and head == 1))
                    mm.then_inc(s["out_ps"], 1)

                x_products(0)
                gate_products(0)
                decays(0)
                keys(0)
                queries(0)
                betas(0)
                norm_sums(0, 0)
                spread_k(0)
                spread_q(0)
                spread_b(0)
                values(0)
                with pe.Fori(0, NB) as b, pe.Fori(0, NT // 2) as i:
                    for p in range(2):
                        n = NT * b + 2 * i + p
                        m = n + 1
                        for c in range(CB):
                            u = n * CB + c
                            for j in range(4):
                                if j == 2:
                                    turn_out(u, n, c)
                                if j == 3 and c == 0:
                                    output(n)
                                    x_products(m)
                                if j == 3 and c == 1:
                                    pe.wait_ge(s["yt_sb"], u + 1 + START)
                                    norm_sums(m, 1 - p)
                                for g in range(2):
                                    if j == 0:
                                        pe.wait_ge(s["lvl_in"][g], u + 1 + START)
                                        pe.wait_ge(s["w_sb"][g], u + START)
                                    elif j == 1:
                                        pe.wait_ge(s["s_sb"][g], u + START)
                                    elif j == 2:
                                        pe.wait_ge(s["yn"][g], u + START)
                                    else:
                                        pe.wait_ge(s["u_ready"][g], 6 * u + 4 + START)
                                        pe.wait_ge(s["qk_part"][g], 5 * u + 2 + START)
                                        for hp in range(G4):
                                            mm = nc.tensor.transpose(bank[g][1][:, P * hp:P * hp + P], U[:, g, 0, hp], ident[:])
                                        mm.then_inc(s["y_ps"][g], 1)
                                    for hp in range(G4):
                                        mm = nc.tensor.matmul(bank[g][j % 3][:, P * hp:P * hp + P], lhs[:, g, 3 - j, hp],
                                                              rhs[:, g, 3 - j, hp].rearrange("p a t -> p (a t)"), start=True, stop=True)
                                    mm.then_inc(s["prod"][g], 1)
                            for j in range(1, 6):
                                for g in range(2):
                                    pe.wait_ge(s["u_ready"][g], 6 * u + (j + 1) + START)
                                    pe.wait_ge(s["t_sb"][g], 5 * u + j + START)
                                    for hp in range(G4):
                                        mm = nc.tensor.matmul(bank[g][1][:, P * hp:P * hp + P], U[:, g, j, hp], Tm[:, g, hp], start=True, stop=True)
                                    mm.then_inc(s["y_ps"][g], 1)
                                for g in range(2):
                                    pe.wait_ge(s["y_sb"][g], 5 * u + j + START)
                                    if j == 1:
                                        pe.wait_ge(s["v2"][g], u + 1 + START)
                                        pe.wait_ge(s["qk_part"][g], 5 * u + 3 + START)
                                        pe.wait_ge(s["u_ready"][g], 6 * u + 6 + START)
                                    else:
                                        pe.wait_ge(s["v_sb"][g], 4 * u + (j - 1) + START)
                                    if j < 5:
                                        for hp in range(G4):
                                            mm = nc.tensor.matmul(bank[g][0][:, P * hp:P * hp + P], V[:, g, hp], Y[:, g, hp], start=True, stop=True)
                                        mm.then_inc(s["dt_ps"][g], 1)
                                    else:
                                        for hp in range(G4):
                                            mm = nc.tensor.matmul(bank[g][2][:, P * hp:P * hp + P], Y[:, g, hp], V[:, g, hp], start=True, stop=True)
                                        mm.then_inc(s["dv_ps"][g], 1)
                                if c == 0:
                                    if j == 2:
                                        pe.wait_ge(s["gated"], 2 * n + 2 + START)
                                        gate_products(m)
                                    if j == 3:
                                        decays(m)
                                    if j == 4:
                                        keys(m)
                                    if j == 5:
                                        queries(m)
                                else:
                                    if j == 2:
                                        spread_k(m)
                                    if j == 3:
                                        spread_q(m)
                                    if j == 4:
                                        spread_b(m)
                                    if j == 5:
                                        values(m)
                                for g in range(2):
                                    if j < 5:
                                        pe.wait_ge(s["t_sb"][g], 5 * u + (j + 1) + START)
                                        for hp in range(G4):
                                            mm = nc.tensor.transpose(bank[g][2][:, P * hp:P * hp + P], Tm[:, g, hp], ident[:])
                                        mm.then_inc(s["v_ps2"][g], 1)
                            for g in range(2):
                                pe.wait_ge(s["state_in"][g], 6 * u + 6 + START)
                                for hp in range(G4):
                                    mm = nc.tensor.transpose(bank[g][0][:, P * hp:P * hp + P], kH[:, g, hp], ident[:])
                                mm.then_inc(s["kt_ps"][g], 1)
                            for g in range(2):
                                if g == 0:
                                    pe.wait_ge(s["reset"], b + 1 + START)
                                pe.wait_ge(s["s_sb"][g], u + START)
                                for hp in range(G4):
                                    mm = nc.tensor.matmul(bank[g][1][:, P * hp:P * hp + P], kG[:, g, hp], S[:, g, hp:hp + 2], start=True, stop=True)
                                mm.then_inc(s["r_ps"][g], 1)
                            if c == 0:
                                betas(m)
                            for g in range(2):
                                pe.wait_ge(s["b_sb"][g], u + 1 + START)
                                pe.wait_ge(s["vd_sb"][g], u + 1 + START)
                                pe.wait_ge(s["kt_sb"][g], u + 1 + START)
                                for hp in range(G4):
                                    mm = nc.tensor.matmul(bank[g][0][:, P * hp:P * hp + P], V[:, g, hp], B[:, g, hp:hp + 2], start=True, stop=True)
                                mm.then_inc(s["w_ps"][g], 1)
                            for g in range(2):
                                pe.wait_ge(s["w_sb"][g], u + 1 + START)
                                for hp in range(G4):
                                    nc.tensor.matmul(bank[g][2][:, P * hp:P * hp + P], qG[:, g, hp], S[:, g, hp:hp + 2], start=True, stop=False)
                                    mm = nc.tensor.matmul(bank[g][2][:, P * hp:P * hp + P], QK[:, g, hp], W[:, g, hp:hp + 2], start=False, stop=True)
                                mm.then_inc(s["o_ps"][g], 1)
                                for hp in range(G4):
                                    mm = nc.tensor.matmul(bank[g][1][:, P * hp:P * hp + P], kH[:, g, hp], W[:, g, hp:hp + 2], start=True, stop=True)
                                mm.then_inc(s["s_ps"][g], 1)
                turn_out(CB * NBLOCKS, NBLOCKS, 0)
                output(NBLOCKS)


def delta_feed_forward(nc, io, x, ones):
    with Phase(nc) as ctx:
        def sem(name):
            return ctx.semaphore("f_" + name)

        def sb(name, shape):
            return ctx.enter_context(nc.sbuf_tensor("f_" + name, shape, F32))

        w1, w3, w2 = sb("w1", [P, KD, FF]), sb("w3", [P, KD, FF]), sb("w2", [P, KF, D])
        norm_w = sb("norm_w", [P, KD])
        mid, y2, z = sb("mid", [P, 2, KD, BLK]), sb("y2", [P, KD, BLK]), sb("z", [P, KD, BLK])
        silu, hidden = sb("silu", [P, 2, BLK]), sb("hidden", [P, KF, BLK])
        rms = Norm(nc, ctx, "f_rms", ones, centred=False)
        norm = Norm(nc, ctx, "f_norm", ones)
        bank = [ctx.enter_context(nc.psum_tensor(f"f_bank{j}", [P, BLK], F32)) for j in range(8)]
        gate_ps, up_ps, acc, mean_ps, var_ps = bank[0:2], bank[2:4], bank[4:6], bank[6], bank[7]
        weights_in, eps_ready, mid_in = sem("weights_in"), sem("eps_ready"), [sem("mid_in0"), sem("mid_in1")]
        x_in, padded = [sem("x_in0"), sem("x_in1")], sem("padded")
        x_old = sb("x_old", [P, 2, KD, BLK])
        y2_ready, gate_done, up_done, silu_ready, hidden_ready = sem("y2_ready"), sem("gate_done"), sem("up_done"), sem("silu_ready"), sem("hidden_ready")
        down_done, z_ready = sem("down_done"), sem("z_ready")
        sum_ready = [sem("sum_ready0"), sem("sum_ready1")]
        HB = NBLK // 2
        N = NB * NBLK

        ctx.preset()
        with nc.Block() as block:
            @block.sync
            def _(sp):
                for dst, name in ((w1, "f_w1"), (w3, "f_w3"), (w2, "f_w2"), (norm_w, "f_norm_w")):
                    sp.dma_start(dst[:], io[name]).then_inc(weights_in, 16)
                with sp.Fori(0, NB) as b, sp.Fori(0, HB) as i:
                    for half in range(2):
                        sp.wait_ge(sum_ready[half], i + HB * b + START)
                        start = 2 * CH + b * T + (2 * i + half) * BLK
                        sp.dma_start(mid[:, half], io["mid"][:, :, bass.ds(start + 2 * CH, BLK)]).then_inc(mid_in[half], 16)
                        sp.dma_start(x_old[:, half], io["x2"][:, :, bass.ds(start, BLK)]).then_inc(x_in[half], 16)
                sp.wait_ge(sum_ready[0], N // 2 + START)
                sp.dma_start(mid[:, 0], io["mid"][:, :, 4 * CH + NB * T - BLK:4 * CH + NB * T]).then_inc(mid_in[0], 16)

            @block.gpsimd
            def _(pool):
                nc.gpsimd.memset(norm.eps[:], 1e-5).then_inc(eps_ready, 1)
                nc.gpsimd.memset(x[:, :, :, 0:PAD], 0.0).then_inc(padded, 1)
                nc.gpsimd.memset(rms.eps[:], 1e-6).then_inc(eps_ready, 1)

            @block.tensor
            def _(pe):
                pe.wait_ge(weights_in, 16 * 4 + START)
                rms.tensor_var(pe, 0, var_ps[:])
                with pe.Fori(0, NB) as b, pe.Fori(0, HB) as i:
                    for half in range(2):
                        n = 2 * i + half + NBLK * b
                        pe.wait_ge(y2_ready, KD * n + KD + START)
                        for m in range(KF):
                            c = KF * n + m
                            if m >= 2:
                                pe.wait_ge(hidden_ready, c - 1 + START)
                            for w, dst, done in ((w1, gate_ps, gate_done), (w3, up_ps, up_done)):
                                for k in range(KD):
                                    mm = nc.tensor.matmul(dst[m % 2][:], w[:, k, P * m:P * m + P], y2[:, k], start=(k == 0), stop=(k == KD - 1))
                                mm.then_inc(done, 1)
                        for f in range(KF):
                            pe.wait_ge(hidden_ready, KF * n + (f + 1) + START)
                            if f == KF - 3:
                                rms.tensor_var(pe, n + 1, var_ps[:])
                            for m in range(KD):
                                mm = nc.tensor.matmul(acc[m][:], w2[:, f, P * m:P * m + P], hidden[:, f], start=(f == 0), stop=(f == KF - 1))
                        mm.then_inc(down_done, 1)
                        norm.tensor(pe, n, z, z_ready, n + 1, mean_ps[:], var_ps[:])

            @block.scalar
            def _(act):
                act.wait_ge(eps_ready, 2 + START)
                rms.scalar(act, 0, var_ps[:], mid[:, 0], mid_in[0], 16)
                with act.Fori(0, NB) as b, act.Fori(0, HB) as i:
                    for half in range(2):
                        n = 2 * i + half + NBLK * b
                        for m in range(KF):
                            c = KF * n + m
                            act.wait_ge(gate_done, c + 1 + START)
                            if m >= 2:
                                act.wait_ge(hidden_ready, c - 1 + START)
                            nc.scalar.activation(silu[:, m % 2], gate_ps[m % 2][:], ACT.Silu).then_inc(silu_ready, 1)
                        rms.scalar(act, n + 1, var_ps[:], mid[:, 1 - half], mid_in[1 - half], 16 * (i + HB * b + (1 + half)))
                        norm.scalar(act, n, var_ps[:])

            @block.vector
            def _(dve):
                dve.wait_ge(weights_in, 16 * 4 + START)

                def prepare(n, half, turn):
                    dve.wait_ge(mid_in[half], 16 * turn + 16 + START)
                    rms.vector(dve, n, mid[:, half], y2[:], mean_ps[:])
                    dve.wait_ge(rms.done, n + 1 + START)
                    for k in range(KD):
                        nc.vector.tensor_scalar(y2[:, k], y2[:, k], norm_w[:, k:k + 1], None, ALU.mult).then_inc(y2_ready, 1)

                prepare(0, 0, 0)
                with dve.Fori(0, NB) as b, dve.Fori(0, HB) as i:
                    for half in range(2):
                        n = 2 * i + half + NBLK * b
                        start = b * (PAD + T) + PAD + (2 * i + half) * BLK
                        x_block = x[:].rearrange("p k b t -> p k (b t)")[:, :, bass.ds(start, BLK)]
                        for m in range(KF):
                            c = KF * n + m
                            dve.wait_ge(silu_ready, c + 1 + START)
                            dve.wait_ge(up_done, c + 1 + START)
                            nc.vector.tensor_tensor(hidden[:, m], up_ps[m % 2][:], silu[:, m % 2], ALU.mult).then_inc(hidden_ready, 1)
                        dve.wait_ge(x_in[half], 16 * (i + HB * b + 1) + START)
                        nc.vector.tensor_tensor(z[:], x_old[:, half], mid[:, half], ALU.add).then_inc(sum_ready[half], 1)
                        prepare(n + 1, 1 - half, i + HB * b + half)
                        dve.wait_ge(down_done, n + 1 + START)
                        dve.wait_ge(sum_ready[half], i + HB * b + 1 + START)
                        for m in range(KD):
                            last = nc.vector.tensor_tensor(z[:, m], acc[m][:], z[:, m], ALU.add)
                        last.then_inc(z_ready, 1)
                        dve.wait_ge(z_ready, n + 1 + START)
                        norm.vector(dve, n, z, x_block, mean_ps[:])
                        dve.wait_ge(norm.done, n + 1 + START)


def channel_mix(nc, io, x, ones):
    with Phase(nc) as ctx:
        def sem(name):
            return ctx.semaphore(name)

        def sb(name, shape):
            return ctx.enter_context(nc.sbuf_tensor(name, shape, F32))

        wr, wk, wv = sb("mix_wr", [P, KD, D]), sb("mix_wk", [P, KD, D]), sb("mix_wv", [P, KD, D])
        mu = sb("mu", [P, 2 * KD])
        step, xr, xk = sb("mix_step", [P, KD, BLK]), sb("xr", [P, KD, BLK]), sb("xk", [P, KD, BLK])
        r, k_relu, k_act = sb("mix_r", [P, KD, BLK]), sb("k_relu", [P, KD, BLK]), sb("k_act", [P, KD, BLK])
        z, y = sb("mix_z", [P, KD, BLK]), sb("mix_y", [P, 2, KD, BLK])
        norm = Norm(nc, ctx, "mix_norm", ones)
        bank = [ctx.enter_context(nc.psum_tensor(f"mix_bank{j}", [P, BLK], F32)) for j in range(8)]
        r_ps, k_ps, v_ps, mean_ps, var_ps = bank[0:2], bank[2:4], bank[4:6], bank[6], bank[7]

        weights_in, eps_ready = sem("mix_weights_in"), sem("mix_eps_ready")
        step_ready, xk_ready, xr_ready = sem("mix_step_ready"), sem("xk_ready"), sem("xr_ready")
        k_done, r_done, v_done = sem("mix_k_done"), sem("mix_r_done"), sem("mix_v_done")
        relu_ready, r_ready, k_act_ready, gated, z_ready = sem("relu_ready"), sem("mix_r_ready"), sem("k_act_ready"), sem("gated"), sem("mix_z_ready")
        stored, written = [sem("out_stored0"), sem("out_stored1")], sem("out_written")
        HB = NBLK // 2

        ctx.preset()
        with nc.Block() as block:
            @block.sync
            def _(sp):
                for dst, name in ((wr, "mix_wr"), (wk, "mix_wk"), (wv, "mix_wv"), (mu, "mu")):
                    sp.dma_start(dst[:], io[name]).then_inc(weights_in, 16)
                sp.sem_inc(stored[1], 16)
                with sp.Fori(0, NB) as b, sp.Fori(0, HB) as i:
                    for half in range(2):
                        n = 2 * i + half + NBLK * b
                        sp.wait_ge(written, n + 2 + START)
                        sp.dma_start(io["out"][:, :, b, bass.ds((2 * i + half) * BLK, BLK)], y[:, half]).then_inc(stored[half], 16)
                for half in range(2):
                    sp.wait_ge(stored[half], 16 * (NB * HB + half) + START)

            @block.gpsimd
            def _(pool):
                nc.gpsimd.memset(norm.eps[:], 1e-5).then_inc(eps_ready, 1)
                nc.gpsimd.memset(z[:], 0.0).then_inc(z_ready, 1)
                with pool.Fori(0, NB) as b, pool.Fori(0, HB) as i:
                    for half in range(2):
                        n = 2 * i + half + NBLK * b
                        pool.wait_ge(relu_ready, n + 1 + START)
                        nc.gpsimd.tensor_tensor(k_act[:], k_relu[:], k_relu[:], ALU.mult).then_inc(k_act_ready, 1)

            @block.tensor
            def _(pe):
                pe.wait_ge(weights_in, 16 * 4 + START)
                with pe.Fori(0, NB) as b, pe.Fori(0, HB) as i:
                    for half in range(2):
                        n = 2 * i + half + NBLK * b
                        for dst, w, src, ready, done in ((k_ps, wk, xk, xk_ready, k_done), (r_ps, wr, xr, xr_ready, r_done)):
                            pe.wait_ge(ready, KD * (n + 1) + START)
                            pe.wait_ge(gated, n + START)
                            for m in range(KD):
                                for k in range(KD):
                                    mm = nc.tensor.matmul(dst[m][:], w[:, k, P * m:P * m + P], src[:, k], start=(k == 0), stop=(k == KD - 1))
                            mm.then_inc(done, 1)
                            if w is wk:
                                norm.tensor_mean(pe, z, z_ready, n + 1, mean_ps[:])
                            else:
                                norm.tensor_var(pe, n, var_ps[:])
                        pe.wait_ge(k_act_ready, n + 1 + START)
                        for m in range(KD):
                            for k in range(KD):
                                mm = nc.tensor.matmul(v_ps[m][:], wv[:, k, P * m:P * m + P], k_act[:, k], start=(k == 0), stop=(k == KD - 1))
                        mm.then_inc(v_done, 1)
                norm.tensor(pe, NB * NBLK, z, z_ready, NB * NBLK + 1, mean_ps[:], var_ps[:])

            @block.scalar
            def _(act):
                act.wait_ge(eps_ready, 1 + START)
                with act.Fori(0, NB) as b, act.Fori(0, HB) as i:
                    for half in range(2):
                        n = 2 * i + half + NBLK * b
                        act.wait_ge(k_done, n + 1 + START)
                        act.wait_ge(k_act_ready, n + START)
                        act.wait_ge(v_done, n + START)
                        for m in range(KD):
                            last = nc.scalar.activation(k_relu[:, m], k_ps[m][:], ACT.Relu)
                        last.then_inc(relu_ready, 1)
                        norm.scalar_square(act, n)
                        act.wait_ge(r_done, n + 1 + START)
                        for m in range(KD):
                            last = nc.scalar.activation(r[:, m], r_ps[m][:], ACT.Sigmoid)
                        last.then_inc(r_ready, 1)
                        norm.scalar_std(act, n, var_ps[:])
                norm.scalar(act, NB * NBLK, var_ps[:])

            @block.vector
            def _(dve):
                dve.wait_ge(weights_in, 16 * 4 + START)
                with dve.Fori(0, NB) as b, dve.Fori(0, HB) as i:
                    for half in range(2):
                        n = 2 * i + half + NBLK * b
                        start = b * (PAD + T) + PAD + (2 * i + half) * BLK
                        tokens = x[:].rearrange("p k b t -> p k (b t)")
                        now, before = tokens[:, :, bass.ds(start, BLK)], tokens[:, :, bass.ds(start - 1, BLK)]
                        nc.vector.tensor_tensor(step[:], now, before, ALU.subtract).then_inc(step_ready, 1)
                        dve.wait_ge(step_ready, n + 1 + START)
                        dve.wait_ge(r_done, n + START)
                        for dst, col, ready in ((xk, KD, xk_ready), (xr, 0, xr_ready)):
                            for k in range(KD):
                                nc.vector.scalar_tensor_tensor(dst[:, k], step[:, k], mu[:, col + k:col + k + 1], before[:, k],
                                                               ALU.mult, ALU.add).then_inc(ready, 1)
                        dve.wait_ge(stored[1 - half], 16 * (i + HB * b) + START)
                        norm.vector(dve, n, z, y[:, 1 - half], mean_ps[:])
                        dve.wait_ge(norm.done, n + 1 + START)
                        dve.sem_inc(written, 1)
                        dve.wait_ge(v_done, n + 1 + START)
                        dve.wait_ge(r_ready, n + 1 + START)
                        for m in range(KD):
                            last = nc.vector.tensor_tensor(r[:, m], v_ps[m][:], r[:, m], ALU.mult)
                        last.then_inc(gated, 1)
                        dve.wait_ge(gated, n + 1 + START)
                        nc.vector.tensor_tensor(z[:], r[:], now, ALU.add).then_inc(z_ready, 1)
                dve.wait_ge(stored[1], 16 * NB * HB + START)
                norm.vector(dve, NB * NBLK, z, y[:, 1], mean_ps[:])
                dve.wait_ge(norm.done, NB * NBLK + 1 + START)
                dve.sem_inc(written, 1)


def host_layout(inputs):
    a = {k: np.asarray(v) for k, v in inputs.items()}

    def rows(w):
        return np.ascontiguousarray(w.reshape(-1, P, w.shape[-1]).transpose(1, 0, 2))

    def cols(*vs):
        return np.ascontiguousarray(np.concatenate([v.reshape(-1, P).T for v in vs], axis=1))

    def spread(v):
        return np.ascontiguousarray(np.broadcast_to(v.reshape(1, -1), (P, v.size)))

    out = {"x": np.ascontiguousarray(a["L0_attn_src"].reshape(NB, T, KD, P).transpose(3, 2, 0, 1))}
    for k, n in (("wq", "Wq"), ("wk", "Wk"), ("wv", "Wv"), ("wo", "Wo"), ("w1", "W1"), ("w2", "W2")):
        out[k] = rows(a["L0_attn_" + n])
    out["bk"], out["bv"] = spread(a["L0_attn_bk"]), spread(a["L0_attn_bv"])
    out["l0_cols"] = cols(*(a["L0_attn_" + n] for n in ("bq", "b1", "bo", "b2", "g1", "be1", "g2", "be2")))
    head = np.arange(P) // DH
    out["pair_mask"] = (head[:, None] == head[None, :]).astype(np.float32)
    out["ident"] = np.eye(P, dtype=np.float32)
    out["router"] = rows(a["L0_ffn_gate_w"].T)
    for name, w in (("gate", "gate"), ("up", "up"), ("down", "down")):
        every = np.concatenate([a["L0_ffn_r_" + w], a["L0_ffn_shared_" + w][None]]).transpose(0, 2, 1)
        out["expert_" + name] = np.ascontiguousarray(np.stack([rows(w) for w in every], axis=1))
    out["c_rank"] = spread(NE - np.arange(NE, dtype=np.float32))
    out["c_before"] = np.triu(np.ones((P, P), np.float32), 1)
    tiles = NB * T // P
    first = np.tile((np.arange(tiles) > 0), NE)
    out["c_consts"] = spread(np.concatenate([first, np.tile(P * np.arange(tiles), NE), 1 + np.arange(tiles + NE), np.ones(NE)]).astype(np.float32))
    for k in ("r", "k", "v"):
        out["mix_w" + k] = rows(a["L1_ffn_W_" + k].T)
    out["mu"] = cols(a["L1_ffn_mu_r"], a["L1_ffn_mu_k"])
    A = {k[8:]: v for k, v in a.items() if k.startswith("L1_attn_")}
    for name, w in (("wq", "q_w"), ("wk", "k_w"), ("wv", "v_w"), ("wa", "alpha_w"), ("wb", "beta_w"), ("u1", "u1_w")):
        out["d_" + name] = rows(A[w])
    out["d_u2"] = np.ascontiguousarray(A["u2_w"])
    conv = A["conv_w"].reshape(KD, P, 4).transpose(1, 0, 2).reshape(P, 4 * KD)
    u1_b, b_b = np.zeros((P, 1), np.float32), np.zeros((P, 1), np.float32)
    u1_b[:DH, 0], b_b[:H, 0] = A["u1_b"], A["beta_b"]
    out["d_cols"] = np.ascontiguousarray(np.concatenate(
        [cols(A["norm_in_w"]), conv, cols(A["conv_b"], A["alpha_b"], A["u2_b"]), u1_b, b_b], axis=1))
    def by_two_pairs(t):
        t = t.reshape(HP // 2, 2, 2, DH, -1).transpose(1, 3, 0, 2, 4)
        return np.ascontiguousarray(t.reshape(P, HP, -1))
    out["d_wo"] = by_two_pairs(A["out_w"])
    out["d_head_norm"] = by_two_pairs(A["head_norm_w"])[:, :, 0].copy()
    pair_head = (2 * np.arange(HP)[:, None] + head[None, :])
    out["d_pick"] = (np.arange(H)[:, None, None] == pair_head[None]).astype(np.float32)
    for w in ("w1", "w3", "w2"):
        out["f_" + w] = rows(A["ff_" + w])
    out["f_norm_w"] = cols(A["ff_norm_w"])
    out["d_gather"] = np.ascontiguousarray(out["d_pick"].transpose(2, 1, 0))
    blocks = np.arange(NB * T // (2 * CH) + 1)
    out["d_goes_on"] = np.ascontiguousarray(np.broadcast_to((blocks % (T // (2 * CH)) > 0).astype(np.float32), (P, blocks.size)))
    t = np.arange(CH)
    j, i = t[:, None], t[None, :]
    masks = np.zeros((2, CH, 6, 2, CH), np.float32)
    for m in range(6):
        s = 1 << m
        ok = (j // (2 * s) == i // (2 * s)) & (j // s % 2 == 0) & (i // s % 2 == 1)
        for w in range(2):
            masks[w, :, m, w] = ok
    out["d_masks"] = masks.reshape(P, 6, 2, CH)
    q_masks = np.stack([(j // 8 == i // 8) & (j <= i)] + [(j // (2 * s) == i // (2 * s)) & (j // s % 2 == 0) & (i // s % 2 == 1) for s in (8, 16)], axis=1)
    out["d_q_masks"] = np.concatenate([q_masks, q_masks]).astype(np.float32)
    out["d_carry_on"] = np.ascontiguousarray(np.broadcast_to((t > 0).astype(np.float32), (P, HP, CH)).reshape(P, HP * CH))
    return out


def kernel(**inputs):
    import concourse.bacc as bacc
    from concourse.bass_utils import run_bass_kernel_spmd as run

    nc = bacc.Bacc("TRN2", target_bir_lowering=False, num_devices=1)
    arrays = {f"in_{k}": v for k, v in host_layout(inputs).items()}
    io = {k[3:]: nc.dram_tensor(k, a.shape, F32, kind="ExternalInput").ap() for k, a in arrays.items()}
    io["out"] = nc.dram_tensor("out", (P, KD, NB, T), F32, kind="ExternalOutput").ap()
    for name in ("x2", "mid"):
        io[name] = nc.dram_tensor(name, (P, KD, NB * T + 4 * CH), F32).ap()
    for name in ("sorted_in", "sorted_out"):
        io[name] = nc.dram_tensor(name, (NB * T + (NE + 1) * P, D), F32).ap()
    decoder_program(nc, io)
    got = run(nc, [arrays], core_ids=[0]).results[0]["out"]
    return np.ascontiguousarray(np.transpose(got, (2, 3, 1, 0)).reshape(NB, T, D))
```
